# Optimizing a Trainium2 kernel written in Bass

```python
import numpy as np
import jax
import jax.numpy as jnp

def _softmax(x, axis=-1):
    return jax.nn.softmax(x, axis=axis)

def _gelu(x):
    return jax.nn.gelu(x, approximate=True)

def _silu(x):
    return jax.nn.silu(x)

def _sigmoid(x):
    return jax.nn.sigmoid(x)

def _layernorm(x, axis=-1, eps=1e-05):
    m = jnp.mean(x, axis=axis, keepdims=True)
    v = jnp.var(x, axis=axis, keepdims=True)
    return (x - m) / jnp.sqrt(v + eps)

def _scatter_add(tgt, idx, src, axis=0):
    return tgt.at[idx].add(src)

def _segment_sum(src, seg, n):
    return jax.ops.segment_sum(src, seg, n)
kernel_name = 'mk_adaln_d1_jaxref_r4_e881f5'

def setup_inputs(seed: int=0):
    np.random.seed(seed)
    _w = jnp.asarray

    def _L0_attn_setup():
        import jax, jax.numpy as jnp
        import numpy as np
        D_MODEL = 256
        N_HEADS = 16
        D_K = D_MODEL // N_HEADS
        THETA = 10000.0
        BATCH = 1
        SEQ = 1024

        def _rope(x, pos, inv_freq):
            angles = pos[:, None].astype(jnp.float32) * inv_freq
            cos = jnp.repeat(jnp.cos(angles), 2, axis=-1)
            sin = jnp.repeat(jnp.sin(angles), 2, axis=-1)
            x_rot = jnp.stack([-x[..., 1::2], x[..., 0::2]], axis=-1).reshape(x.shape)
            return x * cos + x_rot * sin
        key = jax.random.key(seed)
        ks = jax.random.split(key, 5)
        std = (2.0 / (D_MODEL + D_MODEL)) ** 0.5
        mk = lambda k: jax.random.truncated_normal(k, -3.0, 3.0, (D_MODEL, D_MODEL), jnp.float32) * std
        return {'x': jax.random.normal(ks[0], (BATCH, SEQ, D_MODEL), jnp.float32), 'Wq': mk(ks[1]), 'Wk': mk(ks[2]), 'Wv': mk(ks[3]), 'Wo': mk(ks[4])}
    _L0_attn_in = _L0_attn_setup()

    def _L0_ffn_setup():
        import jax, jax.numpy as jnp
        import numpy as np
        D = 256
        H = 1024
        E = 8
        TOPK = 2
        CAP_F = 1.25
        key = jax.random.key(seed)
        ks = jax.random.split(key, 6)
        sc = 0.02
        return {'x': jax.random.normal(ks[0], (4, 512, D), jnp.float32), 'Wg': jax.random.normal(ks[1], (D, E), jnp.float32) * sc, 'bg': jnp.zeros((E,), jnp.float32), 'W1': jax.random.normal(ks[2], (E, D, H), jnp.float32) * sc, 'W2': jax.random.normal(ks[3], (E, D, H), jnp.float32) * sc, 'W3': jax.random.normal(ks[4], (E, H, D), jnp.float32) * sc}
    _L0_ffn_in = _L0_ffn_setup()
    _L0_c = _w((lambda *s: np.random.randn(*s).astype(np.float32) * 0.05)(4, 256))
    _L0_wmod = _w((lambda *s: np.random.randn(*s).astype(np.float32) * 0.05)(256, 6 * 256) * 256 ** (-0.5))
    _d = {'L0_attn_x': _L0_attn_in['x'], 'L0_attn_Wq': _L0_attn_in['Wq'], 'L0_attn_Wk': _L0_attn_in['Wk'], 'L0_attn_Wv': _L0_attn_in['Wv'], 'L0_attn_Wo': _L0_attn_in['Wo'], 'L0_ffn_Wg': _L0_ffn_in['Wg'], 'L0_ffn_bg': _L0_ffn_in['bg'], 'L0_ffn_W1': _L0_ffn_in['W1'], 'L0_ffn_W2': _L0_ffn_in['W2'], 'L0_ffn_W3': _L0_ffn_in['W3'], 'L0_c': _L0_c, 'L0_wmod': _L0_wmod}
    _x0 = _d['L0_attn_x']
    _d['L0_attn_x'] = jax.random.normal(jax.random.fold_in(jax.random.key(seed), 1), (4, 1024, 256), dtype=_x0.dtype)
    del _x0
    return _d

def reference(L0_attn_x, L0_attn_Wq, L0_attn_Wk, L0_attn_Wv, L0_attn_Wo, L0_ffn_Wg, L0_ffn_bg, L0_ffn_W1, L0_ffn_W2, L0_ffn_W3, L0_c, L0_wmod):

    def _L0_attn_ref(x, Wq, Wk, Wv, Wo):
        import jax, jax.numpy as jnp
        import numpy as np
        D_MODEL = 256
        N_HEADS = 16
        D_K = D_MODEL // N_HEADS
        THETA = 10000.0
        BATCH = 1
        SEQ = 1024

        def _rope(x, pos, inv_freq):
            angles = pos[:, None].astype(jnp.float32) * inv_freq
            cos = jnp.repeat(jnp.cos(angles), 2, axis=-1)
            sin = jnp.repeat(jnp.sin(angles), 2, axis=-1)
            x_rot = jnp.stack([-x[..., 1::2], x[..., 0::2]], axis=-1).reshape(x.shape)
            return x * cos + x_rot * sin
        b, s, _ = x.shape
        h, dk = (N_HEADS, D_K)
        proj = lambda W: jnp.einsum('bsi,oi->bso', x, W).reshape(b, s, h, dk).transpose(0, 2, 1, 3)
        q = proj(Wq)
        k = proj(Wk)
        v = proj(Wv)
        pos = jnp.arange(s)
        inv_freq = 1.0 / THETA ** (jnp.arange(0, dk, 2, dtype=jnp.float32) / dk)
        q = _rope(q, pos, inv_freq)
        k = _rope(k, pos, inv_freq)
        scores = jnp.einsum('bhqd,bhkd->bhqk', q, k) / jnp.sqrt(jnp.asarray(dk, jnp.float32))
        causal_mask = jnp.arange(s)[None, :] > jnp.arange(s)[:, None]
        scores = jnp.where(causal_mask, -jnp.inf, scores)
        weights = jax.nn.softmax(scores, axis=-1)
        out = jnp.einsum('bhqk,bhkd->bhqd', weights, v)
        out = out.transpose(0, 2, 1, 3).reshape(b, s, h * dk)
        return jnp.einsum('bsi,oi->bso', out, Wo)

    def _L0_ffn_ref(x, Wg, bg, W1, W2, W3):
        import jax, jax.numpy as jnp
        import numpy as np
        D = 256
        H = 1024
        E = 8
        TOPK = 2
        CAP_F = 1.25
        b, s, d = x.shape
        xt = x.reshape(-1, d)
        T = xt.shape[0]
        capacity = int(T / E * CAP_F)
        gate_logits = xt @ Wg + bg
        top_v, top_i = jax.lax.top_k(gate_logits, TOPK)
        expert_label = jax.nn.one_hot(top_i, E, dtype=xt.dtype).sum(axis=1)
        seq = jnp.cumsum(expert_label, axis=0) * expert_label
        valid = (seq > 0) & (seq <= capacity)
        slot = (seq - 1.0).astype(jnp.int32)
        flat_idx = jnp.where(valid, jnp.arange(E, dtype=jnp.int32)[None, :] * capacity + slot, E * capacity)
        src = jnp.broadcast_to(xt[:, None, :], (T, E, d)).reshape(-1, d)
        buf = jnp.zeros((E * capacity + 1, d), xt.dtype).at[flat_idx.reshape(-1)].set(src)
        disp = buf[:-1].reshape(E, capacity, d)
        h = jax.nn.silu(jnp.einsum('ecd,edh->ech', disp, W1)) * jnp.einsum('ecd,edh->ech', disp, W2)
        out = jnp.einsum('ech,ehd->ecd', h, W3)
        out_flat = jnp.concatenate([out.reshape(E * capacity, d), jnp.zeros((1, d), xt.dtype)], axis=0)
        all_expert_output = out_flat[flat_idx]
        sel = jnp.take_along_axis(all_expert_output, top_i[:, :, None], axis=1)
        routing_w = jax.nn.softmax(top_v, axis=-1)
        y = (routing_w[:, :, None] * sel).sum(axis=1)
        return y.reshape(b, s, d)
    x = L0_attn_x
    mod = (_silu(L0_c) @ L0_wmod).reshape(L0_c.shape[0], 6, 1, -1)
    sa, ca, ga, sb, cb, gb = (mod[:, 0], mod[:, 1], mod[:, 2], mod[:, 3], mod[:, 4], mod[:, 5])
    ga = (2 * (ga >= 0) - 1) * jnp.maximum(jnp.abs(ga), 0.25)
    gb = (2 * (gb >= 0) - 1) * jnp.maximum(jnp.abs(gb), 0.25)
    h = _layernorm(x, axis=-1) * (1 + ca) + sa
    x = x + ga * _L0_attn_ref(h, L0_attn_Wq, L0_attn_Wk, L0_attn_Wv, L0_attn_Wo)
    h = _layernorm(x, axis=-1) * (1 + cb) + sb
    x = x + gb * _L0_ffn_ref(h, L0_ffn_Wg, L0_ffn_bg, L0_ffn_W1, L0_ffn_W2, L0_ffn_W3)
    return x

_drawn_inputs = setup_inputs


def setup_inputs(seed=0):
    import zlib

    import numpy as np

    out = dict(_drawn_inputs(seed))
    spreads = {'L0_ffn_bg': (0.0, 0.8)}
    factors = {'L0_ffn_Wg': 8.0, 'L0_ffn_W1': 8.0, 'L0_ffn_W2': 8.0, 'L0_ffn_W3': 8.0}
    for name, (base, spread) in spreads.items():
        noise = np.random.default_rng([zlib.crc32(name.encode()), seed]).standard_normal(out[name].shape)
        drawn = base * np.exp(spread * noise) if base else spread * noise
        out[name] = jnp.asarray(drawn.astype(out[name].dtype))
    for name, factor in factors.items():
        out[name] = (out[name] * factor).astype(out[name].dtype)
    return out
```

```python
from contextlib import ExitStack

import concourse.bass as bass
import numpy as np
from concourse import mybir

F32 = mybir.dt.float32
BF16 = mybir.dt.bfloat16
U32 = mybir.dt.uint32
ALU = mybir.AluOpType
ACT = mybir.ActivationFunctionType
AX = mybir.AxisListType

P = 128
B, S, D = 4, 1024, 256
NH, DK = 16, 16
E, H, TOPK = 8, 1024, 2
T = B * S
CAP = int(T / E * 1.25)
TRASH = E * CAP
EPS = 1e-5
BIG = 1.0e30
DC = D // P
NT = S // P
HU = 4
NU = NH // HU
BANK = 512
CH = S // BANK
PARTS_Q = (0, 0, 0, 1, 1, 2)
PARTS_K = (0, 1, 2, 0, 1, 0)
MROW = 16 * len(PARTS_Q)
STACK = MROW + 3
STK_DMAS = 2 * 3


def spans(lo, hi):
    return [(a, b) for a, b in ((lo, min(hi, BANK)), (max(lo, BANK), hi)) if a < b]


def max_tiles(i):
    out = []
    for s, (a, b) in enumerate(spans(0, P * (i + 1))):
        n = min(HU, BANK // (b - a))
        out += [(s, a, b, list(range(h, h + n))) for h in range(0, HU, n)]
    return out


def att_quads(j):
    out = []
    for a, b in spans(P * j, S):
        n = min(HU, BANK // (b - a))
        out.append((a, b, [list(range(h, h + n)) for h in range(0, HU, n)]))
    return out


def wide(ap, axis, n):
    shape = list(ap.shape)
    shape[axis] = n
    return ap.broadcast_to(tuple(shape))


MAX_BASE = np.cumsum([0] + [len(max_tiles(i)) for i in range(NT)]).tolist()
ATT_BASE = np.cumsum([0] + [sum(len(q[2]) for q in att_quads(j)) for j in range(NT)]).tolist()
UT = MAX_BASE[-1]
NPROB = 8
assert ATT_BASE[-1] == UT and UT % 2 == 0 and (NU * UT) % NPROB == 0

NEXT_T = [("T", c, d) for c in range(CH) for d in range(DC)]
NEXT_QK = [("QK", c, w, eo) for c in range(CH) for w in range(2) for eo in range(2)]
V_USES = [("V", p) for p in range(NT // 2)]
POST = [("O", p) for p in range(NT // 2)] + [("T2", c, d) for c in range(CH) for d in range(DC)] + [("G",), ("C",)]
MODROW = [("R", b, f) for f in range(2) for b in range(B)] + [("MT",)]
FIRST = MODROW + NEXT_T + NEXT_QK + [("M", 0)] + V_USES
BODY = ([("M", 1)] + NEXT_T + [("M", 2)] + NEXT_QK + [("M", 3), ("M", 0)] + V_USES + POST)
LAST = [("M", 1), ("M", 2), ("M", 3)] + POST
if len(FIRST) % 2:
    FIRST.append(("pad",))
assert len(BODY) % 2 == 0
CONSTS = 11
POOL_FIRST, POOL_BODY, POOL_LAST = 16, 18, 2
DVE_FIRST, DVE_BODY, DVE_LAST = 18, 48, 42


def attention_block(nc, io, disp, keep):
    x, modrow, slot_of, weight_of = keep["x"], keep["modrow"], keep["slot"], keep["weight"]
    ctx = ExitStack()
    with ctx:
        def sb(name, shape, dt=F32):
            return ctx.enter_context(nc.sbuf_tensor(name, shape, dt))

        def sem(name):
            return ctx.enter_context(nc.semaphore(name))

        wq = sb("wq", [P, 2, DC, D])
        wv = sb("wv", [P, DC, D])
        wo = sb("wo", [P, NU, D])
        wg = sb("wg", [P, DC, E])
        bg = sb("bg", [P, E])
        rope = sb("rope", [P, 2, S])
        modT = sb("modT", [P, 2 * DC, B])
        identf = sb("identf", [P, P])
        ident = sb("ident", [P, P], BF16)
        mask_k = sb("mask_k", [P, P], BF16)
        mask_q = sb("mask_q", [P, P], BF16)
        tri = sb("tri", [P, P], BF16)
        ones = sb("ones", [P, P], BF16)
        half = sb("half", [P, NT])
        eio = sb("eio", [P, E])
        ebase = sb("ebase", [P, E])
        stats = sb("stats", [P, NT, 6])
        meanvar = sb("meanvar", [P, NT, 2])
        vareps = sb("vareps", [P, NT])
        rstd = sb("rstd", [P, NT])
        h1T = sb("h1T", [P, DC, S])
        rt = sb("rt", [P, 4, BANK])
        rr = rt[:, 0:2]
        parts = sb("parts", [P, 2, 3, 2, S], BF16)
        va = sb("va", [P, NT, NH, 32])
        stk = sb("stk", [STACK, 2, 2, HU, S], BF16)
        mx = sb("mx", [P, 2, HU, NT])
        mxr = sb("mxr", [P, HU, NT])
        mp = sb("mp", [P, 3, HU, NT], BF16)
        mT = sb("mT", [3 * HU, S], BF16)
        prob = sb("prob", [P, NPROB, BANK])
        pvs = sb("pvs", [P, 2, BANK])
        attnT = sb("attnT", [P, NU, S])
        h2 = sb("h2", [P, NT, D])
        yb = rt[:, 0].rearrange("p (t d) -> p t d", t=2)
        lg = sb("lg", [P, NT, E])
        top = sb("top", [P, NT, 8])
        topi = sb("topi", [P, NT, 8], U32)
        topf = sb("topf", [P, NT, 8])
        oh = sb("oh", [P, 2, NT, E])
        label = sb("label", [P, NT, E], BF16)
        lsum = sb("lsum", [P, E])
        lsumb = sb("lsumb", [P, E], BF16)
        seqb = sb("seqb", [P, E])
        rw = sb("rw", [P, 4, NT, E])
        slotf = sb("slotf", [P, 2, NT])
        slotb = sb("slotb", [P, 2, NT], U32)
        gap = sb("gap", [P, 4, NT])
        silc = prob[:, 0:2, :].rearrange("p a (b m) -> p a b m", b=B)
        cT = sb("cT", [P, DC, B])
        sc = sb("sc", [P, 3, DC, B])

        psS = ctx.enter_context(nc.psum_tensor("psS", [P, 2, BANK], F32))
        psT = ctx.enter_context(nc.psum_tensor("psT", [P, 2, BANK], F32))
        psO = ctx.enter_context(nc.psum_tensor("psO", [P, 2, BANK], F32))
        psM = ctx.enter_context(nc.psum_tensor("psM", [P, 2, BANK], F32))
        psM_bf16 = [psM[:, i, :].bitcast(BF16) for i in range(2)]
        xn = h2[:, 0:4]
        wm = parts[:, 0, 0:2].rearrange("p z e n -> p (z e n)").bitcast(F32)[:, 0:DC * BANK].rearrange(
            "p (a n) -> p a n", a=DC)

        c_in = sem("c_in")
        wm_in = sem("wm_in")
        w_in = sem("w_in")
        x0_in = sem("x0_in")
        x_in = sem("x_in")
        consts = sem("consts")
        wo_zero = sem("wo_zero")
        minus_ones = sem("minus_ones")
        silu_e = sem("silu_e")
        silu_r = sem("silu_r")
        zeroed = sem("zeroed")
        zero_out = sem("zero_out")
        bank_ready = [sem(f"bank_ready{i}") for i in range(2)]
        bank_free = [sem(f"bank_free{i}") for i in range(2)]
        var_ready = sem("var_ready")
        rstd_ready = sem("rstd_ready")
        xn_ready = sem("xn_ready")
        h2m_ready = sem("h2m_ready")
        parts_ready = sem("parts_ready")
        scr_ready = [sem(f"scr_ready{i}") for i in range(2)]
        stk_ready = [sem(f"stk_ready{i}") for i in range(2)]
        mrow_ready = [sem(f"mrow_ready{i}") for i in range(2)]
        v_ready = sem("v_ready")
        s_ready = sem("s_ready")
        s_maxed = sem("s_maxed")
        mp_ready = sem("mp_ready")
        t_ready = sem("t_ready")
        exp_done = sem("exp_done")
        pv_done = sem("pv_done")
        pv_copied = sem("pv_copied")
        norm_ready = sem("norm_ready")
        attn_ready = sem("attn_ready")
        gap_ready = sem("gap_ready")
        gap_exp = sem("gap_exp")
        label_ready = sem("label_ready")
        slot_ready = sem("slot_ready")
        scattered = sem("scattered")
        h2_free = sem("h2_free")
        held_back = sem("held_back")
        dve_step = sem("dve_step")
        pool_step = sem("pool_step")

        def use(name, b):
            if b is None:
                k, base = FIRST.index(name), 0
                return k % 2, k // 2 + 1
            seq = LAST if isinstance(b, int) else BODY
            k = seq.index(name)
            return k % 2, b * (len(BODY) // 2) + (len(FIRST) // 2 + k // 2 + 1)

        def claim(pe, name, b):
            bank, n = use(name, b)
            if not (isinstance(n, int) and n == 1):
                pe.wait_ge(bank_free[bank], n - 1)
            return bank

        def filled(eng, name, b):
            bank, n = use(name, b)
            eng.wait_ge(bank_ready[bank], n)
            return bank

        def emptied(eng, name, b):
            bank, n = use(name, b)
            eng.wait_ge(bank_free[bank], n)

        def ge(eng, s, value):
            if not (isinstance(value, int) and value <= 0):
                eng.wait_ge(s, value)

        def unit(b, g):
            return b * NU + g

        def hold(eng):
            eng.sem_inc(held_back, 1)

        block = ctx.enter_context(nc.Block())

        @block.sync
        def _(sp):
            sp.dma_start(cT[:], io["cT"].rearrange("(a p) b -> p a b", p=P)).then_inc(c_in, 16)
            sp.dma_start(x[:, 0:NT, :], io["x"][0:S, :].rearrange("(t p) d -> p t d", p=P)).then_inc(x0_in, 16)
            for w, src in enumerate((io["wq"], io["wk"])):
                sp.dma_start(wq[:, w], src.rearrange("(a p) n -> p a n", p=P)).then_inc(w_in, 16)
            sp.dma_start(wv[:], io["wv"].rearrange("(a p) n -> p a n", p=P)).then_inc(w_in, 16)
            sp.dma_start(wg[:], io["wg"].rearrange("(a p) n -> p a n", p=P)).then_inc(w_in, 16)
            sp.dma_start(bg[:], wide(io["bg"].rearrange("(a e) -> a e", a=1), 0, P)).then_inc(w_in, 16)
            sp.dma_start(rope[:, 0], io["cos"]).then_inc(w_in, 16)
            sp.dma_start(rope[:, 1], io["sin"]).then_inc(w_in, 16)
            sp.wait_ge(wo_zero, 1)
            for i in range(HU):
                sp.dma_start(wo[32 * i:32 * i + DK],
                             io["wo"].rearrange("(g i d) n -> i d g n", g=NU, i=HU)[i]).then_inc(w_in, 16)
            for n in range(3):
                if n:
                    filled(sp, ("R", B - 1, n - 1), None)
                sp.dma_start(wm, io["wmod"][n].rearrange("(a p) n -> p a n", p=P)).then_inc(wm_in, 16)
            for b in range(1, B):
                sp.dma_start(x[:, NT * b:NT * (b + 1), :],
                             io["x"][S * b:S * (b + 1), :].rearrange("(t p) d -> p t d", p=P)).then_inc(x_in, 16)
            sp.wait_ge(zeroed, 1)
            for r in range(0, E * CAP, 4 * P):
                sp.dma_start(disp[r:r + 4 * P, :].rearrange("(t p) d -> p t d", p=P),
                             attnT[:, 0].rearrange("p (t d) -> p t d", t=4)).then_inc(zero_out, 16)

            def stacks(b, g):
                s = g % 2
                sp.wait_ge(parts_ready, b * 4 + 4)
                hold(sp)
                if not (isinstance(b, int) and b == 0 and g == 0):
                    sp.wait_ge(s_maxed, b * (NU * UT) + ((g - 1) * UT + 2))
                hold(sp)
                for w in range(2):
                    sp.dma_start(io["scr"][s, w].rearrange("z e q n -> q (z e) n"),
                                 parts[32 * g:32 * g + 32, w].rearrange("p z e n -> p (z e) n"),
                                 ).then_inc(scr_ready[s], 16)
                sp.wait_ge(scr_ready[s], (b * 2 + (g // 2 + 1)) * 32)
                hold(sp)
                if not (isinstance(b, int) and b == 0 and g == 0):
                    sp.wait_ge(pv_done, b * (NU * UT) + ((g - 1) * UT + NPROB))
                hold(sp)
                rows = io["scr"][s].rearrange("w z e (r i) n -> w (z e r) i n", i=HU)
                for n, r0 in enumerate((0, 48, 80)):
                    count = 16 * (3 - n)
                    sp.dma_start(stk[r0:r0 + count, s, 1], rows[1, 0:count]).then_inc(stk_ready[s], 16)
                    sp.dma_start(stk[r0:r0 + count, s, 0],
                                 wide(rows[0, 16 * n:16 * n + 16].unsqueeze(0), 0, 3 - n),
                                 ).then_inc(stk_ready[s], 16)

            def max_rows(b, g, at):
                emptied(sp, ("M", g), at)
                hold(sp)
                for part in range(3):
                    sp.dma_start(stk[MROW + part:MROW + part + 1, g % 2, 0],
                                 mT[HU * part:HU * part + HU, :],
                                 ).then_inc(mrow_ready[g % 2], 16)

            stacks(0, 0)
            max_rows(0, 0, None)

            def body(b, last):
                for g in range(1, NU):
                    stacks(b, g)
                    max_rows(b, g, b)
                if not last:
                    stacks(b + 1, 0)
                    max_rows(b + 1, 0, b)

            with sp.Fori(0, B - 1) as b:
                body(b, False)
            body(B - 1, True)

        @block.gpsimd
        def _(pool):
            n = [0]

            def step(ins):
                n[0] += 1
                ins.then_inc(pool_step, 1)
                pool.wait_ge(pool_step, n[0])

            pool.sem_inc(attn_ready, 1)
            pool.sem_inc(h2_free, 1)
            nc.gpsimd.memset(wo[:], 0.0).then_inc(wo_zero, 1)
            nc.gpsimd.memset(half[:], -0.5).then_inc(consts, 1)
            nc.gpsimd.memset(attnT[:, 0], 0.0).then_inc(zeroed, 1)
            step(nc.gpsimd.memset(identf[:], 0.0))
            step(nc.gpsimd.memset(ident[:], 0.0))
            step(nc.gpsimd.memset(mask_k[:], 0.0))
            step(nc.gpsimd.memset(mask_q[:], 0.0))
            step(nc.gpsimd.memset(tri[:], 1.0))
            for t in (identf, ident):
                nc.gpsimd.affine_select(out=t[:], in_=t[:], compare_op=ALU.not_equal, fill=1.0, base=0,
                                        pattern=[[-1, P]], channel_multiplier=1).then_inc(consts, 1)
            nc.gpsimd.affine_select(out=mask_k[:], in_=mask_k[:], compare_op=ALU.is_ge, fill=-BIG, base=0,
                                    pattern=[[-1, P]], channel_multiplier=1).then_inc(consts, 1)
            nc.gpsimd.affine_select(out=mask_q[:], in_=mask_q[:], compare_op=ALU.is_ge, fill=-BIG, base=0,
                                    pattern=[[1, P]], channel_multiplier=-1).then_inc(consts, 1)
            nc.gpsimd.affine_select(out=tri[:], in_=tri[:], compare_op=ALU.is_ge, fill=0.0, base=0,
                                    pattern=[[1, P]], channel_multiplier=-1).then_inc(consts, 1)
            nc.gpsimd.memset(ones[:], 1.0).then_inc(consts, 1)
            nc.gpsimd.iota(eio[:], pattern=[[1, E]], base=0, channel_multiplier=0,
                           allow_small_or_imprecise_dtypes=True).then_inc(consts, 1)
            nc.gpsimd.iota(ebase[:], pattern=[[CAP, E]], base=-1 - TRASH, channel_multiplier=0,
                           allow_small_or_imprecise_dtypes=True).then_inc(consts, 1)
            nc.gpsimd.memset(va[:, :, :, DK:32], 1.0).then_inc(consts, 1)
            nc.gpsimd.memset(seqb[:], 0.0).then_inc(consts, 1)
            pre = n[0]
            per = [0]

            def chained(b, ins):
                per[0] += 1
                ins.then_inc(pool_step, 1)
                base = pre if b is None else pre + POOL_FIRST
                pool.wait_ge(pool_step, (0 if b is None else b * POOL_BODY) + (base + per[0]))
                hold(pool)

            def power(count):
                pool.wait_ge(var_ready, count)
                hold(pool)
                nc.gpsimd.tensor_tensor(rstd[:], vareps[:], half[:], ALU.pow).then_inc(rstd_ready, 1)

            def rotate(b, at, c, w):
                for eo in range(2):
                    emptied(pool, ("QK", c, w, eo), at)
                    hold(pool)
                cs = slice(BANK * c, BANK * (c + 1))
                nc.gpsimd.tensor_tensor(rr[:, 0], rt[:, 0], rt[:, 3], ALU.subtract)
                chained(at, nc.gpsimd.tensor_tensor(rr[:, 1], rt[:, 2], rt[:, 1], ALU.add))
                chained(at, nc.gpsimd.tensor_copy(parts[:, w, 0, :, cs], rr))
                chained(at, nc.gpsimd.tensor_tensor(rr, rr, parts[:, w, 0, :, cs], ALU.subtract))
                chained(at, nc.gpsimd.tensor_copy(parts[:, w, 1, :, cs], rr))
                nc.gpsimd.tensor_tensor(parts[:, w, 2, :, cs], rr, parts[:, w, 1, :, cs],
                                        ALU.subtract).then_inc(parts_ready, 1)

            def normalise(b, g, hf):
                pool.wait_ge(norm_ready, unit(b, g) * 2 + (hf + 1))
                hold(pool)
                nc.gpsimd.tensor_tensor(attnT[:, g, BANK * hf:BANK * (hf + 1)], pvs[:, 0], pvs[:, 1],
                                        ALU.mult).then_inc(attn_ready, 1)

            pool.wait_ge(consts, CONSTS)
            power(1)
            for c in range(CH):
                for w in range(2):
                    rotate(0, None, c, w)

            pool.wait_ge(zero_out, 16 * E * CAP // (4 * P))
            pool_first, per[0] = per[0], 0
            assert pool_first == POOL_FIRST, pool_first

            def body(b, last):
                per[0] = 0
                for g in range(NU):
                    if g == 2 and not last:
                        pool.wait_ge(stk_ready[1], (b * 2 + 2) * (16 * STK_DMAS))
                        pool.wait_ge(stk_ready[0], (b * 2 + 2) * (16 * STK_DMAS))
                        hold(pool)
                    if g == 0 and not last:
                        power(b * 2 + 2)
                    for hf in range(2):
                        if g == 2 and not last:
                            for w in range(2):
                                rotate(b + 1, b, hf, w)
                        normalise(b, g, hf)
                power(b * 2 + 3 if not last else 2 * B)
                ms = modrow[:, bass.ds(b, 1)] if not last else modrow[:, B - 1:B]
                for hf in range(2):
                    pool.wait_ge(xn_ready, (b * 4 + (5 if not last else 3)) + hf)
                    hold(pool)
                    ts = slice(4 * hf, 4 * hf + 4)
                    chained(b, nc.gpsimd.tensor_tensor(
                        h2[:, ts], h2[:, ts], wide(ms[:, :, 2], 1, 4), ALU.mult))
                    nc.gpsimd.tensor_tensor(
                        h2[:, ts], h2[:, ts], wide(ms[:, :, 1], 1, 4), ALU.add).then_inc(h2m_ready, 1)
                pool.wait_ge(slot_ready, b + 1)
                pool.wait_ge(h2m_ready, b * 2 + 2)
                hold(pool)
                for t in range(NT):
                    for c in range(TOPK):
                        nc.gpsimd.indirect_dma_start(
                            disp[:, :], bass.IndirectOffsetOnAxis(ap=slotb[:, c, t:t + 1], axis=0),
                            h2[:, t], None, bounds_check=TRASH - 1, oob_is_err=False,
                        ).then_inc(scattered, 16)
                pool.wait_ge(scattered, b * (NT * TOPK * 16) + NT * TOPK * 16)
                pool.sem_inc(h2_free, 1)
                assert per[0] == (POOL_BODY if not last else POOL_LAST), per[0]

            with pool.Fori(0, B - 1) as b:
                body(b, False)
            body(B - 1, True)

        @block.scalar
        def _(act):
            act.sem_inc(exp_done, 2)
            act.wait_ge(c_in, 16)
            nc.scalar.activation(sc[:, 0], cT[:], ACT.Exp, scale=-1.0).then_inc(silu_e, 1)

            def evac_T(name, b):
                bank = filled(act, name, b)
                hold(act)
                _, c, d = name
                out = h1T[:, d, BANK * c:BANK * (c + 1)]
                if name[0] == "T":
                    if b is None:
                        shift, scale = modT[:, d, 0:1], modT[:, DC + d, 0:1]
                    else:
                        shift, scale = modT[:, d, bass.ds(b + 1, 1)], modT[:, DC + d, bass.ds(b + 1, 1)]
                    nc.scalar.activation(out, psM[:, bank], ACT.Identity, bias=shift,
                                         scale=scale).then_inc(bank_free[bank], 1)
                else:
                    nc.scalar.copy(out, psM[:, bank]).then_inc(bank_free[bank], 1)

            def evac_V(p, b):
                bank = filled(act, ("V", p), b)
                nc.scalar.copy(va[:, 2 * p:2 * p + 2, :, 0:DK],
                               psM[:, bank].rearrange("p (t h d) -> p t h d", t=2, h=NH)).then_inc(bank_free[bank], 1)
                emptied(act, ("V", p), b)
                act.sem_inc(v_ready, 1)

            def exps(b, g, j):
                k = ATT_BASE[j]
                for a, e, tiles in att_quads(j):
                    for heads in tiles:
                        n = unit(b, g) * UT + k
                        slot = (g * UT + k) % NPROB
                        w = (e - a) * len(heads)
                        act.wait_ge(t_ready, n + 1)
                        act.wait_ge(pv_done, n + 1)
                        nc.scalar.activation(prob[:, slot, 0:w], psT[:, k % 2, 0:w], ACT.Exp,
                                             scale=DK ** -0.5).then_inc(exp_done, 1)
                        k += 1

            act.wait_ge(silu_r, 3)
            for name in NEXT_T:
                evac_T(name, None)
            act.wait_ge(consts, CONSTS)
            for p in range(NT // 2):
                evac_V(p, None)

            def body(b, last):
                for g in range(NU):
                    for j in range(NT):
                        exps(b, g, j)
                        if g == 1 and j % 2 == 0 and not last:
                            evac_T(NEXT_T[j // 2], b)
                if not last:
                    for p in range(NT // 2):
                        evac_V(p, b)
                for c in range(CH):
                    for d in range(DC):
                        evac_T(("T2", c, d), b)
                act.wait_ge(gap_ready, b + 1)
                nc.scalar.activation(gap[:, 1], gap[:, 0], ACT.Exp).then_inc(gap_exp, 1)

            with act.Fori(0, B - 1) as b:
                body(b, False)
            body(B - 1, True)

        @block.vector
        def _(dve):
            v = nc.vector
            pre = [0]
            per = [0]

            def first(ins):
                pre[0] += 1
                ins.then_inc(dve_step, 1)
                dve.wait_ge(dve_step, pre[0])

            def chained(b, ins):
                if b is None:
                    return first(ins)
                per[0] += 1
                ins.then_inc(dve_step, 1)
                dve.wait_ge(dve_step, b * DVE_BODY + (DVE_FIRST + per[0]))

            for s in range(2):
                v.memset(stk[MROW:STACK, s, 1], -1.0).then_inc(minus_ones, 1)
            dve.wait_ge(silu_e, 1)
            first(v.tensor_scalar_add(sc[:, 1], sc[:, 0], 1.0))
            first(v.reciprocal(sc[:, 2], sc[:, 1]))
            first(v.tensor_tensor(sc[:, 0], sc[:, 2], cT[:], ALU.mult))
            for a in range(DC):
                v.tensor_copy(silc[:, a], wide(sc[:, 0, a].unsqueeze(2), 2, P)).then_inc(silu_r, 1)
            for f in range(2):
                for b in range(B):
                    bank = filled(dve, ("R", b, f), None)
                    src = psM[:, bank].rearrange("p (z d) -> p z d", z=2)
                    v.tensor_copy(modrow[:, b, 2 * f:2 * f + 2], src).then_inc(bank_free[bank], 1)
            bank = filled(dve, ("MT",), None)
            v.tensor_copy(modT[:], psM[:, bank, 0:2 * DC * B].rearrange("p (z b) -> p z b", b=B),
                          ).then_inc(bank_free[bank], 1)
            emptied(dve, ("MT",), None)
            v.tensor_scalar_add(modT[:, DC:2 * DC], modT[:, DC:2 * DC], 1.0).then_inc(silu_r, 1)
            dve.wait_ge(silu_r, 3)
            for f in range(2):
                emptied(dve, ("R", B - 1, f), None)
                emptied(dve, ("R", B - 2, f), None)
            first(v.tensor_scalar_add(modrow[:, :, 2], modrow[:, :, 2], 1.0))
            for z in (0, 3):
                g_ = modrow[:, :, z]
                sgn = rt[:, 0:2].rearrange("p a n -> p (a n)").rearrange("p (b d) -> p b d", b=B)
                mag = rt[:, 2:4].rearrange("p a n -> p (a n)").rearrange("p (b d) -> p b d", b=B)
                first(v.tensor_scalar(sgn, g_, 0.0, 2.0, ALU.is_ge, ALU.mult))
                first(v.tensor_scalar_add(sgn, sgn, -1.0))
                first(v.tensor_tensor(mag, g_, sgn, ALU.mult))
                first(v.scalar_tensor_tensor(out=g_, in0=mag, scalar=0.25, in1=sgn, op0=ALU.max, op1=ALU.mult))

            def xt(b, t, n=1):
                if isinstance(b, int):
                    return x[:, NT * b + t:NT * b + t + n, :]
                return x[:, bass.ds(b * NT + t, n), :]

            def layer_stats(at, b):
                if at is not None:
                    hold(dve)
                for t in range(NT):
                    ins = v.bn_stats(stats[:, t], xt(b, t)[:, 0])
                chained(at, ins)
                hold(dve)
                for t in range(NT):
                    ins = v.bn_aggr(meanvar[:, t], stats[:, t])
                chained(at, ins)
                v.tensor_scalar_add(vareps[:], meanvar[:, :, 1], EPS).then_inc(var_ready, 1)

            def normed(b, hf, out):
                for t in range(4 * hf, 4 * hf + 4):
                    ins = v.tensor_scalar(out[:, t % 4] if out is xn else out[:, t], xt(b, t)[:, 0], meanvar[:, t, 0:1], rstd[:, t:t + 1],
                                          ALU.subtract, ALU.mult)
                ins.then_inc(xn_ready, 1)

            def rope_mul(b, at, c, w):
                ge(dve, parts_ready, b * 4 + (2 * c + w))
                cs = slice(BANK * c, BANK * (c + 1))
                for eo in range(2):
                    bank = filled(dve, ("QK", c, w, eo), at)
                    v.tensor_tensor(rt[:, eo], psM[:, bank], rope[:, 0, cs], ALU.mult)
                    v.tensor_tensor(rt[:, 2 + eo], psM[:, bank], rope[:, 1, cs], ALU.mult).then_inc(bank_free[bank], 1)

            def maxes(b, g, i):
                k = MAX_BASE[i]
                for s, a, e, heads in max_tiles(i):
                    dve.wait_ge(s_ready, unit(b, g) * UT + (k + 1))
                    w, nh = e - a, len(heads)
                    v.tensor_reduce(mx[:, s, heads[0]:heads[0] + nh, i],
                                    psS[:, k % 2, 0:w * nh].rearrange("p (h w) -> p h w", h=nh), AX.X,
                                    ALU.max).then_inc(s_maxed, 1)
                    k += 1

            def max_parts(b, g, at):
                dve.wait_ge(s_maxed, (unit(b, g) + 1) * UT + 2)
                v.tensor_copy(mxr[:, :, 0:4], mx[:, 0, :, 0:4])
                chained(at, v.tensor_tensor(mxr[:, :, 4:8], mx[:, 0, :, 4:8], mx[:, 1, :, 4:8], ALU.max))
                chained(at, v.tensor_copy(mp[:, 0], mxr[:]))
                chained(at, v.tensor_tensor(mxr[:], mxr[:], mp[:, 0], ALU.subtract))
                chained(at, v.tensor_copy(mp[:, 1], mxr[:]))
                v.tensor_tensor(mp[:, 2], mxr[:], mp[:, 1], ALU.subtract).then_inc(mp_ready, 1)
                bank = filled(dve, ("M", g), at)
                if not (isinstance(b, int) and b == 0 and g == 0):
                    prev = (g + 1) % 2
                    cnt = (b * 2 + (g + 1) // 2) if g else b * 2
                    dve.wait_ge(mrow_ready[prev], cnt * 48)
                v.tensor_copy(mT[:], psM_bf16[bank][0:3 * HU, :]).then_inc(bank_free[bank], 1)

            def norm(b, at, g, hf):
                dve.wait_ge(pv_done, unit(b, g) * UT + (ATT_BASE[3] + 1 if hf == 0 else UT) + NPROB)
                dve.wait_ge(attn_ready, unit(b, g) * 2 + (hf + 1))
                v.tensor_copy(pvs[:, 0], psO[:, hf]).then_inc(pv_copied, 1)
                dve.wait_ge(pv_copied, unit(b, g) * 2 + (hf + 3))
                hold(dve)
                chained(at, v.stream_shuffle(pvs[:, 1], pvs[:, 0], mask=[DK] * 32))
                v.reciprocal(pvs[:, 1], pvs[:, 1]).then_inc(norm_ready, 1)

            dve.wait_ge(consts, CONSTS)
            dve.sem_inc(pv_copied, 2)
            dve.sem_inc(s_maxed, 2)
            dve.wait_ge(x0_in, 16)
            layer_stats(None, 0)
            dve.wait_ge(rstd_ready, 1)
            for hf in range(CH):
                if hf:
                    for d in range(DC):
                        filled(dve, ("T", 0, d), None)
                normed(0, hf, xn)
            dve.wait_ge(w_in, 16 * 11)
            for c in range(CH):
                for w in range(2):
                    rope_mul(0, None, c, w)
            dve.wait_ge(x_in, 16 * (B - 1))
            for i in range(NT):
                maxes(0, 0, i)
            max_parts(0, 0, None)
            assert pre[0] == DVE_FIRST, pre[0]

            def body(b, last):
                per[0] = 0
                for g in range(NU):
                    if g == 0 and not last:
                        layer_stats(b, b + 1)
                    for j in range(NT):
                        if g < NU - 1:
                            maxes(b, g + 1, j)
                        elif not last and j >= 4:
                            maxes(b + 1, 0, 2 * j - 8)
                            maxes(b + 1, 0, 2 * j - 7)
                        if g == 0 and j == 2 and not last:
                            dve.wait_ge(rstd_ready, b * 2 + 2)
                            dve.wait_ge(h2_free, b + 1)
                            normed(b + 1, 0, xn)
                        if g == 1 and j == 4 and not last:
                            for d in range(DC):
                                filled(dve, ("T", 0, d), b)
                            normed(b + 1, 1, xn)
                        if g == 2 and j % 2 and not last:
                            rope_mul(b + 1, b, (j // 2) // 2, (j // 2) % 2)
                        if j == 4:
                            norm(b, b, g, 0)
                    if g < NU - 1:
                        max_parts(b, g + 1, b)
                    elif not last:
                        max_parts(b + 1, 0, b)
                    norm(b, b, g, 1)
                if isinstance(b, int):
                    ga = modrow[:, b:b + 1, 0]
                else:
                    ga = modrow[:, bass.ds(b, 1), 0]
                dve.wait_ge(parts_ready, b * 4 + (4 if last else 8))
                for p in range(NT // 2):
                    bank = filled(dve, ("O", p), b)
                    src = psM[:, bank].rearrange("p (t d) -> p t d", t=2)
                    v.tensor_tensor(yb, src, wide(ga, 1, 2), ALU.mult).then_inc(bank_free[bank], 1)
                    emptied(dve, ("O", p), b)
                    chained(b, v.tensor_tensor(xt(b, 2 * p, 2), xt(b, 2 * p, 2), yb, ALU.add))
                layer_stats(b, b)
                dve.wait_ge(rstd_ready, (b * 2 + 3) if not last else 2 * B)
                dve.wait_ge(h2_free, b + 1)
                for hf in range(2):
                    normed(b, hf, h2)
                bank = filled(dve, ("G",), b)
                v.tensor_tensor(lg[:], psM[:, bank, 0:NT * E].rearrange("p (t e) -> p t e", e=E),
                                wide(bg[:].unsqueeze(1), 1, NT), ALU.add).then_inc(bank_free[bank], 1)
                emptied(dve, ("G",), b)
                hold(dve)
                for t in range(NT):
                    ins = v.max(top[:, t], lg[:, t])
                chained(b, ins)
                v.tensor_tensor(gap[:, 0], top[:, :, 1], top[:, :, 0], ALU.subtract).then_inc(gap_ready, 1)
                for t in range(NT):
                    ins = v.max_index(topi[:, t], top[:, t], lg[:, t])
                chained(b, ins)
                chained(b, v.tensor_copy(topf[:], topi[:]))
                for c in range(TOPK):
                    ins = v.tensor_tensor(oh[:, c], wide(eio[:].unsqueeze(1), 1, NT),
                                          wide(topf[:, :, c:c + 1], 2, E), ALU.is_equal)
                chained(b, ins)
                v.tensor_tensor(label[:], oh[:, 0], oh[:, 1], ALU.add)
                chained(b, v.tensor_tensor(rw[:, 0], oh[:, 0], oh[:, 1], ALU.add))
                chained(b, v.tensor_reduce(lsum[:], rw[:, 0].rearrange("p t e -> p e t"), AX.X, ALU.add))
                v.tensor_copy(lsumb[:], lsum[:]).then_inc(label_ready, 1)
                bank = filled(dve, ("C",), b)
                cum = psM[:, bank, 0:NT * E].rearrange("p (t e) -> p t e", e=E)
                chained(b, v.tensor_tensor(rw[:, 0], cum, wide(seqb[:].unsqueeze(1), 1, NT), ALU.add))
                chained(b, v.tensor_tensor(seqb[:], psM[:, bank, NT * E:NT * E + E], seqb[:], ALU.add))
                v.tensor_copy(lsum[:], psM[:, bank, 0:E]).then_inc(bank_free[bank], 1)
                v.tensor_scalar(rw[:, 1], rw[:, 0], float(CAP), None, ALU.is_le)
                chained(b, v.tensor_tensor(rw[:, 2], rw[:, 0], wide(ebase[:].unsqueeze(1), 1, NT), ALU.add))
                chained(b, v.tensor_tensor(rw[:, 0], rw[:, 1], rw[:, 2], ALU.mult))
                for c in range(TOPK):
                    ins = v.tensor_tensor(rw[:, 2 + c], rw[:, 0], oh[:, c], ALU.mult)
                chained(b, ins)
                for c in range(TOPK):
                    ins = v.tensor_reduce(slotf[:, c], rw[:, 2 + c], AX.X, ALU.add)
                chained(b, ins)
                v.tensor_scalar_add(slotb[:], slotf[:], float(TRASH)).then_inc(slot_ready, 1)
                dve.wait_ge(slot_ready, b + 1)
                if isinstance(b, int):
                    sl, wt = slot_of[:, b], weight_of[:, b]
                else:
                    sl, wt = slot_of[:, bass.ds(b, 1)][:, 0], weight_of[:, bass.ds(b, 1)][:, 0]
                chained(b, v.tensor_copy(sl, slotb[:]))
                dve.wait_ge(gap_exp, b + 1)
                chained(b, v.tensor_scalar_add(gap[:, 2], gap[:, 1], 1.0))
                chained(b, v.reciprocal(gap[:, 2], gap[:, 2]))
                v.tensor_copy(wt[:, 0], gap[:, 2])
                chained(b, v.tensor_tensor(wt[:, 1], gap[:, 1], gap[:, 2], ALU.mult))
                assert per[0] == (DVE_BODY if not last else DVE_LAST), per[0]

            with dve.Fori(0, B - 1) as b:
                body(b, False)
            body(B - 1, True)


        @block.tensor
        def _(pe):
            mm, tr = nc.tensor.matmul, nc.tensor.transpose
            pe.sem_inc(pv_done, NPROB)
            for f in range(2):
                pe.wait_ge(wm_in, 16 * (f + 1))
                for b in range(B):
                    pe.wait_ge(silu_r, DC)
                    bank = claim(pe, ("R", b, f), None)
                    for a in range(DC):
                        ins = mm(psM[:, bank], silc[:, a, b], wm[:, a], start=a == 0, stop=a == DC - 1)
                    ins.then_inc(bank_ready[bank], 1)
            pe.wait_ge(wm_in, 48)
            bank = claim(pe, ("MT",), None)
            for z in range(2 * DC):
                for a in range(DC):
                    ins = mm(psM[:, bank, B * z:B * (z + 1)], wm[:, a, P * z:P * (z + 1)], sc[:, 0, a],
                             start=a == 0, stop=a == DC - 1)
            ins.then_inc(bank_ready[bank], 1)

            def turn(name, b, src, ready, count):
                _, c, d = name
                pe.wait_ge(ready, count)
                bank = claim(pe, name, b)
                for t in range(4):
                    ins = tr(psM[:, bank, P * t:P * (t + 1)], src[:, t, P * d:P * (d + 1)], identf[:])
                ins.then_inc(bank_ready[bank], 1)

            def turn_x(name, b):
                turn(name, b, xn, xn_ready, name[1] + 1 if b is None else b * 4 + (3 + name[1]))

            def project(name, b):
                _, c, w, eo = name
                for d in range(DC):
                    emptied(pe, ("T", c, d), b)
                bank = claim(pe, name, b)
                for a in range(DC):
                    ins = mm(psM[:, bank], wq[:, w, a, P * eo:P * (eo + 1)], h1T[:, a, BANK * c:BANK * (c + 1)],
                             start=a == 0, stop=a == DC - 1)
                ins.then_inc(bank_ready[bank], 1)

            def values(p, b):
                bank = claim(pe, ("V", p), b)
                for t in range(2):
                    for a in range(DC):
                        ins = mm(psM[:, bank, D * t:D * (t + 1)], h1T[:, a, P * (2 * p + t):P * (2 * p + t + 1)],
                                 wv[:, a], start=a == 0, stop=a == DC - 1)
                ins.then_inc(bank_ready[bank], 1)

            def maxima_turn(g, b, count):
                pe.wait_ge(mp_ready, count)
                bank = claim(pe, ("M", g), b)
                cols = mp[:].rearrange("p z h t -> p (z h) t")
                for i in range(NT):
                    ins = tr(psM_bf16[bank][0:3 * HU, P * i:P * (i + 1)], cols[:, :, i], ident[:])
                ins.then_inc(bank_ready[bank], 1)

            def first_pass(b, g, i):
                s = g % 2
                if i == 0:
                    pe.wait_ge(stk_ready[s], (b * 2 + (g // 2 + 1)) * (16 * STK_DMAS))
                k = MAX_BASE[i]
                for _, a, e, heads in max_tiles(i):
                    pe.wait_ge(s_maxed, unit(b, g) * UT + (k + 1))
                    w = e - a
                    for n, h in enumerate(heads):
                        out = psS[:, k % 2, w * n:w * (n + 1)]
                        diag = e == P * (i + 1)
                        ins = mm(out, stk[0:MROW, s, 0, h, P * i:P * (i + 1)], stk[0:MROW, s, 1, h, a:e],
                                 start=True, stop=not diag)
                        if diag:
                            ins = mm(out[:, w - P:w], ident[:], mask_k[:], start=False, stop=True)
                    ins.then_inc(s_ready, 1)
                    k += 1

            def second_pass(b, g, j, k, a, e, tiles):
                s = g % 2
                for heads in tiles:
                    pe.wait_ge(exp_done, unit(b, g) * UT + (k + 1))
                    w = e - a
                    for n, h in enumerate(heads):
                        out = psT[:, k % 2, w * n:w * (n + 1)]
                        diag = a == P * j
                        ins = mm(out, stk[:, s, 1, h, P * j:P * (j + 1)], stk[:, s, 0, h, a:e],
                                 start=True, stop=not diag)
                        if diag:
                            ins = mm(out[:, 0:P], ident[:], mask_q[:], start=False, stop=True)
                    ins.then_inc(t_ready, 1)
                    k += 1

            def weigh(b, g, j, k, a, e, tiles):
                hf, w = a // BANK, e - a
                pe.wait_ge(exp_done, unit(b, g) * UT + (k + len(tiles) + 2))
                if j == 0:
                    pe.wait_ge(pv_copied, unit(b, g) * 2 + (hf + 1))
                for n, heads in enumerate(tiles):
                    slot = (g * UT + k + n) % NPROB
                    for m, h in enumerate(heads):
                        ins = mm(psO[32 * h:32 * h + 32, hf, a - BANK * hf:e - BANK * hf], va[:, j, HU * g + h],
                                 prob[:, slot, w * m:w * (m + 1)], start=j == 0,
                                 stop=j == (NT // 2 - 1 if hf == 0 else NT - 1), tile_position=(0, 32 * h),
                                 skip_group_check=True)
                    ins.then_inc(pv_done, 1)

            pe.wait_ge(consts, CONSTS)
            pe.wait_ge(minus_ones, 2)
            for name in NEXT_T:
                turn_x(name, None)
            pe.wait_ge(w_in, 16 * 11)
            for name in NEXT_QK:
                project(name, None)
            for i in range(NT):
                first_pass(0, 0, i)
            maxima_turn(0, None, 1)
            for p in range(NT // 2):
                values(p, None)

            def body(b, last):
                for g in range(NU):
                    held = None
                    pe.wait_ge(mrow_ready[g % 2], (b * 2 + (g // 2 + 1)) * 48)
                    if g == 0:
                        pe.wait_ge(v_ready, b * (NT // 2) + NT // 2)
                    for j in range(NT):
                        k = ATT_BASE[j]
                        for a, e, tiles in att_quads(j):
                            second_pass(b, g, j, k, a, e, tiles)
                            if held:
                                weigh(*held)
                            held = (b, g, j, k, a, e, tiles)
                            k += len(tiles)
                        if g < NU - 1:
                            first_pass(b, g + 1, j)
                        elif not last and j >= 4:
                            first_pass(b + 1, 0, 2 * j - 8)
                            first_pass(b + 1, 0, 2 * j - 7)
                        if g == 1 and j % 2 == 0 and not last:
                            turn_x(NEXT_T[j // 2], b)
                        if g == 2 and j % 2 and not last:
                            for eo in range(2):
                                project(NEXT_QK[(j // 2) * 2 + eo], b)
                    weigh(*held)
                    if g < NU - 1:
                        maxima_turn(g + 1, b, b * NU + (g + 2))
                    elif not last:
                        maxima_turn(0, b, b * NU + (NU + 1))
                if not last:
                    for p in range(NT // 2):
                        values(p, b)
                pe.wait_ge(attn_ready, b * (2 * NU) + (2 * NU + 1))
                for p in range(NT // 2):
                    bank = claim(pe, ("O", p), b)
                    for t in range(2):
                        ts = slice(P * (2 * p + t), P * (2 * p + t + 1))
                        for g in range(NU):
                            ins = mm(psM[:, bank, D * t:D * (t + 1)], attnT[:, g, ts], wo[:, g],
                                     start=g == 0, stop=g == NU - 1)
                    ins.then_inc(bank_ready[bank], 1)
                for c in range(CH):
                    for d in range(DC):
                        turn(("T2", c, d), b, h2[:, 4 * c:4 * c + 4], h2m_ready, b * 2 + (c + 1))
                for c in range(CH):
                    for d in range(DC):
                        emptied(pe, ("T2", c, d), b)
                bank = claim(pe, ("G",), b)
                for t in range(NT):
                    for a in range(DC):
                        ins = mm(psM[:, bank, E * t:E * (t + 1)], h1T[:, a, P * t:P * (t + 1)], wg[:, a],
                                 start=a == 0, stop=a == DC - 1)
                ins.then_inc(bank_ready[bank], 1)
                pe.wait_ge(label_ready, b + 1)
                bank = claim(pe, ("C",), b)
                mm(psM[:, bank, 0:NT * E], tri[:], label[:].rearrange("p t e -> p (t e)"), start=True, stop=False)
                for t in range(NT - 1):
                    mm(psM[:, bank, E * (t + 1):NT * E], ones[:],
                       wide(label[:, t:t + 1], 1, NT - 1 - t), start=False, stop=t == NT - 2)
                mm(psM[:, bank, NT * E:NT * E + E], ones[:], lsumb[:], start=True,
                   stop=True).then_inc(bank_ready[bank], 1)

            with pe.Fori(0, B - 1) as b:
                body(b, False)
            body(B - 1, True)


def expert_block(nc, io, disp, outs):
    NTE = CAP // P
    HC = H // P
    HS = CAP // 2
    STEPS = 2 * HC
    with ExitStack() as ctx:
        def sb(name, shape, dt=F32):
            return ctx.enter_context(nc.sbuf_tensor(name, shape, dt))

        def sem(name):
            return ctx.enter_context(nc.semaphore(name))

        w12 = sb("w12", [P, 2, 2, DC, H])
        w3 = sb("w3", [P, 2, HC, D])
        dx = sb("dx", [P, 2, NTE, D])
        dT = sb("dT", [P, DC, CAP])
        hT = sb("hT", [P, HC, CAP])
        sg = sb("sg", [P, 2, HS])
        eo = sb("eo", [P, 2, NTE, D])
        fid = sb("fid", [P, P])
        zrow = sb("zrow", [1, D])
        psH = ctx.enter_context(nc.psum_tensor("psH", [P, 2, 2, BANK], F32))
        psY = ctx.enter_context(nc.psum_tensor("psY", [P, 2, BANK], F32))
        fid_ready = sem("fid_ready")
        zr_ready = sem("zr_ready")
        w_ready = [sem(f"w_ready{i}") for i in range(2)]
        y_ready = [sem(f"y_ready{i}") for i in range(2)]
        y_free = [sem(f"y_free{i}") for i in range(2)]
        pair_ready = sem("pair_ready")
        silu_done = sem("silu_done")
        h_done = sem("h_done")
        expert_done = sem("expert_done")
        eo_ready = sem("eo_ready")
        stored = sem("stored")
        eo_free = sem("eo_free")
        zrow_stored = sem("zrow_stored")
        TURNS = [(d, g) for d in range(DC) for g in range(2)]
        OUTS = [(0, 1), (2, 3), (4,)]
        USES = len(TURNS) + len(OUTS)
        block = ctx.enter_context(nc.Block())

        def y_use(i, e2, k):
            k += USES * e2
            return k % 2, i * USES + (k // 2 + 1)

        def turn_cols(d, g):
            return (0, 4 * P) if g == 0 else (4 * P, CAP)

        @block.sync
        def _(sp):
            sp.wait_ge(zr_ready, 1)
            sp.dma_start(outs[TRASH:TRASH + 1, :], zrow[:]).then_inc(zrow_stored, 16)
            sp.wait_ge(zrow_stored, 16)
            with sp.Fori(0, E // 2) as i:
                for e2 in range(2):
                    sp.wait_ge(expert_done, i * 2 + (e2 + 1))
                    ex = bass.ds(i * 2 + e2, 1)
                    for w, src in enumerate((io["w1"], io["w2"])):
                        sp.dma_start(w12[:, e2, w], src[ex].rearrange("e (a p) n -> p (e a) n", p=P)).then_inc(w_ready[e2], 16)
                    sp.dma_start(w3[:, e2], io["w3"][ex].rearrange("e (a p) n -> p (e a) n", p=P)).then_inc(w_ready[e2], 16)
                    sp.dma_start(dx[:, e2], disp.rearrange("(e t p) n -> e p t n", e=E, p=P)[ex]
                                 .rearrange("e p t n -> p (e t) n")).then_inc(w_ready[e2], 16)

        @block.gpsimd
        def _(pool):
            pool.sem_inc(eo_free, 2)
            nc.gpsimd.memset(fid[:], 0.0).then_inc(fid_ready, 1)
            nc.gpsimd.memset(zrow[:], 0.0).then_inc(zr_ready, 1)
            pool.wait_ge(fid_ready, 1)
            nc.gpsimd.affine_select(out=fid[:], in_=fid[:], compare_op=ALU.not_equal, fill=1.0, base=0,
                                    pattern=[[-1, P]], channel_multiplier=1).then_inc(fid_ready, 1)
            with pool.Fori(0, E // 2) as i:
                for e2 in range(2):
                    pool.wait_ge(eo_ready, i * (2 * len(OUTS)) + (len(OUTS) * (e2 + 1)))
                    pool.dma_start(outs[0:TRASH].rearrange("(e t p) n -> e p t n", e=E, p=P)[bass.ds(i * 2 + e2, 1)]
                                   .rearrange("e p t n -> p (e t) n"), eo[:, e2]).then_inc(stored, 16)
                    pool.wait_ge(stored, i * 32 + 16 * (e2 + 1))
                    pool.sem_inc(eo_free, 1)

        @block.tensor
        def _(pe):
            mm, tr = nc.tensor.matmul, nc.tensor.transpose
            pe.sem_inc(expert_done, 2)
            pe.wait_ge(fid_ready, 2)
            with pe.Fori(0, E // 2) as i:
                for e2 in range(2):
                    pe.wait_ge(w_ready[e2], i * 64 + 64)
                    for k, (d, g) in enumerate(TURNS):
                        bank, n = y_use(i, e2, k)
                        pe.wait_ge(y_free[bank], n)
                        a, e = turn_cols(d, g)
                        for t in range(a // P, e // P):
                            ins = tr(psY[:, bank, P * t - a:P * (t + 1) - a], dx[:, e2, t, P * d:P * (d + 1)], fid[:])
                        ins.then_inc(y_ready[bank], 1)
                    for k in range(2):
                        bank, n = y_use(i, e2, len(TURNS) - 1 - k)
                        pe.wait_ge(y_free[bank], n + 1)
                    for r in range(STEPS):
                        hc, s = divmod(r, 2)
                        pe.wait_ge(h_done, i * (2 * STEPS) + (STEPS * e2 + r + 1))
                        for w in range(2):
                            for a in range(DC):
                                ins = mm(psH[:, r % 2, w, 0:HS], w12[:, e2, w, a, P * hc:P * (hc + 1)],
                                         dT[:, a, HS * s:HS * (s + 1)], start=a == 0, stop=a == DC - 1)
                        ins.then_inc(pair_ready, 1)
                    pe.wait_ge(h_done, i * (2 * STEPS) + (STEPS * (e2 + 1) + 2))
                    for k, tiles in enumerate(OUTS):
                        bank, n = y_use(i, e2, len(TURNS) + k)
                        pe.wait_ge(y_free[bank], n)
                        for m, t in enumerate(tiles):
                            for hc in range(HC):
                                ins = mm(psY[:, bank, D * m:D * (m + 1)], hT[:, hc, P * t:P * (t + 1)], w3[:, e2, hc],
                                         start=hc == 0, stop=hc == HC - 1)
                        ins.then_inc(y_ready[bank], 1)
                    pe.wait_ge(y_ready[bank], n)
                    pe.sem_inc(expert_done, 1)

        @block.scalar
        def _(act):
            with act.Fori(0, E // 2) as i:
                for e2 in range(2):
                    for r in range(STEPS):
                        act.wait_ge(pair_ready, i * (2 * STEPS) + (STEPS * e2 + r + 1))
                        nc.scalar.activation(sg[:, r % 2], psH[:, r % 2, 0, 0:HS], ACT.Silu).then_inc(silu_done, 1)
                    act.wait_ge(eo_free, i * 2 + (e2 + 1))
                    for k, tiles in enumerate(OUTS):
                        bank, n = y_use(i, e2, len(TURNS) + k)
                        act.wait_ge(y_ready[bank], n)
                        nc.scalar.copy(eo[:, e2, tiles[0]:tiles[-1] + 1].rearrange("p t d -> p (t d)"),
                                       psY[:, bank, 0:D * len(tiles)]).then_inc(y_free[bank], 1)
                        act.wait_ge(y_free[bank], n + 1)
                        act.sem_inc(eo_ready, 1)

        @block.vector
        def _(dve):
            dve.sem_inc(h_done, 2)
            for bank in range(2):
                dve.sem_inc(y_free[bank], 1)
            with dve.Fori(0, E // 2) as i:
                for e2 in range(2):
                    for k, (d, g) in enumerate(TURNS):
                        bank, n = y_use(i, e2, k)
                        dve.wait_ge(y_ready[bank], n)
                        a, e = turn_cols(d, g)
                        nc.vector.tensor_copy(dT[:, d, a:e], psY[:, bank, 0:e - a]).then_inc(y_free[bank], 1)
                    for r in range(STEPS):
                        hc, s = divmod(r, 2)
                        dve.wait_ge(silu_done, i * (2 * STEPS) + (STEPS * e2 + r + 1))
                        nc.vector.tensor_tensor(hT[:, hc, HS * s:HS * (s + 1)], psH[:, r % 2, 1, 0:HS], sg[:, r % 2],
                                                ALU.mult).then_inc(h_done, 1)


def combine_block(nc, io, outs, keep):
    x, modrow, slot_of, weight_of = keep["x"], keep["modrow"], keep["slot"], keep["weight"]
    G = 4
    with ExitStack() as ctx:
        def sb(name, shape, dt=F32):
            return ctx.enter_context(nc.sbuf_tensor(name, shape, dt))

        def sem(name):
            return ctx.enter_context(nc.semaphore(name))

        slots = sb("slots", [P, 2, TOPK, NT], U32)
        rows = sb("rows", [P, 4, TOPK, G, D])
        y = sb("y", [P, 2, G, D])
        slots_ready = sem("slots_ready")
        gathered = [sem(f"gathered{i}") for i in range(4)]
        rows_used = sem("rows_used")
        y_step = sem("y_step")
        x_ready = sem("x_ready")
        stored = sem("out_stored")
        block = ctx.enter_context(nc.Block())

        @block.gpsimd
        def _(pool):
            for b in range(B):
                pool.wait_ge(slots_ready, b + 1)
                for h in range(2):
                    step = 2 * b + h
                    if step >= 4:
                        pool.wait_ge(rows_used, step - 3)
                    for t in range(G):
                        for c in range(TOPK):
                            nc.gpsimd.indirect_dma_start(
                                rows[:, step % 4, c, t], None, outs[:, :],
                                bass.IndirectOffsetOnAxis(ap=slots[:, b % 2, c, G * h + t:G * h + t + 1], axis=0),
                            ).then_inc(gathered[step % 4], 16)

        @block.vector
        def _(dve):
            v = nc.vector
            for b in range(2):
                v.tensor_copy(slots[:, b], slot_of[:, b]).then_inc(slots_ready, 1)
            for b in range(B):
                for h in range(2):
                    step = 2 * b + h
                    s = step % 4
                    dve.wait_ge(gathered[s], 16 * G * TOPK * (step // 4 + 1))
                    for t in range(G):
                        n = G * h + t
                        v.tensor_scalar(y[:, step % 2, t], rows[:, s, 0, t], weight_of[:, b, 0, n:n + 1], None,
                                        ALU.mult).then_inc(y_step, 1)
                    dve.wait_ge(y_step, step * 10 + 4)
                    for t in range(G):
                        n = G * h + t
                        v.scalar_tensor_tensor(out=y[:, step % 2, t], in0=rows[:, s, 1, t],
                                               scalar=weight_of[:, b, 1, n:n + 1], in1=y[:, step % 2, t],
                                               op0=ALU.mult, op1=ALU.add).then_inc(y_step, 1)
                    dve.wait_ge(y_step, step * 10 + 8)
                    v.tensor_tensor(y[:, step % 2], y[:, step % 2], wide(modrow[:, b:b + 1, 3], 1, G),
                                    ALU.mult).then_inc(y_step, 1)
                    dve.wait_ge(y_step, step * 10 + 9)
                    xs = x[:, NT * b + G * h:NT * b + G * (h + 1), :]
                    v.tensor_tensor(xs, xs, y[:, step % 2], ALU.add).then_inc(x_ready, 1)
                    v.tensor_copy(slots[:, b % 2, 0, 0:1], slots[:, b % 2, 0, 0:1]) if False else None
                    dve.wait_ge(x_ready, step + 1)
                    dve.sem_inc(rows_used, 1)
                    dve.sem_inc(y_step, 1)
                if b + 2 < B:
                    v.tensor_copy(slots[:, b % 2], slot_of[:, b + 2]).then_inc(slots_ready, 1)

        @block.sync
        def _(sp):
            for step in range(2 * B):
                sp.wait_ge(x_ready, step + 1)
                sp.dma_start(io["out"][G * P * step:G * P * (step + 1), :].rearrange("(t p) d -> p t d", p=P),
                             x[:, G * step:G * (step + 1), :]).then_inc(stored, 16)
            sp.wait_ge(stored, 16 * 2 * B)


def build(nc, io):
    disp = nc.dram_tensor("disp", (TRASH, D), F32, kind="Internal").ap()
    io["scr"] = nc.dram_tensor("scr", (2, 2, 3, 2, 32, S), BF16, kind="Internal").ap()
    outs = nc.dram_tensor("outs", (TRASH + 1, D), F32, kind="Internal").ap()
    with (
        nc.sbuf_tensor("x_rows", [P, B * NT, D], F32) as x,
        nc.sbuf_tensor("mod_rows", [P, B, 4, D], F32) as modrow,
        nc.sbuf_tensor("slot_of", [P, B, TOPK, NT], U32) as slot_of,
        nc.sbuf_tensor("weight_of", [P, B, TOPK, NT], F32) as weight_of,
    ):
        keep = {"x": x, "modrow": modrow, "slot": slot_of, "weight": weight_of}
        attention_block(nc, io, disp, keep)
        expert_block(nc, io, disp, outs)
        combine_block(nc, io, outs, keep)


def kernel(**inputs):
    import concourse.bacc as bacc
    from concourse.bass_utils import run_bass_kernel_spmd

    g = {k.removeprefix("L0_"): np.asarray(a) for k, a in inputs.items()}
    heads = np.arange(NH).reshape(NU, 1, HU) * DK
    pairs = np.arange(0, DK, 2).reshape(1, -1, 1)
    order = np.concatenate([(heads + pairs).ravel(), (heads + pairs + 1).ravel()])
    freq = (1.0 / np.float32(10000.0) ** (np.arange(0, DK, 2, dtype=np.float32) / DK)).astype(np.float32)
    angle = np.arange(S, dtype=np.float32)[None, :] * freq[:, None]
    arrays = {
        "x": g["attn_x"].reshape(T, D),
        "wq": g["attn_Wq"][order].T,
        "wk": g["attn_Wk"][order].T,
        "wv": g["attn_Wv"].T,
        "wo": g["attn_Wo"].T,
        "wg": g["ffn_Wg"],
        "bg": g["ffn_bg"],
        "w1": g["ffn_W1"],
        "w2": g["ffn_W2"],
        "w3": g["ffn_W3"],
        "cT": g["c"].T,
        "wmod": g["wmod"].reshape(D, 3, 2 * D).transpose(1, 0, 2)[[1, 2, 0]],
        "cos": np.tile(np.repeat(np.cos(angle), HU, 0), (NU, 1)),
        "sin": np.tile(np.repeat(np.sin(angle), HU, 0), (NU, 1)),
    }
    arrays = {f"in_{k}": np.ascontiguousarray(a) for k, a in arrays.items()}
    nc = bacc.Bacc("TRN2", target_bir_lowering=False, num_devices=1)
    io = {k[3:]: nc.dram_tensor(k, a.shape, mybir.dt.from_np(a.dtype), kind="ExternalInput").ap()
          for k, a in arrays.items()}
    io["out"] = nc.dram_tensor("out", (T, D), F32, kind="ExternalOutput").ap()
    build(nc, io)
    r = run_bass_kernel_spmd(nc, [arrays], core_ids=[0])
    return r.results[0]["out"].reshape(B, S, D)
```

```python
from contextlib import ExitStack

import concourse.bass as bass
import numpy as np
from concourse import mybir

F32 = mybir.dt.float32
BF16 = mybir.dt.bfloat16
U32 = mybir.dt.uint32
ALU = mybir.AluOpType
ACT = mybir.ActivationFunctionType
AX = mybir.AxisListType

P = 128
B, S, D = 4, 1024, 256
NH, DK = 16, 16
E, H, TOPK = 8, 1024, 2
T = B * S
CAP = int(T / E * 1.25)
TRASH = E * CAP
EPS = 1e-5
BIG = 1.0e30
DC = D // P
NT = S // P
HU = 4
NU = NH // HU
BANK = 512
CH = S // BANK
SLOTS = ((0, 48), (48, 32), (80, 16))
MROW = 96
STACK = MROW + 2
STK_DMAS = 3 + 6


def spans(lo, hi):
    return [(a, b) for a, b in ((lo, min(hi, BANK)), (max(lo, BANK), hi)) if a < b]


def bank_tiles(lo, hi):
    out = []
    for s, (a, b) in enumerate(spans(lo, hi)):
        n = min(HU, BANK // (b - a))
        out += [(s, a, b, list(range(h, h + n))) for h in range(0, HU, n)]
    return out


def wide(ap, axis, n):
    shape = list(ap.shape)
    shape[axis] = n
    return ap.broadcast_to(tuple(shape))


MAX_TILES = [(i, *t) for i in range(NT) for t in bank_tiles(0, P * (i + 1))]
ATT_TILES = [(j, *t) for j in range(NT) for t in bank_tiles(P * j, S)]
QUAD_END = [n for n, t in enumerate(ATT_TILES) if t[4][-1] == HU - 1]
HALF_END = [max(n for n, t in enumerate(ATT_TILES) if t[2] // BANK == h) for h in range(2)]
UT = len(ATT_TILES)
MAX_HALF = [t[0] for t in MAX_TILES].index(NT // 2)
PAST_HALF = [t[0] for t in ATT_TILES].index(NT // 2)
NPROB = 8
assert len(MAX_TILES) == UT and UT % 2 == 0 and (NU * UT) % NPROB == 0

MAX_FROM, MAX_TO = 0, 28
MAX_AT = [range(0)] * UT
for _n in range(MAX_FROM, MAX_TO):
    MAX_AT[_n] = range(UT * (_n - MAX_FROM) // (MAX_TO - MAX_FROM), UT * (_n + 1 - MAX_FROM) // (MAX_TO - MAX_FROM))

EVERY = [(9, "recip"), (28, "maxparts"), (31, "M"), (33, "mT")]
POST = {0: [(14, "O0"), (16, "O1"), (18, "O2"), (20, "O3"), (21, "stats2"), (26, "norm2a"), (30, "norm2b"),
            (35, "T2a"), (36, "T2b")],
        1: [(2, "T2c"), (3, "T2d"), (6, "G"), (7, "route1"), (11, "C"), (12, "route2")]}
PRE = {1: [(14, "stats1"), (16, "norm1a"), (19, "Ta"), (20, "Tb"), (21, "norm1b"), (25, "Tc"), (26, "Td"),
           (29, "QK0"), (32, "rot0"), (34, "sub0"), (36, "low0")],
       2: [(0, "QK1"), (3, "rot1"), (5, "sub1"), (7, "low1"),
           (11, "QK2"), (14, "rot2"), (16, "sub2"), (18, "low2"),
           (22, "QK3"), (25, "rot3"), (27, "sub3"), (29, "low3")]}


def steps(kind, g):
    out = list(EVERY)
    if kind == "last" and g == NU - 1:
        out = [x for x in out if x[1] == "recip"]
    if kind in ("turn", "last"):
        out += POST.get(g, [])
    if kind in ("first", "turn"):
        out += PRE.get(g, [])
    return sorted(out, key=lambda x: x[0])


POST_STEPS = [n for g in range(2) for _, n in POST[g]]
PRE_STEPS = ["stats1", "norm1a", "Ta", "Tb", "norm1b", "Tc", "Td"] + [
    f"{s}{n}" for n in range(4) for s in ("QK", "rot", "sub", "low")]
LETTER = {"a": (0, 0), "b": (0, 1), "c": (1, 0), "d": (1, 1)}


def uses(name, g=0):
    if name == "M":
        return [("M", (g + 1) % NU)]
    if name[:2] == "QK":
        return [(name, 0), (name, 1)]
    return [(name,)] if name[0] in "OGCT" else []


V_USES = [("V", p) for p in range(NT // 2)]
SEQ = {"init": [("MT",)] + [u for n in PRE_STEPS for u in uses(n)]
       + [("R", b, f) for f in range(2) for b in range(B)] + [("M", 0)] + V_USES}
for _kind in ("first", "turn", "last"):
    SEQ[_kind] = [u for g in range(NU) for _, n in steps(_kind, g) for u in uses(n, g)]
    if _kind != "last":
        SEQ[_kind] += V_USES
SEQ["tail"] = [u for n in POST_STEPS for u in uses(n)]
TURNS = B - 2
START = {"init": 0, "first": len(SEQ["init"])}
START["turn"] = START["first"] + len(SEQ["first"])
START["last"] = START["turn"] + TURNS * len(SEQ["turn"])
START["tail"] = START["last"] + len(SEQ["last"])
assert len(SEQ["turn"]) % 2 == 0
CONSTS = 11
MINUS_ONES = float(np.array([0xBF80BF80], np.uint32).view(np.float32)[0])


class Turn:

    def __init__(self, reg, mul=1, add=0):
        self.reg, self.mul, self.add = reg, mul, add

    def __add__(self, n):
        return Turn(self.reg, self.mul, self.add + n)

    def __sub__(self, n):
        return self + -n

    def __mul__(self, n):
        return Turn(self.reg, self.mul * n, self.add * n)


def apart(n):
    return Turn(n.reg + 1, n.mul, n.add - n.mul) if isinstance(n, Turn) else n


def val(n):
    if not isinstance(n, Turn):
        return n
    v = n.reg * n.mul if n.mul > 1 else n.reg
    return v + n.add if n.add else v


class Counter:

    def __init__(self, eng, sem, per):
        self.eng, self.sem, self.per, self.n = eng, sem, per, 0
        self.base = {"init": 0, "first": per["init"]}
        self.base["turn"] = self.base["first"] + per["first"]
        self.base["last"] = self.base["turn"] + TURNS * per["turn"]
        self.base["tail"] = self.base["last"] + per["last"]

    def step(self, at, ins):
        kind, pb = at
        self.n += 1
        ins.then_inc(self.sem, 1)
        if kind == "turn":
            self.eng.wait_ge(self.sem, val(pb * self.per["turn"] + (self.base[kind] + self.n)))
        else:
            self.eng.wait_ge(self.sem, val(self.base[kind] + self.n))

    def close(self, kind):
        assert self.n == self.per[kind], (kind, self.n)
        self.n = 0


POOL_STEPS = {"init": 1, "first": 0, "turn": 2, "last": 2, "tail": 2}
DVE_STEPS = {"init": 16, "first": 10, "turn": 30, "last": 26, "tail": 20}


def attention_block(nc, io, disp, keep):
    x, modrow, slot_of, weight_of = keep["x"], keep["modrow"], keep["slot"], keep["weight"]
    ctx = ExitStack()
    with ctx:
        def sb(name, shape, dt=F32):
            return ctx.enter_context(nc.sbuf_tensor(name, shape, dt))

        def sem(name):
            return ctx.enter_context(nc.semaphore(name))

        wq = sb("wq", [P, 2, DC, D])
        wv = sb("wv", [P, DC, D])
        wo = sb("wo", [P, NU, D])
        wg = sb("wg", [P, DC, E])
        bg = sb("bg", [P, E])
        rope = sb("rope", [P, 2, S])
        cT = sb("cT", [P, DC, B])
        sc = sb("sc", [P, 3, DC, B])
        modT = sb("modT", [P, 2 * DC, B])
        identf = sb("identf", [P, P])
        ident = sb("ident", [P, P], BF16)
        mask_k = sb("mask_k", [P, P], BF16)
        mask_q = sb("mask_q", [P, P], BF16)
        tri = sb("tri", [P, P], BF16)
        ones = sb("ones", [P, P], BF16)
        half = sb("half", [P, NT])
        eio = sb("eio", [P, E])
        ebase = sb("ebase", [P, E])
        stats = sb("stats", [P, 2, NT, 6])
        meanvar = sb("meanvar", [P, 2, NT, 2])
        vareps = sb("vareps", [P, 2, NT])
        rstd = sb("rstd", [P, 2, NT])
        xn = sb("xn", [P, 4, D])
        hT = sb("hT1", [P, DC, S])
        rt = sb("rt", [P, 2, 4, BANK])
        parts = sb("parts", [P, 2, 3, 2, BANK], BF16)
        va = sb("va", [P, NT, NH, 32])
        stk = sb("stk", [STACK, 2, 2, HU, S], BF16)
        mx = sb("mx", [P, 2, HU, NT])
        mxr = sb("mxr", [P, HU, NT])
        mp = sb("mp", [P, 2, HU, NT], BF16)
        mT = sb("mT", [2 * HU, S], BF16)
        prob = sb("prob", [P, NPROB, BANK])
        attnT = sb("attnT", [P, NU, S])
        sums = sb("sums", [P, HU * S // P])
        rsum = sb("rsum", [P, S])
        h2 = sb("h2", [P, NT, D])
        yb = xn[:, 0:2]
        lg = sb("lg", [P, NT, E])
        top = sb("top", [P, NT, 8])
        topi = sb("topi", [P, NT, 8], U32)
        topf = sb("topf", [P, NT, 8])
        oh = sb("oh", [P, 2, NT, E])
        label = sb("label", [P, NT, E], BF16)
        lsum = sb("lsum", [P, E])
        lsumb = sb("lsumb", [P, E], BF16)
        seqb = sb("seqb", [P, E])
        rw = sb("rw", [P, 4, NT, E])
        slotf = sb("slotf", [P, 2, NT])
        slotb = sb("slotb", [P, 2, NT], U32)
        gap = sb("gap", [P, 3, NT])
        silc = prob[:, 0:2, :].rearrange("p a (b m) -> p a b m", b=B)
        wm = [h2[:, 4 * i:4 * i + 4].rearrange("p (a t) d -> p a (t d)", a=DC) for i in range(2)]

        psS = ctx.enter_context(nc.psum_tensor("psS", [P, 2, BANK], F32))
        psT = ctx.enter_context(nc.psum_tensor("psT", [P, 2, BANK], F32))
        psO = ctx.enter_context(nc.psum_tensor("psO", [P, 2, BANK], F32))
        psM = ctx.enter_context(nc.psum_tensor("psM", [P, 2, BANK], F32))
        psM_bf16 = [psM[:, i, :].bitcast(BF16) for i in range(2)]

        c_in = sem("c_in")
        wm_in = [sem(f"wm_in{i}") for i in range(3)]
        qk_in = sem("qk_in")
        w_in = sem("w_in")
        x0_in = sem("x0_in")
        x_in = sem("x_in")
        consts = sem("consts")
        wo_zero = sem("wo_zero")
        minus_ones = sem("minus_ones")
        silu_e = sem("silu_e")
        silu_r = sem("silu_r")
        zeroed = sem("zeroed")
        zero_out = sem("zero_out")
        bank_ready = [sem(f"bank_ready{i}") for i in range(2)]
        bank_free = [sem(f"bank_free{i}") for i in range(2)]
        var_ready = [sem(f"var_ready{i}") for i in range(2)]
        rstd_ready = [sem(f"rstd_ready{i}") for i in range(2)]
        xn_ready = [sem(f"xn_ready{i}") for i in range(2)]
        h2m_ready = sem("h2m_ready")
        rotated = sem("rotated")
        part0_ready = sem("part0_ready")
        rest_ready = sem("rest_ready")
        part1_ready = sem("part1_ready")
        part2_ready = sem("part2_ready")
        scr_ready = [sem(f"scr_ready{i}") for i in range(2)]
        stk_ready = [[sem(f"stk_ready{i}{ch}") for ch in range(CH)] for i in range(2)]
        mrow_ready = [sem(f"mrow_ready{i}") for i in range(2)]
        v_ready = sem("v_ready")
        s_ready = sem("s_ready")
        s_maxed = sem("s_maxed")
        mp_ready = sem("mp_ready")
        t_ready = sem("t_ready")
        exp_done = sem("exp_done")
        pv_done = sem("pv_done")
        pv_copied = sem("pv_copied")
        sums_out = sem("sums_out")
        sums_in = sem("sums_in")
        recip_done = sem("recip_done")
        recip_out = sem("recip_out")
        rsum_in = sem("rsum_in")
        attn_ready = sem("attn_ready")
        gap_ready = sem("gap_ready")
        gap_exp = sem("gap_exp")
        label_ready = sem("label_ready")
        slot_ready = sem("slot_ready")
        scattered = sem("scattered")
        h2_free = sem("h2_free")
        held_back = sem("held_back")
        dve_step = sem("dve_step")
        pool_step = sem("pool_step")

        def use(name, at):
            kind, pb = at
            k = START[kind] + SEQ[kind].index(name)
            n = k // 2 + 1
            return k % 2, (pb * (len(SEQ["turn"]) // 2) + n if kind == "turn" else n)

        def claim(pe, name, at):
            bank, n = use(name, at)
            if at[0] != "init" or n > 1:
                pe.wait_ge(bank_free[bank], val(n - 1))
            return bank

        def filled(eng, name, at):
            bank, n = use(name, at)
            eng.wait_ge(bank_ready[bank], val(n))
            return bank

        def emptied(eng, name, at):
            bank, n = use(name, at)
            eng.wait_ge(bank_free[bank], val(n))

        def unit(b, g):
            return b * NU + g

        def hold(eng):
            eng.sem_inc(held_back, 1)

        def after_unit(b, g):
            return (b, g + 1) if g < NU - 1 else (b + 1, 0)

        def program(eng, body, tail):
            body(0, ("first", None))
            with eng.Fori(0, TURNS) as turn:
                pb = Turn(turn)
                body(pb + 1, ("turn", pb))
            body(B - 1, ("last", None))
            tail(("tail", None))

        def batch(t, b, n=1, axis=1):
            return t[:, b:b + n] if isinstance(b, int) else t[:, bass.ds(val(b), n)]

        block = ctx.enter_context(nc.Block())

        @block.sync
        def _(sp):
            def rows_in(n, ap, where):
                sp.dma_start(where, ap.rearrange("(a p) n -> p a n", p=P)).then_inc(wm_in[n], 16)

            sp.dma_start(cT[:], io["cT"].rearrange("(a p) b -> p a b", p=P)).then_inc(c_in, 16)
            sp.dma_start(x[:, 0:NT, :], io["x"][0:S, :].rearrange("(t p) d -> p t d", p=P)).then_inc(x0_in, 16)
            rows_in(0, io["wmod"][0], wm[0])
            for w, src in enumerate((io["wq"], io["wk"])):
                sp.dma_start(wq[:, w], src.rearrange("(a p) n -> p a n", p=P)).then_inc(qk_in, 16)
            sp.dma_start(rope[:, 0], io["cos"]).then_inc(qk_in, 16)
            sp.dma_start(rope[:, 1], io["sin"]).then_inc(qk_in, 16)
            rows_in(1, io["wmod"][1], wm[1])
            filled(sp, ("MT",), ("init", None))
            rows_in(2, io["wmod"][2], wm[0])
            sp.dma_start(wv[:], io["wv"].rearrange("(a p) n -> p a n", p=P)).then_inc(w_in, 16)
            sp.dma_start(wg[:], io["wg"].rearrange("(a p) n -> p a n", p=P)).then_inc(w_in, 16)
            sp.dma_start(bg[:], wide(io["bg"].rearrange("(a e) -> a e", a=1), 0, P)).then_inc(w_in, 16)
            sp.wait_ge(wo_zero, 1)
            for i in range(HU):
                sp.dma_start(wo[32 * i:32 * i + DK],
                             io["wo"].rearrange("(g i d) n -> i d g n", g=NU, i=HU)[i]).then_inc(w_in, 16)

            def rest_in():
                for b in range(1, B):
                    sp.dma_start(x[:, NT * b:NT * (b + 1), :],
                                 io["x"][S * b:S * (b + 1), :].rearrange("(t p) d -> p t d", p=P)).then_inc(x_in, 16)
                sp.wait_ge(zeroed, 1)
                for r in range(0, E * CAP, 4 * P):
                    sp.dma_start(disp[r:r + 4 * P, :].rearrange("(t p) d -> p t d", p=P),
                                 attnT[:, NU - 1].rearrange("p (t d) -> p t d", t=4)).then_inc(zero_out, 16)

            def stack(b, g, ch):
                s = g % 2
                for i in range(2):
                    sp.wait_ge(scr_ready[i], val(b * 32 + 32))
                hold(sp)
                if not (isinstance(b, int) and b == 0 and g < 2):
                    sp.wait_ge(t_ready, val(unit(b, g - 2) * UT + (UT, PAST_HALF)[ch == 0]))
                    hold(sp)
                cols = slice(BANK * ch, BANK * (ch + 1))
                for w in (1, 0):
                    table = io["scr"][b:b + 1, w] if isinstance(b, int) else io["scr"][bass.ds(val(b), 1), w]
                    rows = table[:, 32 * g:32 * g + 32].rearrange("o (r i) z n -> (o z) r i n", i=HU)[:, :, :, cols]
                    for n, (r0, count) in enumerate(SLOTS):
                        if w:
                            sp.dma_start(stk[r0:r0 + count, s, 1, :, cols],
                                         rows[0:count // 8]).then_inc(stk_ready[s][ch], 16)
                        else:
                            for r in range(r0, r0 + count, 16):
                                sp.dma_start(stk[r:r + 16, s, 0, :, cols],
                                             rows[2 * n:2 * n + 2]).then_inc(stk_ready[s][ch], 16)

            def max_rows(b, g, at):
                emptied(sp, ("M", g), at)
                hold(sp)
                for part in range(2):
                    sp.dma_start(stk[MROW + part:MROW + part + 1, g % 2, 0],
                                 mT[HU * part:HU * part + HU, :]).then_inc(mrow_ready[g % 2], 16)

            def reciprocals(b, g):
                u = unit(b, g)
                sp.wait_ge(pv_copied, val(u * 2 + 4))
                hold(sp)
                sp.dma_start(io["sums"], attnT[DK:P:32, g]).then_inc(sums_out, 16)
                sp.wait_ge(sums_out, val(u * 16 + 16))
                hold(sp)
                sp.dma_start(sums[:], io["sums"].rearrange("i (p c) -> (i p) c", p=P // HU)).then_inc(sums_in, 16)
                sp.wait_ge(recip_done, val(u + 1))
                hold(sp)
                sp.dma_start(io["rsums"].rearrange("i (p c) -> (i p) c", p=P // HU), sums[:]).then_inc(recip_out, 16)
                sp.wait_ge(recip_out, val(u * 16 + 16))
                hold(sp)
                sp.wait_ge(attn_ready, val(u + 1))
                hold(sp)
                for i in range(HU):
                    sp.dma_start(rsum[32 * i:32 * i + 32], wide(io["rsums"][i:i + 1], 0, 32)).then_inc(rsum_in, 16)

            stack(0, 0, 0)
            stack(0, 0, 1)
            stack(0, 1, 0)
            max_rows(0, 0, ("init", None))

            def body(b, at):
                last = at[0] == "last"
                for g in range(NU):
                    nb, ng = after_unit(b, g)
                    n2b, n2g = after_unit(nb, ng)
                    if not (last and g == NU - 1):
                        stack(nb, ng, 1)
                    if at[0] != "first" or g:
                        reciprocals(*((b, g - 1) if g else (b - 1 if isinstance(b, int) else at[1], NU - 1)))
                    early = g != 2
                    if early and not (last and g >= NU - 2):
                        stack(n2b, n2g, 0)
                    if not (last and g == NU - 1):
                        max_rows(nb, ng, at)
                    if at[0] == "first" and g == 0:
                        rest_in()
                    if not early and not last:
                        stack(n2b, n2g, 0)

            def tail(at):
                reciprocals(B - 1, NU - 1)

            program(sp, body, tail)

        @block.gpsimd
        def _(pool):
            c = Counter(pool, pool_step, POOL_STEPS)
            tt = nc.gpsimd.tensor_tensor
            init = ("init", None)

            def step(at, ins):
                c.step(at, ins)
                hold(pool)

            pool.sem_inc(attn_ready, 1)
            pool.sem_inc(h2_free, 1)
            nc.gpsimd.memset(wo[:], 0.0).then_inc(wo_zero, 1)
            nc.gpsimd.memset(half[:], -0.5).then_inc(consts, 1)
            nc.gpsimd.memset(attnT[:, NU - 1], 0.0).then_inc(zeroed, 1)
            nc.gpsimd.memset(identf[:], 0.0)
            nc.gpsimd.memset(ident[:], 0.0)
            nc.gpsimd.memset(mask_k[:], 0.0)
            nc.gpsimd.memset(mask_q[:], 0.0)
            step(init, nc.gpsimd.memset(tri[:], 1.0))
            for t in (identf, ident):
                nc.gpsimd.affine_select(out=t[:], in_=t[:], compare_op=ALU.not_equal, fill=1.0, base=0,
                                        pattern=[[-1, P]], channel_multiplier=1).then_inc(consts, 1)
            nc.gpsimd.affine_select(out=mask_k[:], in_=mask_k[:], compare_op=ALU.is_ge, fill=-BIG, base=0,
                                    pattern=[[-1, P]], channel_multiplier=1).then_inc(consts, 1)
            nc.gpsimd.affine_select(out=mask_q[:], in_=mask_q[:], compare_op=ALU.is_ge, fill=-BIG, base=0,
                                    pattern=[[1, P]], channel_multiplier=-1).then_inc(consts, 1)
            nc.gpsimd.affine_select(out=tri[:], in_=tri[:], compare_op=ALU.is_ge, fill=0.0, base=0,
                                    pattern=[[1, P]], channel_multiplier=-1).then_inc(consts, 1)
            nc.gpsimd.memset(ones[:], 1.0).then_inc(consts, 1)
            nc.gpsimd.iota(eio[:], pattern=[[1, E]], base=0, channel_multiplier=0,
                           allow_small_or_imprecise_dtypes=True).then_inc(consts, 1)
            nc.gpsimd.iota(ebase[:], pattern=[[CAP, E]], base=-1 - TRASH, channel_multiplier=0,
                           allow_small_or_imprecise_dtypes=True).then_inc(consts, 1)
            nc.gpsimd.memset(va[:, :, :, DK:32], 1.0).then_inc(consts, 1)
            nc.gpsimd.memset(seqb[:], 0.0).then_inc(consts, 1)
            pool.wait_ge(consts, CONSTS)

            def power(which, count):
                pool.wait_ge(var_ready[which], val(count))
                hold(pool)
                tt(rstd[:, which], vareps[:, which], half[:], ALU.pow).then_inc(rstd_ready[which], 1)

            def rotate(b, at, n):
                for eo in range(2):
                    emptied(pool, (f"QK{n}", eo), at)
                hold(pool)
                r = rt[:, n % 2]
                tt(r[:, 0], r[:, 0], r[:, 3], ALU.subtract)
                tt(r[:, 1], r[:, 2], r[:, 1], ALU.add).then_inc(rotated, 1)

            def third_part(b, at, n):
                ch, w = divmod(n, 2)
                pool.wait_ge(part1_ready, val(b * 4 + (n + 1)))
                hold(pool)
                tt(parts[:, n % 2, 2], rt[:, n % 2, 0:2], parts[:, n % 2, 1], ALU.subtract).then_inc(part2_ready, 1)
                pool.wait_ge(part2_ready, val(b * 4 + (n + 1)))
                hold(pool)
                table = io["scr"][b:b + 1, w] if isinstance(b, int) else io["scr"][bass.ds(val(b), 1), w]
                pool.dma_start(table.rearrange("o q z n -> (o q) z n")[:, :, BANK * ch:BANK * (ch + 1)],
                               parts[:, n % 2].rearrange("p z e n -> p (z e) n"),
                               ).then_inc(scr_ready[n % 2], 16)

            def normalise(b, g):
                pool.wait_ge(rsum_in, val(unit(b, g) * (16 * HU) + 16 * HU))
                hold(pool)
                tt(attnT[:, g], attnT[:, g], rsum[:], ALU.mult).then_inc(attn_ready, 1)

            def modulate(pb, at, hf):
                pool.wait_ge(xn_ready[1], val(pb * 2 + (hf + 1)))
                hold(pool)
                ts = slice(4 * hf, 4 * hf + 4)
                rows = batch(modrow, pb)
                step(at, tt(h2[:, ts], h2[:, ts], wide(rows[:, :, 2], 1, 4), ALU.mult))
                tt(h2[:, ts], h2[:, ts], wide(rows[:, :, 1], 1, 4), ALU.add).then_inc(h2m_ready, 1)

            def scatter(pb, tiles):
                pool.wait_ge(slot_ready, val(pb + 1))
                pool.wait_ge(h2m_ready, val(pb * 2 + 2))
                hold(pool)
                for t in tiles:
                    for ch in range(TOPK):
                        nc.gpsimd.indirect_dma_start(
                            disp[:, :], bass.IndirectOffsetOnAxis(ap=slotb[:, ch, t:t + 1], axis=0),
                            h2[:, t], None, bounds_check=TRASH - 1, oob_is_err=False,
                        ).then_inc(scattered, 16)
                if tiles[-1] == NT - 1:
                    pool.wait_ge(scattered, val(pb * (NT * TOPK * 16) + NT * TOPK * 16))
                    pool.sem_inc(h2_free, 1)

            power(0, 1)
            for n in range(4):
                rotate(0, init, n)
                third_part(0, init, n)
            c.close("init")

            def do(name, b, g, at):
                pb = at[1] if at[0] == "turn" else b - 1
                if name == "recip" and (at[0] != "first" or g):
                    normalise(*((b, g - 1) if g else (pb, NU - 1)))
                elif name == "stats2":
                    power(1, pb + 1)
                elif name in ("norm2a", "norm2b"):
                    modulate(pb, at, name == "norm2b")
                elif name == "route2":
                    scatter(pb, range(0, 4))
                elif name == "stats1":
                    power(0, b + 2)
                elif name[:3] == "rot":
                    rotate(b + 1, at, int(name[3]))
                elif name[:3] == "low":
                    third_part(b + 1, at, int(name[3]))

            def body(b, at):
                for g in range(NU):
                    if g == 3 and at[0] == "first":
                        pool.wait_ge(zero_out, 16 * E * CAP // (4 * P))
                    if g == 3 and at[0] != "first":
                        scatter(at[1] if at[0] == "turn" else b - 1, range(4, NT))
                    for _, name in steps(at[0], g):
                        do(name, b, g, at)
                c.close(at[0])

            def tail(at):
                normalise(B - 1, NU - 1)
                for name in POST_STEPS:
                    do(name, B, 0, at)
                scatter(B - 1, range(4, NT))
                c.close(at[0])

            program(pool, body, tail)

        @block.scalar
        def _(act):
            init = ("init", None)
            act.sem_inc(exp_done, 2)
            act.sem_inc(pv_copied, 2)
            act.wait_ge(c_in, 16)
            nc.scalar.activation(sc[:, 0], cT[:], ACT.Exp, scale=-1.0).then_inc(silu_e, 1)

            def evac_T(b, name, at):
                ch, d = LETTER[name[-1]]
                bank = filled(act, (name,), at)
                hold(act)
                out = hT[:, d, BANK * ch:BANK * (ch + 1)]
                if name[1] == "2":
                    nc.scalar.copy(out, psM[:, bank]).then_inc(bank_free[bank], 1)
                else:
                    shift = modT[:, d, b:b + 1] if isinstance(b, int) else modT[:, d, bass.ds(val(b), 1)]
                    scale = modT[:, DC + d, b:b + 1] if isinstance(b, int) else modT[:, DC + d, bass.ds(val(b), 1)]
                    nc.scalar.activation(out, psM[:, bank], ACT.Identity, bias=shift,
                                         scale=scale).then_inc(bank_free[bank], 1)

            def evac_V(b, p, at):
                bank = filled(act, ("V", p), at)
                nc.scalar.copy(va[:, 2 * p:2 * p + 2, :, 0:DK],
                               psM[:, bank].rearrange("p (t h d) -> p t h d", t=2, h=NH)).then_inc(bank_free[bank], 1)
                emptied(act, ("V", p), at)
                act.sem_inc(v_ready, 1)

            def part(b, n, z):
                if z == 0:
                    act.wait_ge(rotated, val(b * 4 + (n + 1)))
                    if not (isinstance(b, int) and b == 0 and n < 2):
                        act.wait_ge(scr_ready[n % 2], val(b * 32 + 16 * (n // 2)))
                else:
                    act.wait_ge(rest_ready, val(b * 4 + (n + 1)))
                nc.scalar.copy(parts[:, n % 2, z], rt[:, n % 2, 0:2]).then_inc((part0_ready, part1_ready)[z], 1)

            def exponentials(b, g, n):
                j, s, a, e, heads = ATT_TILES[n]
                w = (e - a) * len(heads)
                act.wait_ge(t_ready, val(unit(b, g) * UT + (n + 1)))
                act.wait_ge(pv_done, val(unit(b, g) * UT + (n + 1)))
                nc.scalar.activation(prob[:, (g * UT + n) % NPROB, 0:w], psT[:, n % 2, 0:w], ACT.Exp,
                                     scale=DK ** -0.5).then_inc(exp_done, 1)

            def evac_O(b, g, hf):
                act.wait_ge(pv_done, val(unit(b, g) * UT + (HALF_END[hf] + 1 + NPROB)))
                nc.scalar.copy(attnT[:, g, BANK * hf:BANK * (hf + 1)], psO[:, hf]).then_inc(pv_copied, 1)

            act.wait_ge(silu_r, 3)
            for name in ("Ta", "Tb", "Tc", "Td"):
                evac_T(0, name, init)
            for n in range(4):
                part(0, n, 0)
                part(0, n, 1)
            act.wait_ge(consts, CONSTS)
            for p in range(NT // 2):
                evac_V(0, p, init)

            def do(name, b, g, at):
                pb = at[1] if at[0] == "turn" else b - 1
                if name[0] == "T":
                    evac_T(b + 1, name, at)
                elif name[:3] == "rot":
                    part(b + 1, int(name[3]), 0)
                elif name[:3] == "low":
                    part(b + 1, int(name[3]), 1)
                elif name == "C":
                    act.wait_ge(gap_ready, val(pb + 1))
                    nc.scalar.activation(gap[:, 1], gap[:, 0], ACT.Exp).then_inc(gap_exp, 1)

            def body(b, at):
                for g in range(NU):
                    todo = steps(at[0], g)
                    if at[0] in ("turn", "last") and g == 0:
                        pb = at[1] if at[0] == "turn" else b - 1
                    for n in range(UT):
                        exponentials(b, g, n)
                        for _, name in [t for t in todo if t[0] == n]:
                            do(name, b, g, at)
                        if n == HALF_END[0] + 6:
                            if g == 0 and at[0] != "first":
                                filled(act, ("O3",), at)
                            if g == NU - 1 and at[0] == "first":
                                act.wait_ge(zero_out, 16 * E * CAP // (4 * P))
                            evac_O(b, g, 0)
                    evac_O(b, g, 1)
                if at[0] != "last":
                    for p in range(NT // 2):
                        evac_V(b + 1, p, at)

            def tail(at):
                for name in POST_STEPS:
                    do(name, B, 0, at)

            program(act, body, tail)

        @block.vector
        def _(dve):
            v = nc.vector
            c = Counter(dve, dve_step, DVE_STEPS)
            init = ("init", None)
            step = c.step
            dve.sem_inc(s_maxed, 2)
            dve.wait_ge(silu_e, 1)
            step(init, v.tensor_scalar_add(sc[:, 1], sc[:, 0], 1.0))
            step(init, v.reciprocal(sc[:, 2], sc[:, 1]))
            step(init, v.tensor_tensor(sc[:, 0], sc[:, 2], cT[:], ALU.mult))
            for a in range(DC):
                v.tensor_copy(silc[:, a], wide(sc[:, 0, a].unsqueeze(2), 2, P)).then_inc(silu_r, 1)
            for s in range(2):
                v.memset(stk[MROW:STACK, s, 1].rearrange("p h n -> p (h n)").bitcast(F32),
                         MINUS_ONES).then_inc(minus_ones, 1)
            bank = filled(dve, ("MT",), init)
            v.tensor_copy(modT[:], psM[:, bank, 0:2 * DC * B].rearrange("p (z b) -> p z b", b=B),
                          ).then_inc(bank_free[bank], 1)
            emptied(dve, ("MT",), init)
            v.tensor_scalar_add(modT[:, DC:2 * DC], modT[:, DC:2 * DC], 1.0).then_inc(silu_r, 1)
            dve.wait_ge(silu_r, 3)

            def rows_of(b):
                return (lambda t, n=1: x[:, NT * b + t:NT * b + t + n, :]) if isinstance(b, int) else (
                    lambda t, n=1: x[:, bass.ds(val(b * NT + t), n), :])

            def layer_stats(b, at, which):
                hold(dve)
                for t in range(NT):
                    ins = v.bn_stats(stats[:, which, t], rows_of(b)(t)[:, 0])
                step(at, ins)
                hold(dve)
                for t in range(NT):
                    ins = v.bn_aggr(meanvar[:, which, t], stats[:, which, t])
                step(at, ins)
                v.tensor_scalar_add(vareps[:, which], meanvar[:, which, :, 1], EPS).then_inc(var_ready[which], 1)

            def normed(b, hf, which, out):
                for t in range(4):
                    n = 4 * hf + t
                    ins = v.tensor_scalar(out[:, t], rows_of(b)(n)[:, 0], meanvar[:, which, n, 0:1],
                                          rstd[:, which, n:n + 1], ALU.subtract, ALU.mult)
                ins.then_inc(xn_ready[which], 1)

            def rope_products(b, n, at):
                ch, _w = divmod(n, 2)
                if not (isinstance(b, int) and b == 0 and n < 2):
                    dve.wait_ge(part2_ready, val(b * 4 + (n - 1)))
                cs = slice(BANK * ch, BANK * (ch + 1))
                for eo in range(2):
                    bank = filled(dve, (f"QK{n}", eo), at)
                    v.tensor_tensor(rt[:, n % 2, eo], psM[:, bank], rope[:, 0, cs], ALU.mult)
                    v.tensor_tensor(rt[:, n % 2, 2 + eo], psM[:, bank], rope[:, 1, cs],
                                    ALU.mult).then_inc(bank_free[bank], 1)

            def rest(b, n):
                r = rt[:, n % 2, 0:2]
                dve.wait_ge(part0_ready, val(b * 4 + (n + 1)))
                v.tensor_tensor(r, r, parts[:, n % 2, 0], ALU.subtract).then_inc(rest_ready, 1)

            def maximum(b, g, n):
                i, s, a, e, heads = MAX_TILES[n]
                w, nh = e - a, len(heads)
                dve.wait_ge(s_ready, val(unit(b, g) * UT + (n + 1)))
                v.tensor_reduce(mx[:, s, heads[0]:heads[0] + nh, i],
                                psS[:, n % 2, 0:w * nh].rearrange("p (h w) -> p h w", h=nh), AX.X,
                                ALU.max).then_inc(s_maxed, 1)

            def max_parts(b, g, at):
                dve.wait_ge(s_maxed, val(unit(b, g) * UT + (UT + 2)))
                v.tensor_copy(mxr[:, :, 0:4], mx[:, 0, :, 0:4])
                step(at, v.tensor_tensor(mxr[:, :, 4:8], mx[:, 0, :, 4:8], mx[:, 1, :, 4:8], ALU.max))
                step(at, v.tensor_copy(mp[:, 0], mxr[:]))
                v.tensor_tensor(mp[:, 1], mxr[:], mp[:, 0], ALU.subtract).then_inc(mp_ready, 1)

            def max_evac(b, g, at):
                bank = filled(dve, ("M", g), at)
                if not (isinstance(b, int) and b == 0 and g == 0):
                    dve.wait_ge(mrow_ready[(g + 1) % 2], val((b * 2 + (g + 1) // 2 if g else b * 2) * 32))
                v.tensor_copy(mT[:], psM_bf16[bank][0:2 * HU, :]).then_inc(bank_free[bank], 1)

            def reciprocal(b, g):
                dve.wait_ge(sums_in, val(unit(b, g) * 16 + 16))
                v.reciprocal(sums[:], sums[:]).then_inc(recip_done, 1)

            def residual(pb, p, at):
                bank = filled(dve, (f"O{p}",), at)
                src = psM[:, bank].rearrange("p (t d) -> p t d", t=2)
                ga = batch(modrow, pb)[:, :, 0]
                v.tensor_tensor(yb[:], src, wide(ga, 1, 2), ALU.mult).then_inc(bank_free[bank], 1)
                emptied(dve, (f"O{p}",), at)
                xt = rows_of(pb)(2 * p, 2)
                step(at, v.tensor_tensor(xt, xt, yb[:], ALU.add))

            def route_labels(pb, at):
                bank = filled(dve, ("G",), at)
                v.tensor_tensor(lg[:], psM[:, bank, 0:NT * E].rearrange("p (t e) -> p t e", e=E),
                                wide(bg[:].unsqueeze(1), 1, NT), ALU.add).then_inc(bank_free[bank], 1)
                emptied(dve, ("G",), at)
                hold(dve)
                for t in range(NT):
                    ins = v.max(top[:, t], lg[:, t])
                step(at, ins)
                v.tensor_tensor(gap[:, 0], top[:, :, 1], top[:, :, 0], ALU.subtract).then_inc(gap_ready, 1)
                for t in range(NT):
                    ins = v.max_index(topi[:, t], top[:, t], lg[:, t])
                step(at, ins)
                step(at, v.tensor_copy(topf[:], topi[:]))
                for ch in range(TOPK):
                    ins = v.tensor_tensor(oh[:, ch], wide(eio[:].unsqueeze(1), 1, NT),
                                          wide(topf[:, :, ch:ch + 1], 2, E), ALU.is_equal)
                step(at, ins)
                v.tensor_tensor(label[:], oh[:, 0], oh[:, 1], ALU.add)
                step(at, v.tensor_tensor(rw[:, 0], oh[:, 0], oh[:, 1], ALU.add))
                step(at, v.tensor_reduce(lsum[:], rw[:, 0].rearrange("p t e -> p e t"), AX.X, ALU.add))
                v.tensor_copy(lsumb[:], lsum[:]).then_inc(label_ready, 1)

            def route_slots(pb, at):
                bank = filled(dve, ("C",), at)
                cum = psM[:, bank, 0:NT * E].rearrange("p (t e) -> p t e", e=E)
                step(at, v.tensor_tensor(rw[:, 0], cum, wide(seqb[:].unsqueeze(1), 1, NT), ALU.add))
                v.tensor_tensor(seqb[:], psM[:, bank, NT * E:NT * E + E], seqb[:],
                                ALU.add).then_inc(bank_free[bank], 1)
                v.tensor_scalar(rw[:, 1], rw[:, 0], float(CAP), None, ALU.is_le)
                step(at, v.tensor_tensor(rw[:, 2], rw[:, 0], wide(ebase[:].unsqueeze(1), 1, NT), ALU.add))
                step(at, v.tensor_tensor(rw[:, 0], rw[:, 1], rw[:, 2], ALU.mult))
                for ch in range(TOPK):
                    ins = v.tensor_tensor(rw[:, 2 + ch], rw[:, 0], oh[:, ch], ALU.mult)
                step(at, ins)
                for ch in range(TOPK):
                    ins = v.tensor_reduce(slotf[:, ch], rw[:, 2 + ch], AX.X, ALU.add)
                step(at, ins)
                dve.wait_ge(h2_free, val(pb + 1))
                v.tensor_scalar_add(slotb[:], slotf[:], float(TRASH)).then_inc(slot_ready, 1)
                dve.wait_ge(slot_ready, val(pb + 1))
                v.tensor_copy(batch(slot_of, pb)[:, 0], slotb[:])
                dve.wait_ge(gap_exp, val(pb + 1))
                step(at, v.tensor_scalar_add(gap[:, 2], gap[:, 1], 1.0))
                step(at, v.reciprocal(gap[:, 2], gap[:, 2]))
                wt = batch(weight_of, pb)[:, 0]
                v.tensor_copy(wt[:, 0], gap[:, 2])
                step(at, v.tensor_tensor(wt[:, 1], gap[:, 1], gap[:, 2], ALU.mult))

            def first_norm(b, hf, at):
                if hf:
                    filled(dve, ("Ta",), at)
                    filled(dve, ("Tb",), at)
                else:
                    dve.wait_ge(rstd_ready[0], val(b + 1))
                    hold(dve)
                normed(b, hf, 0, xn)

            dve.wait_ge(consts, CONSTS)
            dve.wait_ge(x0_in, 16)
            layer_stats(0, init, 0)
            for hf in range(2):
                first_norm(0, hf, init)
            dve.wait_ge(qk_in, 16 * 4)
            for n in range(4):
                rope_products(0, n, init)
                if n:
                    rest(0, n - 1)
            rest(0, 3)
            for f in range(2):
                for b in range(B):
                    bank = filled(dve, ("R", b, f), init)
                    src = psM[:, bank].rearrange("p (z d) -> p z d", z=2)
                    v.tensor_copy(modrow[:, b, 2 * f:2 * f + 2], src).then_inc(bank_free[bank], 1)
            dve.wait_ge(w_in, 16 * 7)
            for n in range(UT):
                maximum(0, 0, n)
            max_parts(0, 0, init)
            max_evac(0, 0, init)
            for bank in range(2):
                emptied(dve, ("R", B - 1 - bank, 1), init)
            step(init, v.tensor_scalar_add(modrow[:, :, 2], modrow[:, :, 2], 1.0))
            dve.wait_ge(part2_ready, 4)
            for z in (0, 3):
                g_ = modrow[:, :, z]
                sgn, mag = (rt[:, i, 0:2].rearrange("p a n -> p (a n)").rearrange("p (b d) -> p b d", b=B)
                            for i in range(2))
                step(init, v.tensor_scalar(sgn, g_, 0.0, 2.0, ALU.is_ge, ALU.mult))
                step(init, v.tensor_scalar_add(sgn, sgn, -1.0))
                step(init, v.tensor_tensor(mag, g_, sgn, ALU.mult))
                step(init, v.scalar_tensor_tensor(out=g_, in0=mag, scalar=0.25, in1=sgn, op0=ALU.max, op1=ALU.mult))
            c.close("init")

            def do(name, b, g, at):
                pb = at[1] if at[0] == "turn" else b - 1
                nb, ng = after_unit(b, g)
                if name == "recip" and (at[0] != "first" or g):
                    reciprocal(*((b, g - 1) if g else (pb, NU - 1)))
                elif name == "maxparts":
                    max_parts(nb, ng, at)
                elif name == "mT":
                    max_evac(nb, ng, at)
                elif name[0] == "O":
                    residual(pb, int(name[1]), at)
                elif name == "stats2":
                    layer_stats(pb, at, 1)
                elif name[:5] == "norm2":
                    if name == "norm2a":
                        dve.wait_ge(rstd_ready[1], val(pb + 1))
                        dve.wait_ge(h2_free, val(pb + 1))
                        hold(dve)
                    hf = int(name == "norm2b")
                    normed(pb, hf, 1, h2[:, 4 * hf:4 * hf + 4])
                elif name == "route1":
                    route_labels(pb, at)
                elif name == "route2":
                    route_slots(pb, at)
                elif name == "stats1":
                    if at[0] == "first":
                        dve.wait_ge(x_in, 16 * (B - 1))
                    layer_stats(b + 1, at, 0)
                elif name[:5] == "norm1":
                    first_norm(b + 1, int(name == "norm1b"), at)
                elif name[:2] == "QK":
                    rope_products(b + 1, int(name[2]), at)
                elif name[:3] == "sub":
                    rest(b + 1, int(name[3]))

            def body(b, at):
                for g in range(NU):
                    nb, ng = after_unit(b, g)
                    todo = steps(at[0], g)
                    for n in range(UT):
                        if not (at[0] == "last" and g == NU - 1):
                            for m in MAX_AT[n]:
                                maximum(nb, ng, m)
                        for _, name in [t for t in todo if t[0] == n]:
                            do(name, b, g, at)
                c.close(at[0])

            def tail(at):
                reciprocal(B - 1, NU - 1)
                for name in POST_STEPS:
                    do(name, B, 0, at)
                c.close(at[0])

            program(dve, body, tail)

        @block.tensor
        def _(pe):
            mm, tr = nc.tensor.matmul, nc.tensor.transpose
            init = ("init", None)
            pe.sem_inc(pv_done, NPROB)
            pe.wait_ge(silu_r, DC)
            pe.wait_ge(wm_in[0], 16)
            bank = claim(pe, ("MT",), init)
            for z in range(2 * DC):
                for a in range(DC):
                    ins = mm(psM[:, bank, B * z:B * (z + 1)], wm[0][:, a, P * z:P * (z + 1)], sc[:, 0, a],
                             start=a == 0, stop=a == DC - 1)
            ins.then_inc(bank_ready[bank], 1)

            def turn(name, at, src):
                _, d = LETTER[name[-1]]
                bank = claim(pe, (name,), at)
                for t in range(4):
                    ins = tr(psM[:, bank, P * t:P * (t + 1)], src[:, t, P * d:P * (d + 1)], identf[:])
                ins.then_inc(bank_ready[bank], 1)

            def turn_x(b, name, at):
                ch, _ = LETTER[name[-1]]
                pe.wait_ge(xn_ready[0], val(b * 2 + (ch + 1)))
                turn(name, at, xn)

            def project(b, n, at):
                ch, w = divmod(n, 2)
                for d in "ab" if ch == 0 else "cd":
                    emptied(pe, ("T" + d,), at)
                for eo in range(2):
                    bank = claim(pe, (f"QK{n}", eo), at)
                    for a in range(DC):
                        ins = mm(psM[:, bank], wq[:, w, a, P * eo:P * (eo + 1)], hT[:, a, BANK * ch:BANK * (ch + 1)],
                                 start=a == 0, stop=a == DC - 1)
                    ins.then_inc(bank_ready[bank], 1)

            def values(p, at):
                bank = claim(pe, ("V", p), at)
                for t in range(2):
                    for a in range(DC):
                        ins = mm(psM[:, bank, D * t:D * (t + 1)], hT[:, a, P * (2 * p + t):P * (2 * p + t + 1)],
                                 wv[:, a], start=a == 0, stop=a == DC - 1)
                ins.then_inc(bank_ready[bank], 1)

            def maxima_turn(b, g, at):
                pe.wait_ge(mp_ready, val(unit(b, g) + 1))
                bank = claim(pe, ("M", g), at)
                cols = mp[:].rearrange("p z h t -> p (z h) t")
                for i in range(NT):
                    ins = tr(psM_bf16[bank][0:2 * HU, P * i:P * (i + 1)], cols[:, :, i], ident[:])
                ins.then_inc(bank_ready[bank], 1)

            def first_pass(b, g, n):
                s = g % 2
                i, _, a, e, heads = MAX_TILES[n]
                for ch in range(CH):
                    if n == (0, MAX_HALF)[ch]:
                        pe.wait_ge(stk_ready[s][ch], val((b * 2 + (g // 2 + 1)) * (16 * STK_DMAS)))
                pe.wait_ge(s_maxed, val(apart(unit(b, g) * UT + (n + 1))))
                w = e - a
                diag = e == P * (i + 1)
                for m, h in enumerate(heads):
                    out = psS[:, n % 2, w * m:w * (m + 1)]
                    ins = mm(out, stk[0:MROW, s, 0, h, P * i:P * (i + 1)], stk[0:MROW, s, 1, h, a:e],
                             start=True, stop=not diag)
                    if diag:
                        ins = mm(out[:, w - P:w], ident[:], mask_k[:], start=False, stop=True)
                ins.then_inc(s_ready, 1)

            def second_pass(b, g, n):
                s = g % 2
                j, _, a, e, heads = ATT_TILES[n]
                pe.wait_ge(exp_done, val(unit(b, g) * UT + (n + 1)))
                w = e - a
                diag = a == P * j
                for m, h in enumerate(heads):
                    out = psT[:, n % 2, w * m:w * (m + 1)]
                    ins = mm(out, stk[:, s, 1, h, P * j:P * (j + 1)], stk[:, s, 0, h, a:e],
                             start=True, stop=not diag)
                    if diag:
                        ins = mm(out[:, 0:P], ident[:], mask_q[:], start=False, stop=True)
                ins.then_inc(t_ready, 1)

            def weigh(b, g, end):
                j, s, a, e, heads = ATT_TILES[end]
                w, first = e - a, end + 1 - HU // len(heads)
                hf = a // BANK
                pe.wait_ge(exp_done, val(unit(b, g) * UT + (end + 3)))
                if j == 0:
                    pe.wait_ge(pv_copied, val(unit(b, g) * 2 + (hf + 1)))
                for n in range(first, end + 1):
                    slot = (g * UT + n) % NPROB
                    for m, h in enumerate(ATT_TILES[n][4]):
                        ins = mm(psO[32 * h:32 * h + 32, hf, a - BANK * hf:e - BANK * hf], va[:, j, HU * g + h],
                                 prob[:, slot, w * m:w * (m + 1)], start=j == 0, stop=n >= HALF_END[hf] - HU + 1
                                 and end == HALF_END[hf], tile_position=(0, 32 * h), skip_group_check=True)
                    ins.then_inc(pv_done, 1)

            def out_project(p, at):
                bank = claim(pe, (f"O{p}",), at)
                for t in range(2):
                    ts = slice(P * (2 * p + t), P * (2 * p + t + 1))
                    for g in range(NU):
                        ins = mm(psM[:, bank, D * t:D * (t + 1)], attnT[:, g, ts], wo[:, g],
                                 start=g == 0, stop=g == NU - 1)
                ins.then_inc(bank_ready[bank], 1)

            def gate(at):
                for name in ("T2a", "T2b", "T2c", "T2d"):
                    emptied(pe, (name,), at)
                bank = claim(pe, ("G",), at)
                for t in range(NT):
                    for a in range(DC):
                        ins = mm(psM[:, bank, E * t:E * (t + 1)], hT[:, a, P * t:P * (t + 1)], wg[:, a],
                                 start=a == 0, stop=a == DC - 1)
                ins.then_inc(bank_ready[bank], 1)

            def count_labels(pb, at):
                pe.wait_ge(label_ready, val(pb + 1))
                bank = claim(pe, ("C",), at)
                mm(psM[:, bank, 0:NT * E], tri[:], label[:].rearrange("p t e -> p (t e)"), start=True, stop=False)
                for t in range(NT - 1):
                    mm(psM[:, bank, E * (t + 1):NT * E], ones[:],
                       wide(label[:, t:t + 1], 1, NT - 1 - t), start=False, stop=t == NT - 2)
                mm(psM[:, bank, NT * E:NT * E + E], ones[:], lsumb[:], start=True,
                   stop=True).then_inc(bank_ready[bank], 1)

            pe.wait_ge(consts, CONSTS)
            for name in ("Ta", "Tb", "Tc", "Td"):
                turn_x(0, name, init)
            pe.wait_ge(qk_in, 16 * 4)
            for n in range(4):
                project(0, n, init)
            for f in range(2):
                pe.wait_ge(wm_in[f + 1], 16)
                for b in range(B):
                    bank = claim(pe, ("R", b, f), init)
                    for a in range(DC):
                        ins = mm(psM[:, bank], silc[:, a, b], wm[1 - f][:, a], start=a == 0, stop=a == DC - 1)
                    ins.then_inc(bank_ready[bank], 1)
            pe.wait_ge(w_in, 16 * 7)
            for n in range(UT):
                first_pass(0, 0, n)
            maxima_turn(0, 0, init)
            for p in range(NT // 2):
                values(p, init)
            pe.wait_ge(minus_ones, 2)

            def do(name, b, g, at):
                pb = at[1] if at[0] == "turn" else b - 1
                if name == "M":
                    maxima_turn(*after_unit(b, g), at)
                elif name[0] == "O":
                    if name == "O0":
                        pe.wait_ge(attn_ready, val(pb * NU + (NU + 1)))
                    out_project(int(name[1]), at)
                elif name[:2] == "T2":
                    ch, _ = LETTER[name[-1]]
                    pe.wait_ge(h2m_ready, val(pb * 2 + (ch + 1)))
                    turn(name, at, h2[:, 4 * ch:4 * ch + 4])
                elif name == "G":
                    gate(at)
                elif name == "C":
                    count_labels(pb, at)
                elif name[0] == "T":
                    turn_x(b + 1, name, at)
                elif name[:2] == "QK":
                    project(b + 1, int(name[2]), at)

            def body(b, at):
                for g in range(NU):
                    nb, ng = after_unit(b, g)
                    held = None
                    todo = steps(at[0], g)
                    pe.wait_ge(mrow_ready[g % 2], val((b * 2 + (g // 2 + 1)) * 32))
                    if g == 0:
                        pe.wait_ge(v_ready, val(b * (NT // 2) + NT // 2))
                    for n in range(UT):
                        second_pass(b, g, n)
                        if n in QUAD_END:
                            if held is not None:
                                weigh(b, g, held)
                            held = n
                        if not (at[0] == "last" and g == NU - 1):
                            for m in MAX_AT[n]:
                                first_pass(nb, ng, m)
                        for _, name in [t for t in todo if t[0] == n]:
                            do(name, b, g, at)
                    weigh(b, g, held)
                if at[0] != "last":
                    for p in range(NT // 2):
                        values(p, at)

            def tail(at):
                for name in POST_STEPS:
                    do(name, B, 0, at)

            program(pe, body, tail)


def expert_block(nc, io, disp, outs):
    NTE = CAP // P
    HC = H // P
    HS = CAP // 2
    STEPS = 2 * HC
    with ExitStack() as ctx:
        def sb(name, shape, dt=F32):
            return ctx.enter_context(nc.sbuf_tensor(name, shape, dt))

        def sem(name):
            return ctx.enter_context(nc.semaphore(name))

        w12 = sb("w12", [P, 2, 2, DC, H])
        w3 = sb("w3", [P, 2, HC, D])
        dx = sb("dx", [P, 2, NTE, D])
        dT = sb("dT", [P, DC, CAP])
        hT = sb("hT", [P, HC, CAP])
        sg = sb("sg", [P, 2, HS])
        eo = sb("eo", [P, 2, NTE, D])
        fid = sb("fid", [P, P])
        zrow = sb("zrow", [1, D])
        psH = ctx.enter_context(nc.psum_tensor("psH", [P, 2, 2, BANK], F32))
        psY = ctx.enter_context(nc.psum_tensor("psY", [P, 2, BANK], F32))
        fid_ready = sem("fid_ready")
        zr_ready = sem("zr_ready")
        w_ready = [sem(f"w_ready{i}") for i in range(2)]
        y_ready = [sem(f"y_ready{i}") for i in range(2)]
        y_free = [sem(f"y_free{i}") for i in range(2)]
        pair_ready = sem("pair_ready")
        silu_done = sem("silu_done")
        h_done = sem("h_done")
        expert_done = sem("expert_done")
        eo_ready = sem("eo_ready")
        stored = sem("stored")
        eo_free = sem("eo_free")
        zrow_stored = sem("zrow_stored")
        TURNS = [(d, g) for d in range(DC) for g in range(2)]
        OUTS = [(0, 1), (2, 3), (4,)]
        USES = len(TURNS) + len(OUTS)
        block = ctx.enter_context(nc.Block())

        def y_use(i, e2, k):
            k += USES * e2
            return k % 2, i * USES + (k // 2 + 1)

        def turn_cols(d, g):
            return (0, 4 * P) if g == 0 else (4 * P, CAP)

        @block.sync
        def _(sp):
            sp.wait_ge(zr_ready, 1)
            sp.dma_start(outs[TRASH:TRASH + 1, :], zrow[:]).then_inc(zrow_stored, 16)
            sp.wait_ge(zrow_stored, 16)
            with sp.Fori(0, E // 2) as i:
                for e2 in range(2):
                    sp.wait_ge(expert_done, i * 2 + (e2 + 1))
                    ex = bass.ds(i * 2 + e2, 1)
                    for w, src in enumerate((io["w1"], io["w2"])):
                        sp.dma_start(w12[:, e2, w], src[ex].rearrange("e (a p) n -> p (e a) n", p=P)).then_inc(w_ready[e2], 16)
                    sp.dma_start(w3[:, e2], io["w3"][ex].rearrange("e (a p) n -> p (e a) n", p=P)).then_inc(w_ready[e2], 16)
                    sp.dma_start(dx[:, e2], disp.rearrange("(e t p) n -> e p t n", e=E, p=P)[ex]
                                 .rearrange("e p t n -> p (e t) n")).then_inc(w_ready[e2], 16)

        @block.gpsimd
        def _(pool):
            pool.sem_inc(eo_free, 2)
            nc.gpsimd.memset(fid[:], 0.0).then_inc(fid_ready, 1)
            nc.gpsimd.memset(zrow[:], 0.0).then_inc(zr_ready, 1)
            pool.wait_ge(fid_ready, 1)
            nc.gpsimd.affine_select(out=fid[:], in_=fid[:], compare_op=ALU.not_equal, fill=1.0, base=0,
                                    pattern=[[-1, P]], channel_multiplier=1).then_inc(fid_ready, 1)
            with pool.Fori(0, E // 2) as i:
                for e2 in range(2):
                    pool.wait_ge(eo_ready, i * (2 * len(OUTS)) + (len(OUTS) * (e2 + 1)))
                    pool.dma_start(outs[0:TRASH].rearrange("(e t p) n -> e p t n", e=E, p=P)[bass.ds(i * 2 + e2, 1)]
                                   .rearrange("e p t n -> p (e t) n"), eo[:, e2]).then_inc(stored, 16)
                    pool.wait_ge(stored, i * 32 + 16 * (e2 + 1))
                    pool.sem_inc(eo_free, 1)

        @block.tensor
        def _(pe):
            mm, tr = nc.tensor.matmul, nc.tensor.transpose
            pe.sem_inc(expert_done, 2)
            pe.wait_ge(fid_ready, 2)
            with pe.Fori(0, E // 2) as i:
                for e2 in range(2):
                    pe.wait_ge(w_ready[e2], i * 64 + 64)
                    for k, (d, g) in enumerate(TURNS):
                        bank, n = y_use(i, e2, k)
                        pe.wait_ge(y_free[bank], n)
                        a, e = turn_cols(d, g)
                        for t in range(a // P, e // P):
                            ins = tr(psY[:, bank, P * t - a:P * (t + 1) - a], dx[:, e2, t, P * d:P * (d + 1)], fid[:])
                        ins.then_inc(y_ready[bank], 1)
                    for k in range(2):
                        bank, n = y_use(i, e2, len(TURNS) - 1 - k)
                        pe.wait_ge(y_free[bank], n + 1)
                    for r in range(STEPS):
                        hc, s = divmod(r, 2)
                        pe.wait_ge(h_done, i * (2 * STEPS) + (STEPS * e2 + r + 1))
                        for w in range(2):
                            for a in range(DC):
                                ins = mm(psH[:, r % 2, w, 0:HS], w12[:, e2, w, a, P * hc:P * (hc + 1)],
                                         dT[:, a, HS * s:HS * (s + 1)], start=a == 0, stop=a == DC - 1)
                        ins.then_inc(pair_ready, 1)
                    pe.wait_ge(h_done, i * (2 * STEPS) + (STEPS * (e2 + 1) + 2))
                    for k, tiles in enumerate(OUTS):
                        bank, n = y_use(i, e2, len(TURNS) + k)
                        pe.wait_ge(y_free[bank], n)
                        for m, t in enumerate(tiles):
                            for hc in range(HC):
                                ins = mm(psY[:, bank, D * m:D * (m + 1)], hT[:, hc, P * t:P * (t + 1)], w3[:, e2, hc],
                                         start=hc == 0, stop=hc == HC - 1)
                        ins.then_inc(y_ready[bank], 1)
                    pe.wait_ge(y_ready[bank], n)
                    pe.sem_inc(expert_done, 1)

        @block.scalar
        def _(act):
            with act.Fori(0, E // 2) as i:
                for e2 in range(2):
                    for r in range(STEPS):
                        act.wait_ge(pair_ready, i * (2 * STEPS) + (STEPS * e2 + r + 1))
                        nc.scalar.activation(sg[:, r % 2], psH[:, r % 2, 0, 0:HS], ACT.Silu).then_inc(silu_done, 1)
                    act.wait_ge(eo_free, i * 2 + (e2 + 1))
                    for k, tiles in enumerate(OUTS):
                        bank, n = y_use(i, e2, len(TURNS) + k)
                        act.wait_ge(y_ready[bank], n)
                        nc.scalar.copy(eo[:, e2, tiles[0]:tiles[-1] + 1].rearrange("p t d -> p (t d)"),
                                       psY[:, bank, 0:D * len(tiles)]).then_inc(y_free[bank], 1)
                        act.wait_ge(y_free[bank], n + 1)
                        act.sem_inc(eo_ready, 1)

        @block.vector
        def _(dve):
            dve.sem_inc(h_done, 2)
            for bank in range(2):
                dve.sem_inc(y_free[bank], 1)
            with dve.Fori(0, E // 2) as i:
                for e2 in range(2):
                    for k, (d, g) in enumerate(TURNS):
                        bank, n = y_use(i, e2, k)
                        dve.wait_ge(y_ready[bank], n)
                        a, e = turn_cols(d, g)
                        nc.vector.tensor_copy(dT[:, d, a:e], psY[:, bank, 0:e - a]).then_inc(y_free[bank], 1)
                    for r in range(STEPS):
                        hc, s = divmod(r, 2)
                        dve.wait_ge(silu_done, i * (2 * STEPS) + (STEPS * e2 + r + 1))
                        nc.vector.tensor_tensor(hT[:, hc, HS * s:HS * (s + 1)], psH[:, r % 2, 1, 0:HS], sg[:, r % 2],
                                                ALU.mult).then_inc(h_done, 1)


def combine_block(nc, io, outs, keep):
    x, modrow, slot_of, weight_of = keep["x"], keep["modrow"], keep["slot"], keep["weight"]
    G = 4
    with ExitStack() as ctx:
        def sb(name, shape, dt=F32):
            return ctx.enter_context(nc.sbuf_tensor(name, shape, dt))

        def sem(name):
            return ctx.enter_context(nc.semaphore(name))

        slots = sb("slots", [P, 2, TOPK, NT], U32)
        rows = sb("rows", [P, 4, TOPK, G, D])
        y = sb("y", [P, 2, G, D])
        slots_ready = sem("slots_ready")
        gathered = [sem(f"gathered{i}") for i in range(4)]
        rows_used = sem("rows_used")
        y_step = sem("y_step")
        x_ready = sem("x_ready")
        stored = sem("out_stored")
        block = ctx.enter_context(nc.Block())

        @block.gpsimd
        def _(pool):
            for b in range(B):
                pool.wait_ge(slots_ready, b + 1)
                for h in range(2):
                    step = 2 * b + h
                    if step >= 4:
                        pool.wait_ge(rows_used, step - 3)
                    for t in range(G):
                        for c in range(TOPK):
                            nc.gpsimd.indirect_dma_start(
                                rows[:, step % 4, c, t], None, outs[:, :],
                                bass.IndirectOffsetOnAxis(ap=slots[:, b % 2, c, G * h + t:G * h + t + 1], axis=0),
                            ).then_inc(gathered[step % 4], 16)

        @block.vector
        def _(dve):
            v = nc.vector
            for b in range(2):
                v.tensor_copy(slots[:, b], slot_of[:, b]).then_inc(slots_ready, 1)
            for b in range(B):
                for h in range(2):
                    step = 2 * b + h
                    s = step % 4
                    dve.wait_ge(gathered[s], 16 * G * TOPK * (step // 4 + 1))
                    for t in range(G):
                        n = G * h + t
                        v.tensor_scalar(y[:, step % 2, t], rows[:, s, 0, t], weight_of[:, b, 0, n:n + 1], None,
                                        ALU.mult).then_inc(y_step, 1)
                    dve.wait_ge(y_step, step * 10 + 4)
                    for t in range(G):
                        n = G * h + t
                        v.scalar_tensor_tensor(out=y[:, step % 2, t], in0=rows[:, s, 1, t],
                                               scalar=weight_of[:, b, 1, n:n + 1], in1=y[:, step % 2, t],
                                               op0=ALU.mult, op1=ALU.add).then_inc(y_step, 1)
                    dve.wait_ge(y_step, step * 10 + 8)
                    v.tensor_tensor(y[:, step % 2], y[:, step % 2], wide(modrow[:, b:b + 1, 3], 1, G),
                                    ALU.mult).then_inc(y_step, 1)
                    dve.wait_ge(y_step, step * 10 + 9)
                    xs = x[:, NT * b + G * h:NT * b + G * (h + 1), :]
                    v.tensor_tensor(xs, xs, y[:, step % 2], ALU.add).then_inc(x_ready, 1)
                    v.tensor_copy(slots[:, b % 2, 0, 0:1], slots[:, b % 2, 0, 0:1]) if False else None
                    dve.wait_ge(x_ready, step + 1)
                    dve.sem_inc(rows_used, 1)
                    dve.sem_inc(y_step, 1)
                if b + 2 < B:
                    v.tensor_copy(slots[:, b % 2], slot_of[:, b + 2]).then_inc(slots_ready, 1)

        @block.sync
        def _(sp):
            for step in range(2 * B):
                sp.wait_ge(x_ready, step + 1)
                sp.dma_start(io["out"][G * P * step:G * P * (step + 1), :].rearrange("(t p) d -> p t d", p=P),
                             x[:, G * step:G * (step + 1), :]).then_inc(stored, 16)
            sp.wait_ge(stored, 16 * 2 * B)


def build(nc, io):
    disp = nc.dram_tensor("disp", (TRASH, D), F32, kind="Internal").ap()
    io["scr"] = nc.dram_tensor("scr", (B, 2, P, 6, S), BF16, kind="Internal").ap()
    io["sums"] = nc.dram_tensor("sums_d", (HU, S), F32, kind="Internal").ap()
    io["rsums"] = nc.dram_tensor("rsums_d", (HU, S), F32, kind="Internal").ap()
    outs = nc.dram_tensor("outs", (TRASH + 1, D), F32, kind="Internal").ap()
    with (
        nc.sbuf_tensor("x_rows", [P, B * NT, D], F32) as x,
        nc.sbuf_tensor("mod_rows", [P, B, 4, D], F32) as modrow,
        nc.sbuf_tensor("slot_of", [P, B, TOPK, NT], U32) as slot_of,
        nc.sbuf_tensor("weight_of", [P, B, TOPK, NT], F32) as weight_of,
    ):
        keep = {"x": x, "modrow": modrow, "slot": slot_of, "weight": weight_of}
        attention_block(nc, io, disp, keep)
        expert_block(nc, io, disp, outs)
        combine_block(nc, io, outs, keep)


def kernel(**inputs):
    import concourse.bacc as bacc
    from concourse.bass_utils import run_bass_kernel_spmd

    g = {k.removeprefix("L0_"): np.asarray(a) for k, a in inputs.items()}
    heads = np.arange(NH).reshape(NU, 1, HU) * DK
    pairs = np.arange(0, DK, 2).reshape(1, -1, 1)
    order = np.concatenate([(heads + pairs).ravel(), (heads + pairs + 1).ravel()])
    freq = (1.0 / np.float32(10000.0) ** (np.arange(0, DK, 2, dtype=np.float32) / DK)).astype(np.float32)
    angle = np.arange(S, dtype=np.float32)[None, :] * freq[:, None]
    arrays = {
        "x": g["attn_x"].reshape(T, D),
        "wq": g["attn_Wq"][order].T,
        "wk": g["attn_Wk"][order].T,
        "wv": g["attn_Wv"].T,
        "wo": g["attn_Wo"].T,
        "wg": g["ffn_Wg"],
        "bg": g["ffn_bg"],
        "w1": g["ffn_W1"],
        "w2": g["ffn_W2"],
        "w3": g["ffn_W3"],
        "cT": g["c"].T,
        "wmod": g["wmod"].reshape(D, 3, 2 * D).transpose(1, 0, 2),
        "cos": np.tile(np.repeat(np.cos(angle), HU, 0), (NU, 1)),
        "sin": np.tile(np.repeat(np.sin(angle), HU, 0), (NU, 1)),
    }
    arrays = {f"in_{k}": np.ascontiguousarray(a) for k, a in arrays.items()}
    nc = bacc.Bacc("TRN2", target_bir_lowering=False, num_devices=1)
    io = {k[3:]: nc.dram_tensor(k, a.shape, mybir.dt.from_np(a.dtype), kind="ExternalInput").ap()
          for k, a in arrays.items()}
    io["out"] = nc.dram_tensor("out", (T, D), F32, kind="ExternalOutput").ap()
    build(nc, io)
    r = run_bass_kernel_spmd(nc, [arrays], core_ids=[0])
    return r.results[0]["out"].reshape(B, S, D)
```

```python
from contextlib import ExitStack

import concourse.bass as bass
import numpy as np
from concourse import mybir

F32 = mybir.dt.float32
F32R = mybir.dt.float32r
BF16 = mybir.dt.bfloat16
U32 = mybir.dt.uint32
ALU = mybir.AluOpType
ACT = mybir.ActivationFunctionType
AX = mybir.AxisListType

P = 128
B, S, D = 4, 1024, 256
NH, DK = 16, 16
E, H, TOPK = 8, 1024, 2
T = B * S
CAP = int(T / E * 1.25)
TRASH = E * CAP
EPS = 1e-5
BIG = 1.0e30
DC = D // P
NT = S // P
HU = 4
NU = NH // HU
BANK = 512
CH = S // BANK
SLOTS = ((0, 48), (48, 32), (80, 16))
MROW = 96
STACK = MROW + 2
STK_DMAS = 3 + 6


def spans(lo, hi):
    return [(a, b) for a, b in ((lo, min(hi, BANK)), (max(lo, BANK), hi)) if a < b]


def bank_tiles(lo, hi):
    out = []
    for s, (a, b) in enumerate(spans(lo, hi)):
        n = min(HU, BANK // (b - a))
        out += [(s, a, b, list(range(h, h + n))) for h in range(0, HU, n)]
    return out


def wide(ap, axis, n):
    shape = list(ap.shape)
    shape[axis] = n
    return ap.broadcast_to(tuple(shape))


MAX_TILES = [(i, *t) for i in range(NT) for t in bank_tiles(0, P * (i + 1))]
ATT_TILES = [(j, *t) for j in range(NT) for t in bank_tiles(P * j, S)]
QUAD_END = [n for n, t in enumerate(ATT_TILES) if t[4][-1] == HU - 1]
HALF_END = [max(n for n, t in enumerate(ATT_TILES) if t[2] // BANK == h) for h in range(2)]
UT = len(ATT_TILES)
MAX_HALF = [t[0] for t in MAX_TILES].index(NT // 2)
PAST_HALF = [t[0] for t in ATT_TILES].index(NT // 2)
NPROB = 8
assert len(MAX_TILES) == UT and UT % 2 == 0 and (NU * UT) % NPROB == 0

MAX_FROM, MAX_TO = 0, 28
MAX_AT = [range(0)] * UT
for _n in range(MAX_FROM, MAX_TO):
    MAX_AT[_n] = range(UT * (_n - MAX_FROM) // (MAX_TO - MAX_FROM), UT * (_n + 1 - MAX_FROM) // (MAX_TO - MAX_FROM))

EVERY = [(9, "recip"), (28, "maxparts"), (31, "M"), (33, "mT")]
POST = {0: [(17, "O0"), (19, "O1"), (21, "O2"), (23, "O3"), (24, "stats2"), (27, "norm2a"), (30, "norm2b"),
            (35, "T2a"), (36, "T2b")],
        1: [(2, "T2c"), (3, "T2d"), (6, "G"), (7, "route1"), (11, "C"), (12, "route2")]}
PRE = {1: [(14, "stats1"), (16, "norm1a"), (19, "Ta"), (20, "Tb"), (21, "norm1b"), (25, "Tc"), (26, "Td"),
           (29, "QK0"), (32, "rot0"), (34, "sub0"), (36, "low0")],
       2: [(0, "QK1"), (3, "rot1"), (5, "sub1"), (7, "low1"),
           (11, "QK2"), (14, "rot2"), (16, "sub2"), (18, "low2"),
           (22, "QK3"), (25, "rot3"), (27, "sub3"), (29, "low3")]}


def steps(kind, g):
    out = list(EVERY)
    if kind == "last" and g == NU - 1:
        out = [x for x in out if x[1] == "recip"]
    if kind in ("turn", "last"):
        out += POST.get(g, [])
    if kind in ("first", "turn"):
        out += PRE.get(g, [])
    return sorted(out, key=lambda x: x[0])


POST_STEPS = [n for g in range(2) for _, n in POST[g]]
PRE_STEPS = ["stats1", "norm1a", "Ta", "Tb", "norm1b", "Tc", "Td"] + [
    f"{s}{n}" for n in range(4) for s in ("QK", "rot", "sub", "low")]
LETTER = {"a": (0, 0), "b": (0, 1), "c": (1, 0), "d": (1, 1)}


def uses(name, g=0):
    if name == "M":
        return [("M", (g + 1) % NU)]
    if name[:2] == "QK":
        return [(name, 0), (name, 1)]
    return [(name,)] if name[0] in "OGCT" else []


V_USES = [("V", p) for p in range(NT // 2)]
SEQ = {"init": [("MT",)] + [u for n in PRE_STEPS for u in uses(n)]
       + [("R", b, f) for f in range(2) for b in range(B)] + [("M", 0)] + V_USES}
for _kind in ("first", "turn", "last"):
    SEQ[_kind] = [u for g in range(NU) for _, n in steps(_kind, g) for u in uses(n, g)]
    if _kind != "last":
        SEQ[_kind] += V_USES
SEQ["tail"] = [u for n in POST_STEPS for u in uses(n)]
TURNS = B - 2
START = {"init": 0, "first": len(SEQ["init"])}
START["turn"] = START["first"] + len(SEQ["first"])
START["last"] = START["turn"] + TURNS * len(SEQ["turn"])
START["tail"] = START["last"] + len(SEQ["last"])
assert len(SEQ["turn"]) % 2 == 0
RING = 4
assert NPROB * BANK == RING * H
CONSTS = 11
MINUS_ONES = float(np.array([0xBF80BF80], np.uint32).view(np.float32)[0])


def weight_piece(io, ex, kind, c):
    if kind == "w12":
        w, a = divmod(c, DC)
        return (io["w1"], io["w2"])[w][ex].rearrange("e (a p) n -> a p (e n)", p=P)[a]
    n = H // D
    return io["w3"][ex].rearrange("e (a p) n -> p (e a) n", p=P)[:, n * c:n * (c + 1)]


class Turn:

    def __init__(self, reg, mul=1, add=0):
        self.reg, self.mul, self.add = reg, mul, add

    def __add__(self, n):
        return Turn(self.reg, self.mul, self.add + n)

    def __sub__(self, n):
        return self + -n

    def __mul__(self, n):
        return Turn(self.reg, self.mul * n, self.add * n)


def apart(n):
    return Turn(n.reg + 1, n.mul, n.add - n.mul) if isinstance(n, Turn) else n


def val(n):
    if not isinstance(n, Turn):
        return n
    v = n.reg * n.mul if n.mul > 1 else n.reg
    return v + n.add if n.add else v


class Counter:

    def __init__(self, eng, sem, per):
        self.eng, self.sem, self.per, self.n = eng, sem, per, 0
        self.base = {"init": 0, "first": per["init"]}
        self.base["turn"] = self.base["first"] + per["first"]
        self.base["last"] = self.base["turn"] + TURNS * per["turn"]
        self.base["tail"] = self.base["last"] + per["last"]

    def step(self, at, ins):
        kind, pb = at
        self.n += 1
        ins.then_inc(self.sem, 1)
        if kind == "turn":
            self.eng.wait_ge(self.sem, val(pb * self.per["turn"] + (self.base[kind] + self.n)))
        else:
            self.eng.wait_ge(self.sem, val(self.base[kind] + self.n))

    def close(self, kind):
        assert self.n == self.per[kind], (kind, self.n)
        self.n = 0


POOL_STEPS = {"init": 1, "first": 0, "turn": 2, "last": 2, "tail": 2}
DVE_STEPS = {"init": 16, "first": 10, "turn": 35, "last": 31, "tail": 25}


def attention_block(nc, io, disp, keep):
    x, gb_row, slot_of, weight_of = keep["x"], keep["gb"], keep["slot"], keep["weight"]
    ctx = ExitStack()
    with ctx:
        def sb(name, shape, dt=F32):
            return ctx.enter_context(nc.sbuf_tensor(name, shape, dt))

        def sem(name):
            return ctx.enter_context(nc.semaphore(name))

        modrow = sb("mod_rows", [P, B, 3, D])
        wq = sb("wq", [P, 2, DC, D])
        wv = sb("wv", [P, DC, D])
        wo = sb("wo", [P, NU, D])
        wg = sb("wg", [P, DC, E])
        bg = sb("bg", [P, E])
        rope = sb("rope", [P, 2, S])
        cT = sb("cT", [P, DC, B])
        sc = sb("sc", [P, 3, DC, B])
        modT = sb("modT", [P, 2 * DC, B])
        identf = sb("identf", [P, P])
        ident = sb("ident", [P, P], BF16)
        mask_k = sb("mask_k", [P, P], BF16)
        mask_q = sb("mask_q", [P, P], BF16)
        tri = sb("tri", [P, P], BF16)
        ones = sb("ones", [P, P], BF16)
        half = sb("half", [P, NT])
        eio = sb("eio", [P, E])
        ebase = sb("ebase", [P, E])
        stats = sb("stats", [P, 2, NT, 6])
        meanvar = sb("meanvar", [P, 2, NT, 2])
        vareps = sb("vareps", [P, 2, NT])
        rstd = sb("rstd", [P, 2, NT])
        xn = sb("xn", [P, 4, D])
        hT = sb("hT1", [P, DC, S])
        rt = sb("rt", [P, 2, 4, BANK])
        parts = sb("parts", [P, 2, 3, 2, BANK], BF16)
        va = sb("va", [P, NT, NH, 32])
        stk = sb("stk", [STACK, 2, 2, HU, S], BF16)
        mx = sb("mx", [P, 2, HU, NT])
        mxr = sb("mxr", [P, HU, NT])
        mp = sb("mp", [P, 2, HU, NT], BF16)
        mT = sb("mT", [2 * HU, S], BF16)
        prob = keep["ring"].rearrange("p a (c n) -> p (a c) n", n=BANK)
        attnT = sb("attnT", [P, NU, S])
        sums = sb("sums", [P, HU * S // P])
        rsum = sb("rsum", [P, S])
        h2 = sb("h2", [P, NT, D])
        yb = xn[:, 0:2]
        lg = sb("lg", [P, NT, E])
        top = sb("top", [P, NT, 8])
        topi = sb("topi", [P, NT, 8], U32)
        topf = sb("topf", [P, NT, 8])
        oh = sb("oh", [P, 2, NT, E])
        label = sb("label", [P, NT, E], BF16)
        lsum = sb("lsum", [P, E])
        lsumb = sb("lsumb", [P, E], BF16)
        seqb = sb("seqb", [P, E])
        rw = sb("rw", [P, 4, NT, E])
        slotf = sb("slotf", [P, 2, NT])
        slotb = sb("slotb", [P, 2, NT], U32)
        gap = sb("gap", [P, 3, NT])
        gx = sb("gx", [P, 10, NT])
        silc = prob[:, 0:2, :].rearrange("p a (b m) -> p a b m", b=B)
        wm = [h2[:, 4 * i:4 * i + 4].rearrange("p (a t) d -> p a (t d)", a=DC) for i in range(2)]

        psS = ctx.enter_context(nc.psum_tensor("psS", [P, 2, BANK], F32))
        psT = ctx.enter_context(nc.psum_tensor("psT", [P, 2, BANK], F32))
        psO = ctx.enter_context(nc.psum_tensor("psO", [P, 2, BANK], F32))
        psM = ctx.enter_context(nc.psum_tensor("psM", [P, 2, BANK], F32))
        psM_bf16 = [psM[:, i, :].bitcast(BF16) for i in range(2)]

        c_in = sem("c_in")
        wm_in = [sem(f"wm_in{i}") for i in range(3)]
        qk_in = sem("qk_in")
        w_in = sem("w_in")
        x0_in = sem("x0_in")
        x_in = sem("x_in")
        consts = sem("consts")
        wo_zero = sem("wo_zero")
        minus_ones = sem("minus_ones")
        silu_e = sem("silu_e")
        silu_r = sem("silu_r")
        zeroed = sem("zeroed")
        zero_out = sem("zero_out")
        bank_ready = [sem(f"bank_ready{i}") for i in range(2)]
        bank_free = [sem(f"bank_free{i}") for i in range(2)]
        var_ready = [sem(f"var_ready{i}") for i in range(2)]
        rstd_ready = [sem(f"rstd_ready{i}") for i in range(2)]
        xn_ready = [sem(f"xn_ready{i}") for i in range(2)]
        h2m_ready = sem("h2m_ready")
        rotated = sem("rotated")
        part0_ready = sem("part0_ready")
        rest_ready = sem("rest_ready")
        part1_ready = sem("part1_ready")
        part2_ready = sem("part2_ready")
        scr_ready = [sem(f"scr_ready{i}") for i in range(2)]
        stk_ready = [[sem(f"stk_ready{i}{ch}") for ch in range(CH)] for i in range(2)]
        mrow_ready = [sem(f"mrow_ready{i}") for i in range(2)]
        v_ready = sem("v_ready")
        s_ready = sem("s_ready")
        s_maxed = sem("s_maxed")
        mp_ready = sem("mp_ready")
        t_ready = sem("t_ready")
        exp_done = sem("exp_done")
        pv_done = sem("pv_done")
        pv_copied = sem("pv_copied")
        sums_out = sem("sums_out")
        sums_in = sem("sums_in")
        recip_done = sem("recip_done")
        recip_out = sem("recip_out")
        rsum_in = sem("rsum_in")
        attn_ready = sem("attn_ready")
        gap_ready = sem("gap_ready")
        gap_exp = sem("gap_exp")
        label_ready = sem("label_ready")
        slot_ready = sem("slot_ready")
        scattered = sem("scattered")
        h2_free = sem("h2_free")
        held_back = sem("held_back")
        dve_step = sem("dve_step")
        pool_step = sem("pool_step")

        def use(name, at):
            kind, pb = at
            k = START[kind] + SEQ[kind].index(name)
            n = k // 2 + 1
            return k % 2, (pb * (len(SEQ["turn"]) // 2) + n if kind == "turn" else n)

        def claim(pe, name, at):
            bank, n = use(name, at)
            if at[0] != "init" or n > 1:
                pe.wait_ge(bank_free[bank], val(n - 1))
            return bank

        def filled(eng, name, at):
            bank, n = use(name, at)
            eng.wait_ge(bank_ready[bank], val(n))
            return bank

        def emptied(eng, name, at):
            bank, n = use(name, at)
            eng.wait_ge(bank_free[bank], val(n))

        def unit(b, g):
            return b * NU + g

        def hold(eng):
            eng.sem_inc(held_back, 1)

        def after_unit(b, g):
            return (b, g + 1) if g < NU - 1 else (b + 1, 0)

        def program(eng, body, tail):
            body(0, ("first", None))
            with eng.Fori(0, TURNS) as turn:
                pb = Turn(turn)
                body(pb + 1, ("turn", pb))
            body(B - 1, ("last", None))
            tail(("tail", None))

        def batch(t, b, n=1, axis=1):
            return t[:, b:b + n] if isinstance(b, int) else t[:, bass.ds(val(b), n)]

        block = ctx.enter_context(nc.Block())

        @block.sync
        def _(sp):
            def rows_in(n, ap, where):
                sp.dma_start(where, ap.rearrange("(a p) n -> p a n", p=P)).then_inc(wm_in[n], 16)

            sp.dma_start(cT[:], io["cT"].rearrange("(a p) b -> p a b", p=P)).then_inc(c_in, 16)
            sp.dma_start(x[:, 0:NT, :], io["x"][0:S, :].rearrange("(t p) d -> p t d", p=P)).then_inc(x0_in, 16)
            rows_in(0, io["wmod"][0], wm[0])
            for w, src in enumerate((io["wq"], io["wk"])):
                sp.dma_start(wq[:, w], src.rearrange("(a p) n -> p a n", p=P)).then_inc(qk_in, 16)
            sp.dma_start(rope[:, 0], io["cos"]).then_inc(qk_in, 16)
            sp.dma_start(rope[:, 1], io["sin"]).then_inc(qk_in, 16)
            rows_in(1, io["wmod"][1], wm[1])
            filled(sp, ("MT",), ("init", None))
            rows_in(2, io["wmod"][2], wm[0])
            sp.dma_start(wv[:], io["wv"].rearrange("(a p) n -> p a n", p=P)).then_inc(w_in, 16)
            sp.dma_start(wg[:], io["wg"].rearrange("(a p) n -> p a n", p=P)).then_inc(w_in, 16)
            sp.dma_start(bg[:], wide(io["bg"].rearrange("(a e) -> a e", a=1), 0, P)).then_inc(w_in, 16)
            sp.wait_ge(wo_zero, 1)
            for i in range(HU):
                sp.dma_start(wo[32 * i:32 * i + DK],
                             io["wo"].rearrange("(g i d) n -> i d g n", g=NU, i=HU)[i]).then_inc(w_in, 16)

            def rest_in():
                for b in range(1, B):
                    sp.dma_start(x[:, NT * b:NT * (b + 1), :],
                                 io["x"][S * b:S * (b + 1), :].rearrange("(t p) d -> p t d", p=P)).then_inc(x_in, 16)
                sp.wait_ge(zeroed, 1)
                for r in range(0, E * CAP, 4 * P):
                    sp.dma_start(disp[r:r + 4 * P, :].rearrange("(t p) d -> p t d", p=P),
                                 attnT[:, NU - 1].rearrange("p (t d) -> p t d", t=4)).then_inc(zero_out, 16)

            def stack(b, g, ch):
                s = g % 2
                for i in range(2):
                    sp.wait_ge(scr_ready[i], val(b * 32 + 32))
                hold(sp)
                if not (isinstance(b, int) and b == 0 and g < 2):
                    sp.wait_ge(t_ready, val(unit(b, g - 2) * UT + (UT, PAST_HALF)[ch == 0]))
                    hold(sp)
                cols = slice(BANK * ch, BANK * (ch + 1))
                for w in (1, 0):
                    table = io["scr"][b:b + 1, w] if isinstance(b, int) else io["scr"][bass.ds(val(b), 1), w]
                    rows = table[:, 32 * g:32 * g + 32].rearrange("o (r i) z n -> (o z) r i n", i=HU)[:, :, :, cols]
                    for n, (r0, count) in enumerate(SLOTS):
                        if w:
                            sp.dma_start(stk[r0:r0 + count, s, 1, :, cols],
                                         rows[0:count // 8]).then_inc(stk_ready[s][ch], 16)
                        else:
                            for r in range(r0, r0 + count, 16):
                                sp.dma_start(stk[r:r + 16, s, 0, :, cols],
                                             rows[2 * n:2 * n + 2]).then_inc(stk_ready[s][ch], 16)

            def max_rows(b, g, at):
                emptied(sp, ("M", g), at)
                hold(sp)
                for part in range(2):
                    sp.dma_start(stk[MROW + part:MROW + part + 1, g % 2, 0],
                                 mT[HU * part:HU * part + HU, :]).then_inc(mrow_ready[g % 2], 16)

            def reciprocals(b, g):
                u = unit(b, g)
                sp.wait_ge(pv_copied, val(u * 2 + 4))
                hold(sp)
                sp.dma_start(io["sums"], attnT[DK:P:32, g]).then_inc(sums_out, 16)
                sp.wait_ge(sums_out, val(u * 16 + 16))
                hold(sp)
                sp.dma_start(sums[:], io["sums"].rearrange("i (p c) -> (i p) c", p=P // HU)).then_inc(sums_in, 16)
                sp.wait_ge(recip_done, val(u + 1))
                hold(sp)
                sp.dma_start(io["rsums"].rearrange("i (p c) -> (i p) c", p=P // HU), sums[:]).then_inc(recip_out, 16)
                sp.wait_ge(recip_out, val(u * 16 + 16))
                hold(sp)
                sp.wait_ge(attn_ready, val(u + 1))
                hold(sp)
                for i in range(HU):
                    sp.dma_start(rsum[32 * i:32 * i + 32], wide(io["rsums"][i:i + 1], 0, 32)).then_inc(rsum_in, 16)

            stack(0, 0, 0)
            stack(0, 0, 1)
            stack(0, 1, 0)
            max_rows(0, 0, ("init", None))

            def body(b, at):
                last = at[0] == "last"
                for g in range(NU):
                    nb, ng = after_unit(b, g)
                    n2b, n2g = after_unit(nb, ng)
                    if not (last and g == NU - 1):
                        stack(nb, ng, 1)
                    if at[0] != "first" or g:
                        reciprocals(*((b, g - 1) if g else (b - 1 if isinstance(b, int) else at[1], NU - 1)))
                    early = g != 2
                    if early and not (last and g >= NU - 2):
                        stack(n2b, n2g, 0)
                    if not (last and g == NU - 1):
                        max_rows(nb, ng, at)
                    if at[0] == "first" and g == 0:
                        rest_in()
                    if not early and not last:
                        stack(n2b, n2g, 0)

            def tail(at):
                reciprocals(B - 1, NU - 1)
                sp.wait_ge(pv_done, B * NU * UT + NPROB)
                for c in range(RING):
                    sp.dma_start(keep["ring"][:, c], weight_piece(io, slice(0, 1), "w12", c),
                                 ).then_inc(keep["raw_ready"][c], 16)

            program(sp, body, tail)

        @block.gpsimd
        def _(pool):
            c = Counter(pool, pool_step, POOL_STEPS)
            tt = nc.gpsimd.tensor_tensor
            init = ("init", None)

            def step(at, ins):
                c.step(at, ins)
                hold(pool)

            pool.sem_inc(attn_ready, 1)
            pool.sem_inc(h2_free, 1)
            nc.gpsimd.memset(wo[:], 0.0).then_inc(wo_zero, 1)
            nc.gpsimd.memset(half[:], -0.5).then_inc(consts, 1)
            nc.gpsimd.memset(attnT[:, NU - 1], 0.0).then_inc(zeroed, 1)
            nc.gpsimd.memset(identf[:], 0.0)
            nc.gpsimd.memset(ident[:], 0.0)
            nc.gpsimd.memset(mask_k[:], 0.0)
            nc.gpsimd.memset(mask_q[:], 0.0)
            step(init, nc.gpsimd.memset(tri[:], 1.0))
            for t in (identf, ident):
                nc.gpsimd.affine_select(out=t[:], in_=t[:], compare_op=ALU.not_equal, fill=1.0, base=0,
                                        pattern=[[-1, P]], channel_multiplier=1).then_inc(consts, 1)
            nc.gpsimd.affine_select(out=mask_k[:], in_=mask_k[:], compare_op=ALU.is_ge, fill=-BIG, base=0,
                                    pattern=[[-1, P]], channel_multiplier=1).then_inc(consts, 1)
            nc.gpsimd.affine_select(out=mask_q[:], in_=mask_q[:], compare_op=ALU.is_ge, fill=-BIG, base=0,
                                    pattern=[[1, P]], channel_multiplier=-1).then_inc(consts, 1)
            nc.gpsimd.affine_select(out=tri[:], in_=tri[:], compare_op=ALU.is_ge, fill=0.0, base=0,
                                    pattern=[[1, P]], channel_multiplier=-1).then_inc(consts, 1)
            nc.gpsimd.memset(ones[:], 1.0).then_inc(consts, 1)
            nc.gpsimd.iota(eio[:], pattern=[[1, E]], base=0, channel_multiplier=0,
                           allow_small_or_imprecise_dtypes=True).then_inc(consts, 1)
            nc.gpsimd.iota(ebase[:], pattern=[[CAP, E]], base=-1 - TRASH, channel_multiplier=0,
                           allow_small_or_imprecise_dtypes=True).then_inc(consts, 1)
            nc.gpsimd.memset(va[:, :, :, DK:32], 1.0).then_inc(consts, 1)
            nc.gpsimd.memset(seqb[:], 0.0).then_inc(consts, 1)
            pool.wait_ge(consts, CONSTS)

            def power(which, count):
                pool.wait_ge(var_ready[which], val(count))
                hold(pool)
                tt(rstd[:, which], vareps[:, which], half[:], ALU.pow).then_inc(rstd_ready[which], 1)

            def rotate(b, at, n):
                for eo in range(2):
                    emptied(pool, (f"QK{n}", eo), at)
                hold(pool)
                r = rt[:, n % 2]
                tt(r[:, 0], r[:, 0], r[:, 3], ALU.subtract)
                tt(r[:, 1], r[:, 2], r[:, 1], ALU.add).then_inc(rotated, 1)

            def third_part(b, at, n):
                ch, w = divmod(n, 2)
                pool.wait_ge(part1_ready, val(b * 4 + (n + 1)))
                hold(pool)
                tt(parts[:, n % 2, 2], rt[:, n % 2, 0:2], parts[:, n % 2, 1], ALU.subtract).then_inc(part2_ready, 1)
                pool.wait_ge(part2_ready, val(b * 4 + (n + 1)))
                hold(pool)
                table = io["scr"][b:b + 1, w] if isinstance(b, int) else io["scr"][bass.ds(val(b), 1), w]
                pool.dma_start(table.rearrange("o q z n -> (o q) z n")[:, :, BANK * ch:BANK * (ch + 1)],
                               parts[:, n % 2].rearrange("p z e n -> p (z e) n"),
                               ).then_inc(scr_ready[n % 2], 16)

            def normalise(b, g):
                pool.wait_ge(rsum_in, val(unit(b, g) * (16 * HU) + 16 * HU))
                hold(pool)
                tt(attnT[:, g], attnT[:, g], rsum[:], ALU.mult).then_inc(attn_ready, 1)

            def modulate(pb, at, hf):
                pool.wait_ge(xn_ready[1], val(pb * 2 + (hf + 1)))
                hold(pool)
                ts = slice(4 * hf, 4 * hf + 4)
                rows = batch(modrow, pb)
                step(at, tt(h2[:, ts], h2[:, ts], wide(rows[:, :, 2], 1, 4), ALU.mult))
                tt(h2[:, ts], h2[:, ts], wide(rows[:, :, 1], 1, 4), ALU.add).then_inc(h2m_ready, 1)

            def scatter(pb, tiles):
                pool.wait_ge(slot_ready, val(pb + 1))
                pool.wait_ge(h2m_ready, val(pb * 2 + 2))
                hold(pool)
                for t in tiles:
                    for ch in range(TOPK):
                        nc.gpsimd.indirect_dma_start(
                            disp[:, :], bass.IndirectOffsetOnAxis(ap=slotb[:, ch, t:t + 1], axis=0),
                            h2[:, t], None, bounds_check=TRASH - 1, oob_is_err=False,
                        ).then_inc(scattered, 16)
                if tiles[-1] == NT - 1:
                    pool.wait_ge(scattered, val(pb * (NT * TOPK * 16) + NT * TOPK * 16))
                    pool.sem_inc(h2_free, 1)

            power(0, 1)
            for n in range(4):
                rotate(0, init, n)
                third_part(0, init, n)
            c.close("init")

            def do(name, b, g, at):
                pb = at[1] if at[0] == "turn" else b - 1
                if name == "recip" and (at[0] != "first" or g):
                    normalise(*((b, g - 1) if g else (pb, NU - 1)))
                elif name == "stats2":
                    power(1, pb + 1)
                elif name in ("norm2a", "norm2b"):
                    modulate(pb, at, name == "norm2b")
                elif name == "route2":
                    scatter(pb, range(0, 4))
                elif name == "stats1":
                    power(0, b + 2)
                elif name[:3] == "rot":
                    rotate(b + 1, at, int(name[3]))
                elif name[:3] == "low":
                    third_part(b + 1, at, int(name[3]))

            def body(b, at):
                for g in range(NU):
                    if g == 3 and at[0] == "first":
                        pool.wait_ge(zero_out, 16 * E * CAP // (4 * P))
                    if g == 3 and at[0] != "first":
                        scatter(at[1] if at[0] == "turn" else b - 1, range(4, NT))
                    for _, name in steps(at[0], g):
                        do(name, b, g, at)
                c.close(at[0])

            def tail(at):
                normalise(B - 1, NU - 1)
                for name in POST_STEPS:
                    do(name, B, 0, at)
                scatter(B - 1, range(4, NT))
                c.close(at[0])

            program(pool, body, tail)

        @block.scalar
        def _(act):
            init = ("init", None)
            act.sem_inc(exp_done, 2)
            act.sem_inc(pv_copied, 2)
            act.wait_ge(c_in, 16)
            nc.scalar.activation(sc[:, 0], cT[:], ACT.Exp, scale=-1.0).then_inc(silu_e, 1)

            def evac_T(b, name, at):
                ch, d = LETTER[name[-1]]
                bank = filled(act, (name,), at)
                hold(act)
                out = hT[:, d, BANK * ch:BANK * (ch + 1)]
                if name[1] == "2":
                    nc.scalar.copy(out, psM[:, bank]).then_inc(bank_free[bank], 1)
                else:
                    shift = modT[:, d, b:b + 1] if isinstance(b, int) else modT[:, d, bass.ds(val(b), 1)]
                    scale = modT[:, DC + d, b:b + 1] if isinstance(b, int) else modT[:, DC + d, bass.ds(val(b), 1)]
                    nc.scalar.activation(out, psM[:, bank], ACT.Identity, bias=shift,
                                         scale=scale).then_inc(bank_free[bank], 1)

            def evac_V(b, p, at):
                bank = filled(act, ("V", p), at)
                nc.scalar.copy(va[:, 2 * p:2 * p + 2, :, 0:DK],
                               psM[:, bank].rearrange("p (t h d) -> p t h d", t=2, h=NH)).then_inc(bank_free[bank], 1)
                emptied(act, ("V", p), at)
                act.sem_inc(v_ready, 1)

            def part(b, n, z):
                if z == 0:
                    act.wait_ge(rotated, val(b * 4 + (n + 1)))
                    if not (isinstance(b, int) and b == 0 and n < 2):
                        act.wait_ge(scr_ready[n % 2], val(b * 32 + 16 * (n // 2)))
                else:
                    act.wait_ge(rest_ready, val(b * 4 + (n + 1)))
                nc.scalar.copy(parts[:, n % 2, z], rt[:, n % 2, 0:2]).then_inc((part0_ready, part1_ready)[z], 1)

            def exponentials(b, g, n):
                j, s, a, e, heads = ATT_TILES[n]
                w = (e - a) * len(heads)
                act.wait_ge(t_ready, val(unit(b, g) * UT + (n + 1)))
                act.wait_ge(pv_done, val(unit(b, g) * UT + (n + 1)))
                nc.scalar.activation(prob[:, (g * UT + n) % NPROB, 0:w], psT[:, n % 2, 0:w], ACT.Exp,
                                     scale=DK ** -0.5).then_inc(exp_done, 1)

            def evac_O(b, g, hf):
                act.wait_ge(pv_done, val(unit(b, g) * UT + (HALF_END[hf] + 1 + NPROB)))
                nc.scalar.copy(attnT[:, g, BANK * hf:BANK * (hf + 1)], psO[:, hf]).then_inc(pv_copied, 1)

            act.wait_ge(silu_r, 3)
            for name in ("Ta", "Tb", "Tc", "Td"):
                evac_T(0, name, init)
            for n in range(4):
                part(0, n, 0)
                part(0, n, 1)
            act.wait_ge(consts, CONSTS)
            for p in range(NT // 2):
                evac_V(0, p, init)

            def do(name, b, g, at):
                pb = at[1] if at[0] == "turn" else b - 1
                if name[0] == "T":
                    evac_T(b + 1, name, at)
                elif name[:3] == "rot":
                    part(b + 1, int(name[3]), 0)
                elif name[:3] == "low":
                    part(b + 1, int(name[3]), 1)
                elif name == "C":
                    act.wait_ge(gap_ready, val(pb + 1))
                    nc.scalar.activation(gap[:, 1], gap[:, 0], ACT.Exp).then_inc(gap_exp, 1)

            def body(b, at):
                for g in range(NU):
                    todo = steps(at[0], g)
                    if at[0] in ("turn", "last") and g == 0:
                        pb = at[1] if at[0] == "turn" else b - 1
                    for n in range(UT):
                        exponentials(b, g, n)
                        for _, name in [t for t in todo if t[0] == n]:
                            do(name, b, g, at)
                        if n == HALF_END[0] + 6:
                            if g == 0 and at[0] != "first":
                                filled(act, ("O3",), at)
                            if g == NU - 1 and at[0] == "first":
                                act.wait_ge(zero_out, 16 * E * CAP // (4 * P))
                            evac_O(b, g, 0)
                    evac_O(b, g, 1)
                if at[0] != "last":
                    for p in range(NT // 2):
                        evac_V(b + 1, p, at)

            def tail(at):
                for name in POST_STEPS:
                    do(name, B, 0, at)

            program(act, body, tail)

        @block.vector
        def _(dve):
            v = nc.vector
            c = Counter(dve, dve_step, DVE_STEPS)
            init = ("init", None)
            step = c.step
            dve.sem_inc(s_maxed, 2)
            dve.wait_ge(silu_e, 1)
            step(init, v.tensor_scalar_add(sc[:, 1], sc[:, 0], 1.0))
            step(init, v.reciprocal(sc[:, 2], sc[:, 1]))
            step(init, v.tensor_tensor(sc[:, 0], sc[:, 2], cT[:], ALU.mult))
            for a in range(DC):
                v.tensor_copy(silc[:, a], wide(sc[:, 0, a].unsqueeze(2), 2, P)).then_inc(silu_r, 1)
            for s in range(2):
                v.memset(stk[MROW:STACK, s, 1].rearrange("p h n -> p (h n)").bitcast(F32),
                         MINUS_ONES).then_inc(minus_ones, 1)
            bank = filled(dve, ("MT",), init)
            v.tensor_copy(modT[:], psM[:, bank, 0:2 * DC * B].rearrange("p (z b) -> p z b", b=B),
                          ).then_inc(bank_free[bank], 1)
            emptied(dve, ("MT",), init)
            v.tensor_scalar_add(modT[:, DC:2 * DC], modT[:, DC:2 * DC], 1.0).then_inc(silu_r, 1)
            dve.wait_ge(silu_r, 3)

            def rows_of(b):
                return (lambda t, n=1: x[:, NT * b + t:NT * b + t + n, :]) if isinstance(b, int) else (
                    lambda t, n=1: x[:, bass.ds(val(b * NT + t), n), :])

            def layer_stats(b, at, which):
                hold(dve)
                for t in range(NT):
                    ins = v.bn_stats(stats[:, which, t], rows_of(b)(t)[:, 0])
                step(at, ins)
                hold(dve)
                for t in range(NT):
                    ins = v.bn_aggr(meanvar[:, which, t], stats[:, which, t])
                step(at, ins)
                v.tensor_scalar_add(vareps[:, which], meanvar[:, which, :, 1], EPS).then_inc(var_ready[which], 1)

            def normed(b, hf, which, out):
                for t in range(4):
                    n = 4 * hf + t
                    ins = v.tensor_scalar(out[:, t], rows_of(b)(n)[:, 0], meanvar[:, which, n, 0:1],
                                          rstd[:, which, n:n + 1], ALU.subtract, ALU.mult)
                ins.then_inc(xn_ready[which], 1)

            def rope_products(b, n, at):
                ch = n // 2
                if not (isinstance(b, int) and b == 0 and n < 2):
                    dve.wait_ge(part2_ready, val(b * 4 + (n - 1)))
                cs = slice(BANK * ch, BANK * (ch + 1))
                for eo in range(2):
                    bank = filled(dve, (f"QK{n}", eo), at)
                    v.tensor_tensor(rt[:, n % 2, eo], psM[:, bank], rope[:, 0, cs], ALU.mult)
                    v.tensor_tensor(rt[:, n % 2, 2 + eo], psM[:, bank], rope[:, 1, cs],
                                    ALU.mult).then_inc(bank_free[bank], 1)

            def rest(b, n):
                r = rt[:, n % 2, 0:2]
                dve.wait_ge(part0_ready, val(b * 4 + (n + 1)))
                v.tensor_tensor(r, r, parts[:, n % 2, 0], ALU.subtract).then_inc(rest_ready, 1)

            def maximum(b, g, n):
                i, s, a, e, heads = MAX_TILES[n]
                w, nh = e - a, len(heads)
                dve.wait_ge(s_ready, val(unit(b, g) * UT + (n + 1)))
                v.tensor_reduce(mx[:, s, heads[0]:heads[0] + nh, i],
                                psS[:, n % 2, 0:w * nh].rearrange("p (h w) -> p h w", h=nh), AX.X,
                                ALU.max).then_inc(s_maxed, 1)

            def max_parts(b, g, at):
                dve.wait_ge(s_maxed, val(unit(b, g) * UT + (UT + 2)))
                v.tensor_copy(mxr[:, :, 0:4], mx[:, 0, :, 0:4])
                step(at, v.tensor_tensor(mxr[:, :, 4:8], mx[:, 0, :, 4:8], mx[:, 1, :, 4:8], ALU.max))
                step(at, v.tensor_copy(mp[:, 0], mxr[:]))
                v.tensor_tensor(mp[:, 1], mxr[:], mp[:, 0], ALU.subtract).then_inc(mp_ready, 1)

            def max_evac(b, g, at):
                bank = filled(dve, ("M", g), at)
                if not (isinstance(b, int) and b == 0 and g == 0):
                    dve.wait_ge(mrow_ready[(g + 1) % 2], val((b * 2 + (g + 1) // 2 if g else b * 2) * 32))
                v.tensor_copy(mT[:], psM_bf16[bank][0:2 * HU, :]).then_inc(bank_free[bank], 1)

            def reciprocal(b, g):
                dve.wait_ge(sums_in, val(unit(b, g) * 16 + 16))
                v.reciprocal(sums[:], sums[:]).then_inc(recip_done, 1)

            def residual(pb, p, at):
                bank = filled(dve, (f"O{p}",), at)
                src = psM[:, bank].rearrange("p (t d) -> p t d", t=2)
                ga = batch(modrow, pb)[:, :, 0]
                v.tensor_tensor(yb[:], src, wide(ga, 1, 2), ALU.mult).then_inc(bank_free[bank], 1)
                emptied(dve, (f"O{p}",), at)
                xt = rows_of(pb)(2 * p, 2)
                step(at, v.tensor_tensor(xt, xt, yb[:], ALU.add))

            def route_labels(pb, at):
                bank = filled(dve, ("G",), at)
                v.tensor_tensor(lg[:], psM[:, bank, 0:NT * E].rearrange("p (t e) -> p t e", e=E),
                                wide(bg[:].unsqueeze(1), 1, NT), ALU.add).then_inc(bank_free[bank], 1)
                emptied(dve, ("G",), at)
                hold(dve)
                for t in range(NT):
                    ins = v.max(top[:, t], lg[:, t])
                step(at, ins)
                v.tensor_tensor(gap[:, 0], top[:, :, 1], top[:, :, 0], ALU.subtract).then_inc(gap_ready, 1)
                for t in range(NT):
                    ins = v.max_index(topi[:, t], top[:, t], lg[:, t])
                step(at, ins)
                step(at, v.tensor_copy(topf[:], topi[:]))
                for ch in range(TOPK):
                    ins = v.tensor_tensor(oh[:, ch], wide(eio[:].unsqueeze(1), 1, NT),
                                          wide(topf[:, :, ch:ch + 1], 2, E), ALU.is_equal)
                step(at, ins)
                v.tensor_tensor(label[:], oh[:, 0], oh[:, 1], ALU.add)
                step(at, v.tensor_tensor(rw[:, 0], oh[:, 0], oh[:, 1], ALU.add))
                step(at, v.tensor_reduce(lsum[:], rw[:, 0].rearrange("p t e -> p e t"), AX.X, ALU.add))
                v.tensor_copy(lsumb[:], lsum[:]).then_inc(label_ready, 1)

            def route_slots(pb, at):
                bank = filled(dve, ("C",), at)
                cum = psM[:, bank, 0:NT * E].rearrange("p (t e) -> p t e", e=E)
                step(at, v.tensor_tensor(rw[:, 0], cum, wide(seqb[:].unsqueeze(1), 1, NT), ALU.add))
                v.tensor_tensor(seqb[:], psM[:, bank, NT * E:NT * E + E], seqb[:],
                                ALU.add).then_inc(bank_free[bank], 1)
                v.tensor_scalar(rw[:, 1], rw[:, 0], float(CAP), None, ALU.is_le)
                step(at, v.tensor_tensor(rw[:, 2], rw[:, 0], wide(ebase[:].unsqueeze(1), 1, NT), ALU.add))
                step(at, v.tensor_tensor(rw[:, 0], rw[:, 1], rw[:, 2], ALU.mult))
                for ch in range(TOPK):
                    ins = v.tensor_tensor(rw[:, 2 + ch], rw[:, 0], oh[:, ch], ALU.mult)
                step(at, ins)
                for ch in range(TOPK):
                    ins = v.tensor_reduce(slotf[:, ch], rw[:, 2 + ch], AX.X, ALU.add)
                step(at, ins)
                dve.wait_ge(h2_free, val(pb + 1))
                v.tensor_scalar_add(slotb[:], slotf[:], float(TRASH)).then_inc(slot_ready, 1)
                step(at, v.tensor_scalar(gx[:, 0:2], slotf[:], 0.0, None, ALU.is_lt))
                step(at, v.scalar_tensor_tensor(out=gx[:, 2:4], in0=slotf[:], scalar=float(TRASH + 1),
                                                in1=gx[:, 0:2], op0=ALU.add, op1=ALU.mult))
                v.tensor_tensor(gx[:, 0], gx[:, 2], gx[:, 3], ALU.min)
                v.tensor_tensor(gx[:, 1], gx[:, 2], gx[:, 3], ALU.max)
                step(at, v.tensor_tensor(gx[:, 4], gx[:, 2], gx[:, 3], ALU.is_gt))
                v.tensor_scalar_add(batch(slot_of, pb)[:, 0], gx[:, 0:2], 0.0)
                dve.wait_ge(gap_exp, val(pb + 1))
                step(at, v.tensor_scalar_add(gap[:, 2], gap[:, 1], 1.0))
                step(at, v.reciprocal(gap[:, 2], gap[:, 2]))
                v.tensor_scalar(gx[:, 5], gx[:, 4], -1.0, 1.0, ALU.mult, ALU.add)
                step(at, v.tensor_tensor(gap[:, 1], gap[:, 1], gap[:, 2], ALU.mult))
                for to, which in ((6, 5), (8, 4)):
                    v.tensor_tensor(gx[:, to], gap[:, 2], gx[:, which], ALU.mult)
                    ins = v.tensor_tensor(gx[:, to + 1], gap[:, 1], gx[:, which], ALU.mult)
                step(at, ins)
                wt = batch(weight_of, pb)[:, 0]
                v.tensor_tensor(wt[:, 0], gx[:, 6], gx[:, 9], ALU.add)
                step(at, v.tensor_tensor(wt[:, 1], gx[:, 7], gx[:, 8], ALU.add))

            def first_norm(b, hf, at):
                if hf:
                    filled(dve, ("Ta",), at)
                    filled(dve, ("Tb",), at)
                else:
                    dve.wait_ge(rstd_ready[0], val(b + 1))
                    hold(dve)
                normed(b, hf, 0, xn)

            dve.wait_ge(consts, CONSTS)
            dve.wait_ge(x0_in, 16)
            layer_stats(0, init, 0)
            for hf in range(2):
                first_norm(0, hf, init)
            dve.wait_ge(qk_in, 16 * 4)
            for n in range(4):
                rope_products(0, n, init)
                if n:
                    rest(0, n - 1)
            rest(0, 3)
            for f in range(2):
                for b in range(B):
                    bank = filled(dve, ("R", b, f), init)
                    src = psM[:, bank].rearrange("p (z d) -> p z d", z=2)
                    if f == 0:
                        v.tensor_copy(modrow[:, b, 0:2], src).then_inc(bank_free[bank], 1)
                    else:
                        v.tensor_copy(modrow[:, b, 2], src[:, 0])
                        v.tensor_copy(gb_row[:, b], src[:, 1]).then_inc(bank_free[bank], 1)
            dve.wait_ge(w_in, 16 * 7)
            for n in range(UT):
                maximum(0, 0, n)
            max_parts(0, 0, init)
            max_evac(0, 0, init)
            for bank in range(2):
                emptied(dve, ("R", B - 1 - bank, 1), init)
            step(init, v.tensor_scalar_add(modrow[:, :, 2], modrow[:, :, 2], 1.0))
            dve.wait_ge(part2_ready, 4)
            for g_ in (modrow[:, :, 0], gb_row[:]):
                sgn, mag = (rt[:, i, 0:2].rearrange("p a n -> p (a n)").rearrange("p (b d) -> p b d", b=B)
                            for i in range(2))
                step(init, v.tensor_scalar(sgn, g_, 0.0, 2.0, ALU.is_ge, ALU.mult))
                step(init, v.tensor_scalar_add(sgn, sgn, -1.0))
                step(init, v.tensor_tensor(mag, g_, sgn, ALU.mult))
                step(init, v.scalar_tensor_tensor(out=g_, in0=mag, scalar=0.25, in1=sgn, op0=ALU.max, op1=ALU.mult))
            c.close("init")

            def do(name, b, g, at):
                pb = at[1] if at[0] == "turn" else b - 1
                nb, ng = after_unit(b, g)
                if name == "recip" and (at[0] != "first" or g):
                    reciprocal(*((b, g - 1) if g else (pb, NU - 1)))
                elif name == "maxparts":
                    max_parts(nb, ng, at)
                elif name == "mT":
                    max_evac(nb, ng, at)
                elif name[0] == "O":
                    residual(pb, int(name[1]), at)
                elif name == "stats2":
                    layer_stats(pb, at, 1)
                elif name[:5] == "norm2":
                    if name == "norm2a":
                        dve.wait_ge(rstd_ready[1], val(pb + 1))
                        dve.wait_ge(h2_free, val(pb + 1))
                        hold(dve)
                    hf = int(name == "norm2b")
                    normed(pb, hf, 1, h2[:, 4 * hf:4 * hf + 4])
                elif name == "route1":
                    route_labels(pb, at)
                elif name == "route2":
                    route_slots(pb, at)
                elif name == "stats1":
                    if at[0] == "first":
                        dve.wait_ge(x_in, 16 * (B - 1))
                    layer_stats(b + 1, at, 0)
                elif name[:5] == "norm1":
                    first_norm(b + 1, int(name == "norm1b"), at)
                elif name[:2] == "QK":
                    rope_products(b + 1, int(name[2]), at)
                elif name[:3] == "sub":
                    rest(b + 1, int(name[3]))

            def body(b, at):
                for g in range(NU):
                    nb, ng = after_unit(b, g)
                    todo = steps(at[0], g)
                    for n in range(UT):
                        if not (at[0] == "last" and g == NU - 1):
                            for m in MAX_AT[n]:
                                maximum(nb, ng, m)
                        for _, name in [t for t in todo if t[0] == n]:
                            do(name, b, g, at)
                c.close(at[0])

            def tail(at):
                reciprocal(B - 1, NU - 1)
                for name in POST_STEPS:
                    do(name, B, 0, at)
                c.close(at[0])

            program(dve, body, tail)

        @block.tensor
        def _(pe):
            mm, tr = nc.tensor.matmul, nc.tensor.transpose
            init = ("init", None)
            pe.sem_inc(pv_done, NPROB)
            pe.wait_ge(silu_r, DC)
            pe.wait_ge(wm_in[0], 16)
            bank = claim(pe, ("MT",), init)
            for z in range(2 * DC):
                for a in range(DC):
                    ins = mm(psM[:, bank, B * z:B * (z + 1)], wm[0][:, a, P * z:P * (z + 1)], sc[:, 0, a],
                             start=a == 0, stop=a == DC - 1)
            ins.then_inc(bank_ready[bank], 1)

            def turn(name, at, src):
                _, d = LETTER[name[-1]]
                bank = claim(pe, (name,), at)
                for t in range(4):
                    ins = tr(psM[:, bank, P * t:P * (t + 1)], src[:, t, P * d:P * (d + 1)], identf[:])
                ins.then_inc(bank_ready[bank], 1)

            def turn_x(b, name, at):
                ch, _ = LETTER[name[-1]]
                pe.wait_ge(xn_ready[0], val(b * 2 + (ch + 1)))
                turn(name, at, xn)

            def project(b, n, at):
                ch, w = divmod(n, 2)
                for d in "ab" if ch == 0 else "cd":
                    emptied(pe, ("T" + d,), at)
                for eo in range(2):
                    bank = claim(pe, (f"QK{n}", eo), at)
                    for a in range(DC):
                        ins = mm(psM[:, bank], wq[:, w, a, P * eo:P * (eo + 1)], hT[:, a, BANK * ch:BANK * (ch + 1)],
                                 start=a == 0, stop=a == DC - 1)
                    ins.then_inc(bank_ready[bank], 1)

            def values(p, at):
                bank = claim(pe, ("V", p), at)
                for t in range(2):
                    for a in range(DC):
                        ins = mm(psM[:, bank, D * t:D * (t + 1)], hT[:, a, P * (2 * p + t):P * (2 * p + t + 1)],
                                 wv[:, a], start=a == 0, stop=a == DC - 1)
                ins.then_inc(bank_ready[bank], 1)

            def maxima_turn(b, g, at):
                pe.wait_ge(mp_ready, val(unit(b, g) + 1))
                bank = claim(pe, ("M", g), at)
                cols = mp[:].rearrange("p z h t -> p (z h) t")
                for i in range(NT):
                    ins = tr(psM_bf16[bank][0:2 * HU, P * i:P * (i + 1)], cols[:, :, i], ident[:])
                ins.then_inc(bank_ready[bank], 1)

            def first_pass(b, g, n):
                s = g % 2
                i, _, a, e, heads = MAX_TILES[n]
                for ch in range(CH):
                    if n == (0, MAX_HALF)[ch]:
                        pe.wait_ge(stk_ready[s][ch], val((b * 2 + (g // 2 + 1)) * (16 * STK_DMAS)))
                pe.wait_ge(s_maxed, val(apart(unit(b, g) * UT + (n + 1))))
                w = e - a
                diag = e == P * (i + 1)
                for m, h in enumerate(heads):
                    out = psS[:, n % 2, w * m:w * (m + 1)]
                    ins = mm(out, stk[0:MROW, s, 0, h, P * i:P * (i + 1)], stk[0:MROW, s, 1, h, a:e],
                             start=True, stop=not diag)
                    if diag:
                        ins = mm(out[:, w - P:w], ident[:], mask_k[:], start=False, stop=True)
                ins.then_inc(s_ready, 1)

            def second_pass(b, g, n):
                s = g % 2
                j, _, a, e, heads = ATT_TILES[n]
                pe.wait_ge(exp_done, val(unit(b, g) * UT + (n + 1)))
                w = e - a
                diag = a == P * j
                for m, h in enumerate(heads):
                    out = psT[:, n % 2, w * m:w * (m + 1)]
                    ins = mm(out, stk[:, s, 1, h, P * j:P * (j + 1)], stk[:, s, 0, h, a:e],
                             start=True, stop=not diag)
                    if diag:
                        ins = mm(out[:, 0:P], ident[:], mask_q[:], start=False, stop=True)
                ins.then_inc(t_ready, 1)

            def weigh(b, g, end):
                j, s, a, e, heads = ATT_TILES[end]
                w, first = e - a, end + 1 - HU // len(heads)
                hf = a // BANK
                pe.wait_ge(exp_done, val(unit(b, g) * UT + (end + 3)))
                if j == 0:
                    pe.wait_ge(pv_copied, val(unit(b, g) * 2 + (hf + 1)))
                for n in range(first, end + 1):
                    slot = (g * UT + n) % NPROB
                    for m, h in enumerate(ATT_TILES[n][4]):
                        ins = mm(psO[32 * h:32 * h + 32, hf, a - BANK * hf:e - BANK * hf], va[:, j, HU * g + h],
                                 prob[:, slot, w * m:w * (m + 1)], start=j == 0, stop=n >= HALF_END[hf] - HU + 1
                                 and end == HALF_END[hf], tile_position=(0, 32 * h), skip_group_check=True)
                    ins.then_inc(pv_done, 1)

            def out_project(p, at):
                bank = claim(pe, (f"O{p}",), at)
                for t in range(2):
                    ts = slice(P * (2 * p + t), P * (2 * p + t + 1))
                    for g in range(NU):
                        ins = mm(psM[:, bank, D * t:D * (t + 1)], attnT[:, g, ts], wo[:, g],
                                 start=g == 0, stop=g == NU - 1)
                ins.then_inc(bank_ready[bank], 1)

            def gate(at):
                for name in ("T2a", "T2b", "T2c", "T2d"):
                    emptied(pe, (name,), at)
                bank = claim(pe, ("G",), at)
                for t in range(NT):
                    for a in range(DC):
                        ins = mm(psM[:, bank, E * t:E * (t + 1)], hT[:, a, P * t:P * (t + 1)], wg[:, a],
                                 start=a == 0, stop=a == DC - 1)
                ins.then_inc(bank_ready[bank], 1)

            def count_labels(pb, at):
                pe.wait_ge(label_ready, val(pb + 1))
                bank = claim(pe, ("C",), at)
                mm(psM[:, bank, 0:NT * E], tri[:], label[:].rearrange("p t e -> p (t e)"), start=True, stop=False)
                for t in range(NT - 1):
                    mm(psM[:, bank, E * (t + 1):NT * E], ones[:],
                       wide(label[:, t:t + 1], 1, NT - 1 - t), start=False, stop=t == NT - 2)
                mm(psM[:, bank, NT * E:NT * E + E], ones[:], lsumb[:], start=True,
                   stop=True).then_inc(bank_ready[bank], 1)

            pe.wait_ge(consts, CONSTS)
            for name in ("Ta", "Tb", "Tc", "Td"):
                turn_x(0, name, init)
            pe.wait_ge(qk_in, 16 * 4)
            for n in range(4):
                project(0, n, init)
            for f in range(2):
                pe.wait_ge(wm_in[f + 1], 16)
                for b in range(B):
                    bank = claim(pe, ("R", b, f), init)
                    for a in range(DC):
                        ins = mm(psM[:, bank], silc[:, a, b], wm[1 - f][:, a], start=a == 0, stop=a == DC - 1)
                    ins.then_inc(bank_ready[bank], 1)
            pe.wait_ge(w_in, 16 * 7)
            for n in range(UT):
                first_pass(0, 0, n)
            maxima_turn(0, 0, init)
            for p in range(NT // 2):
                values(p, init)
            pe.wait_ge(minus_ones, 2)

            def do(name, b, g, at):
                pb = at[1] if at[0] == "turn" else b - 1
                if name == "M":
                    maxima_turn(*after_unit(b, g), at)
                elif name[0] == "O":
                    if name == "O0":
                        pe.wait_ge(attn_ready, val(pb * NU + (NU + 1)))
                    out_project(int(name[1]), at)
                elif name[:2] == "T2":
                    ch, _ = LETTER[name[-1]]
                    pe.wait_ge(h2m_ready, val(pb * 2 + (ch + 1)))
                    turn(name, at, h2[:, 4 * ch:4 * ch + 4])
                elif name == "G":
                    gate(at)
                elif name == "C":
                    count_labels(pb, at)
                elif name[0] == "T":
                    turn_x(b + 1, name, at)
                elif name[:2] == "QK":
                    project(b + 1, int(name[2]), at)

            def body(b, at):
                for g in range(NU):
                    nb, ng = after_unit(b, g)
                    held = None
                    todo = steps(at[0], g)
                    pe.wait_ge(mrow_ready[g % 2], val((b * 2 + (g // 2 + 1)) * 32))
                    if g == 0:
                        pe.wait_ge(v_ready, val(b * (NT // 2) + NT // 2))
                    for n in range(UT):
                        second_pass(b, g, n)
                        ahead = [] if at[0] == "last" and g == NU - 1 else list(MAX_AT[n])
                        for m in ahead[0:1]:
                            first_pass(nb, ng, m)
                        if n in QUAD_END:
                            if held is not None:
                                weigh(b, g, held)
                            held = n
                        for m in ahead[1:]:
                            first_pass(nb, ng, m)
                        for _, name in [t for t in todo if t[0] == n]:
                            do(name, b, g, at)
                    weigh(b, g, held)
                if at[0] != "last":
                    for p in range(NT // 2):
                        values(p, at)

            def tail(at):
                for name in POST_STEPS:
                    do(name, B, 0, at)

            program(pe, body, tail)


def expert_block(nc, io, disp, outs, keep):
    NTE = CAP // P
    HC = H // P
    HS = CAP // 2
    STEPS = 2 * HC
    NHM = 4
    x, gb_row, slot_of, weight_of = keep["x"], keep["gb"], keep["slot"], keep["weight"]
    raw, raw_ready = keep["ring"], keep["raw_ready"]
    PIECES = {2: ("w3", 0), 3: ("w3", 1), 5: ("w12", 0), 7: ("w12", 1), 9: ("w12", 2), 11: ("w12", 3)}
    NPIECES = len(PIECES)
    with ExitStack() as ctx:
        def sb(name, shape, dt=F32):
            return ctx.enter_context(nc.sbuf_tensor(name, shape, dt))

        def sem(name):
            return ctx.enter_context(nc.semaphore(name))

        w12_hi = sb("w12_hi", [P, 2, 2 * DC, H], F32R)
        w12_lo = sb("w12_lo", [P, 2, 2 * DC, H], F32R)
        w3_hi = sb("w3_hi", [P, HC, D], F32R)
        w3_lo = sb("w3_lo", [P, HC, D], F32R)
        dx = sb("dx", [P, 2, NTE, D])
        dT = sb("dT", [P, 2, DC, CAP], F32R)
        hT = sb("hT", [P, 2, HC, CAP], F32R)
        sg = sb("sg", [P, 2, HS])
        hm = sb("hm", [P, NHM, HS])
        eo = sb("eo", [P, NTE, D])
        fid = sb("fid", [P, P])
        zrow = sb("zrow", [1, D])
        psH = ctx.enter_context(nc.psum_tensor("psH", [P, 2, 2, BANK], F32))
        psY = ctx.enter_context(nc.psum_tensor("psY", [P, 2, BANK], F32))
        held_back = sem("held_back_2")
        fid_ready = sem("fid_ready")
        zr_ready = sem("zr_ready")
        w_hi_ready = sem("w_hi_ready")
        w_lo_ready = sem("w_lo_ready")
        dx_ready = [sem(f"dx_ready{i}") for i in range(2)]
        y_ready = [sem(f"y_ready{i}") for i in range(2)]
        y_free = [sem(f"y_free{i}") for i in range(2)]
        d_hi_ready = sem("d_hi_ready")
        pair_ready = sem("pair_ready")
        silu_done = sem("silu_done")
        h_done = sem("h_done")
        h_hi_ready = sem("h_hi_ready")
        h_lo_ready = sem("h_lo_ready")
        expert_done = sem("expert_done")
        eo_ready = sem("eo_ready")
        stored = sem("stored")
        eo_free = sem("eo_free")
        zrow_stored = sem("zrow_stored")
        lo_in = [sem(f"lo_in{i}") for i in range(2)]
        lo_scaled = sem("lo_scaled")
        lo_used = sem("lo_used")
        TURNED = [(d, g) for d in range(DC) for g in range(2)]
        OUTS = [(0, 1), (2, 3), (4,)]
        SEQ_Y = [("T", 0), ("T", 1), ("O", 0), ("T", 2), ("O", 1), ("T", 3), ("O", 2)]
        USES = len(SEQ_Y)
        HEAD = 4
        block = ctx.enter_context(nc.Block())

        def w12(part, e2, w, a, cols):
            return (w12_hi, w12_lo)[part][:, e2, DC * w + a, cols]

        def w3(part, hc):
            return (w3_hi, w3_lo)[part][:, hc]

        def piece_out(part, e2, kind, c):
            if kind == "w12":
                return (w12_hi, w12_lo)[part][:, 1 - e2, c]
            return (w3_hi, w3_lo)[part][:, H // D * c:H // D * (c + 1)].rearrange("p a n -> p (a n)")

        def pieces(last):
            return [(r, n, kind, c) for n, (r, (kind, c)) in enumerate(PIECES.items()) if kind == "w3" or not last]

        def ring_use(i, e2, n):
            k = RING + NPIECES * e2 + n
            return k % RING, i * (2 * NPIECES // RING) + (k // RING + 1)

        def y_use(i, e2, name):
            k = SEQ_Y.index(name) + USES * e2 + HEAD
            return k % 2, i * USES + (k // 2 + 1)

        def head_use(n):
            return n % 2, n // 2 + 1

        def last_use(n):
            k = HEAD + USES * E - USES + n
            return k % 2, k // 2 + 1

        def turned_cols(n):
            d, g = TURNED[n]
            return d, *((0, 4 * P) if g == 0 else (4 * P, CAP))

        def experts(eng, body):
            with eng.Fori(0, E // 2 - 1) as turn:
                for e2 in range(2):
                    body(Turn(turn), e2, False)
            for e2 in range(2):
                body(E // 2 - 1, e2, e2 == 1)

        def count(i, e2, per, n):
            return val(i * (2 * per) + (per * e2 + n))

        @block.sync
        def _(sp):
            def slots_in(ex, e2):
                sp.dma_start(dx[:, e2], disp.rearrange("(e t p) n -> e p t n", e=E, p=P)[ex]
                             .rearrange("e p t n -> p (e t) n")).then_inc(dx_ready[e2], 16)

            def piece_in(ex, slot, kind, c):
                out = raw[:, slot] if kind == "w12" else raw[:, slot].rearrange("p (a n) -> p a n", n=D)
                sp.dma_start(out, weight_piece(io, ex, kind, c)).then_inc(raw_ready[slot], 16)

            def expert_at(i, e2):
                return slice(2 * i + e2, 2 * i + e2 + 1) if isinstance(i, int) else bass.ds(val(i * 2 + e2), 1)

            slots_in(expert_at(0, 0), 0)
            sp.wait_ge(zr_ready, 1)
            sp.dma_start(outs[0:1, :], zrow[:]).then_inc(zrow_stored, 16)
            sp.wait_ge(zrow_stored, 16)

            def body(i, e2, last):
                if not last:
                    sp.wait_ge(expert_done, count(i, e2, 1, 1))
                    sp.sem_inc(held_back, 1)
                    slots_in(expert_at(i, e2 + 1), 1 - e2)
                for _, n, kind, c in pieces(last):
                    sp.wait_ge(w_lo_ready, count(i, e2, NPIECES, n + 1))
                    sp.sem_inc(held_back, 1)
                    piece_in(expert_at(i, e2 + (kind == "w12")), ring_use(i, e2, n)[0], kind, c)

            experts(sp, body)

        @block.gpsimd
        def _(pool):
            pool.sem_inc(eo_free, 1)
            nc.gpsimd.memset(fid[:], 0.0).then_inc(fid_ready, 1)
            nc.gpsimd.memset(zrow[:], 0.0).then_inc(zr_ready, 1)
            pool.wait_ge(fid_ready, 1)
            nc.gpsimd.affine_select(out=fid[:], in_=fid[:], compare_op=ALU.not_equal, fill=1.0, base=0,
                                    pattern=[[-1, P]], channel_multiplier=1).then_inc(fid_ready, 1)

            def piece_rest(before, slot, out, hi):
                pool.wait_ge(w_hi_ready, val(before))
                pool.sem_inc(held_back, 1)
                nc.gpsimd.tensor_tensor(out, raw[:, slot], hi.bitcast(F32), ALU.subtract).then_inc(w_lo_ready, 1)

            pool.wait_ge(w_lo_ready, RING)

            def body(i, e2, last):
                for _, n, kind, c in pieces(last):
                    piece_rest(i * (2 * NPIECES) + (NPIECES * e2 + RING + n + 1), ring_use(i, e2, n)[0],
                               piece_out(1, e2, kind, c), piece_out(0, e2, kind, c))
                if last:
                    pool.wait_ge(zrow_stored, 16)
                    pool.wait_ge(w_lo_ready, RING + NPIECES * (E - 1))
                    for step in range(B * NT // 4):
                        if step >= 2:
                            pool.wait_ge(lo_used, 2 * (step - 1))
                        for t in range(4):
                            b, n = divmod(4 * step + t, NT)
                            nc.gpsimd.indirect_dma_start(
                                raw[:, step % 2, D * t:D * (t + 1)], None, outs[0:1 + TRASH - CAP, :],
                                bass.IndirectOffsetOnAxis(ap=slot_of[:, b, 0, n:n + 1], axis=0),
                            ).then_inc(lo_in[step % 2], 16)
                pool.wait_ge(eo_ready, count(i, e2, len(OUTS), len(OUTS)))
                pool.sem_inc(held_back, 1)
                rows = outs[1:1 + TRASH].rearrange("(e t p) n -> e p t n", e=E, p=P)
                if isinstance(i, int):
                    rows = rows[2 * i + e2:2 * i + e2 + 1]
                else:
                    rows = rows[bass.ds(val(i * 2 + e2), 1)]
                pool.dma_start(rows.rearrange("e p t n -> p (e t) n"), eo[:]).then_inc(stored, 16)
                pool.wait_ge(stored, count(i, e2, 16, 16))
                pool.sem_inc(eo_free, 1)

            experts(pool, body)

        @block.tensor
        def _(pe):
            mm, tr = nc.tensor.matmul, nc.tensor.transpose
            pe.sem_inc(expert_done, 2)
            pe.wait_ge(fid_ready, 2)
            PASSES = ((0, 1), (1, 0), (0, 0))

            def turn(n, e2, bank):
                d, a, e = turned_cols(n)
                for t in range(a // P, e // P):
                    ins = tr(psY[:, bank, P * t - a:P * (t + 1) - a], dx[:, e2, t, P * d:P * (d + 1)], fid[:])
                ins.then_inc(y_ready[bank], 1)

            pe.wait_ge(dx_ready[0], 16)
            for n in range(4):
                bank, k = head_use(n)
                pe.wait_ge(y_free[bank], k)
                turn(n, 0, bank)
            for n in (2, 3):
                bank, k = head_use(n)
                pe.wait_ge(y_free[bank], k + 1)

            def body(i, e2, last):
                pe.wait_ge(w_lo_ready, count(i, e2, NPIECES, RING))
                bank, k = y_use(i, e2 - 1, ("T", 3))
                pe.wait_ge(y_free[bank], val(k + 1))
                for r in range(STEPS):
                    hc, s = divmod(r, 2)
                    pe.wait_ge(h_done, count(i, e2, STEPS, r + 1))
                    for w in range(2):
                        for a in range(DC):
                            for z, (x1, x2) in enumerate(PASSES):
                                ins = mm(psH[:, r % 2, w, 0:HS],
                                         w12(x1, e2, w, a, slice(P * hc, P * (hc + 1))),
                                         dT[:, x2, a, HS * s:HS * (s + 1)],
                                         start=a == 0 and z == 0, stop=a == DC - 1 and z == 2)
                    ins.then_inc(pair_ready, 1)
                for name, n in SEQ_Y:
                    if name == "T" and last:
                        continue
                    bank, k = y_use(i, e2, (name, n))
                    if last:
                        bank, k = last_use(n)
                    pe.wait_ge(y_free[bank], val(k))
                    if name == "T":
                        if n == 0:
                            pe.wait_ge(dx_ready[1 - e2], val(i * 16 + 16 * (e2 + 1)))
                        turn(n, 1 - e2, bank)
                        continue
                    if n == 0:
                        pe.wait_ge(h_lo_ready, count(i, e2, STEPS, STEPS + NHM))
                        pe.wait_ge(w_lo_ready, count(i, e2, NPIECES, RING + 2))
                    for m, t in enumerate(OUTS[n]):
                        for hc in range(HC):
                            for z, (x1, x2) in enumerate(PASSES):
                                ins = mm(psY[:, bank, D * m:D * (m + 1)], hT[:, x1, hc, P * t:P * (t + 1)],
                                         w3(x2, hc),
                                         start=hc == 0 and z == 0, stop=hc == HC - 1 and z == 2)
                    ins.then_inc(y_ready[bank], 1)
                pe.wait_ge(y_ready[bank], val(k))
                pe.sem_inc(expert_done, 1)

            experts(pe, body)

        @block.scalar
        def _(act):
            def piece_round(slot, used, out):
                act.wait_ge(raw_ready[slot], val(used * 16))
                nc.scalar.copy(out, raw[:, slot]).then_inc(w_hi_ready, 1)

            def slots_round(n, bank, k):
                d, a, e = turned_cols(n)
                act.wait_ge(y_ready[bank], val(k))
                nc.scalar.copy(dT[:, 0, d, a:e], psY[:, bank, 0:e - a]).then_inc(d_hi_ready, 1)

            def hidden_round(i, e2, r):
                hc, s = divmod(r, 2)
                act.wait_ge(h_done, count(i, e2, STEPS, r + 3))
                nc.scalar.copy(hT[:, 0, hc, HS * s:HS * (s + 1)], hm[:, r % NHM]).then_inc(h_hi_ready, 1)

            for c in range(RING):
                piece_round(c, 1, piece_out(0, 1, "w12", c))
            for n in range(4):
                slots_round(n, *head_use(n))

            def body(i, e2, last):
                for r in range(STEPS):
                    act.wait_ge(pair_ready, count(i, e2, STEPS, r + 1))
                    nc.scalar.activation(sg[:, r % 2], psH[:, r % 2, 0, 0:HS], ACT.Silu).then_inc(silu_done, 1)
                    if r:
                        hidden_round(i, e2, r - 1)
                    for at, n, kind, c in pieces(last):
                        if at == r:
                            piece_round(*ring_use(i, e2, n), piece_out(0, e2, kind, c))
                hidden_round(i, e2, STEPS - 1)
                for name, n in SEQ_Y:
                    if name == "T" and last:
                        continue
                    bank, k = y_use(i, e2, (name, n)) if not last else last_use(n)
                    if name == "T":
                        slots_round(n, bank, k)
                        continue
                    if n == 0:
                        act.wait_ge(eo_free, count(i, e2, 1, 1))
                    act.wait_ge(y_ready[bank], val(k))
                    tiles = OUTS[n]
                    nc.scalar.copy(eo[:, tiles[0]:tiles[-1] + 1].rearrange("p t d -> p (t d)"),
                                   psY[:, bank, 0:D * len(tiles)]).then_inc(y_free[bank], 1)
                    act.wait_ge(y_free[bank], val(k + 1))
                    act.sem_inc(eo_ready, 1)

            experts(act, body)

        @block.vector
        def _(dve):
            v = nc.vector
            dve.sem_inc(h_done, 2)
            dve.sem_inc(h_lo_ready, NHM)
            for bank in range(2):
                dve.sem_inc(y_free[bank], 1)

            def slots_rest(n, bank, count_d):
                d, a, e = turned_cols(n)
                dve.wait_ge(d_hi_ready, count_d)
                v.tensor_tensor(dT[:, 1, d, a:e], psY[:, bank, 0:e - a], dT[:, 0, d, a:e].bitcast(F32),
                                ALU.subtract).then_inc(y_free[bank], 1)

            def hidden_rest(i, e2, r):
                hc, s = divmod(r, 2)
                dve.wait_ge(h_hi_ready, count(i, e2, STEPS, r + 1))
                cols = slice(HS * s, HS * (s + 1))
                v.tensor_tensor(hT[:, 1, hc, cols], hm[:, r % NHM], hT[:, 0, hc, cols].bitcast(F32),
                                ALU.subtract).then_inc(h_lo_ready, 1)

            for c in range(RING):
                dve.wait_ge(w_hi_ready, c + 1)
                v.tensor_tensor(piece_out(1, 1, "w12", c), raw[:, c], piece_out(0, 1, "w12", c).bitcast(F32),
                                ALU.subtract).then_inc(w_lo_ready, 1)
            for n in range(4):
                slots_rest(n, head_use(n)[0], n + 1)

            def lower_scaled(pair):
                step = pair // 2
                if pair % 2 == 0:
                    dve.wait_ge(lo_in[step % 2], 64 * (step // 2 + 1))
                for m in (2 * pair, 2 * pair + 1):
                    b, n = divmod(m, NT)
                    row = raw[:, step % 2, D * (m % 4):D * (m % 4 + 1)]
                    ins = v.scalar_tensor_tensor(out=row, in0=row, scalar=weight_of[:, b, 0, n:n + 1],
                                                 in1=gb_row[:, b], op0=ALU.mult, op1=ALU.mult)
                ins.then_inc(lo_scaled, 1)

            def lower_added(pair):
                dve.wait_ge(lo_scaled, pair + 1)
                xs = x[:, 2 * pair:2 * pair + 2, :]
                rows = raw[:, pair // 2 % 2, 2 * D * (pair % 2):2 * D * (pair % 2 + 1)]
                v.tensor_tensor(xs, xs, rows.rearrange("p (t d) -> p t d", d=D), ALU.add).then_inc(lo_used, 1)

            PAIRS = B * NT // 2
            LOWER_AT = (9, 11, 13, 15)

            def body(i, e2, last):
                for r in range(STEPS):
                    dve.wait_ge(silu_done, count(i, e2, STEPS, r + 1))
                    dve.wait_ge(h_lo_ready, count(i, e2, STEPS, r + 1))
                    v.tensor_tensor(hm[:, r % NHM], psH[:, r % 2, 1, 0:HS], sg[:, r % 2],
                                    ALU.mult).then_inc(h_done, 1)
                    if r:
                        hidden_rest(i, e2, r - 1)
                    if last and r in LOWER_AT:
                        pair = LOWER_AT.index(r)
                        if pair:
                            lower_added(pair - 1)
                        lower_scaled(pair)
                hidden_rest(i, e2, STEPS - 1)
                if last:
                    for pair in range(len(LOWER_AT), PAIRS):
                        lower_added(pair - 1)
                        lower_scaled(pair)
                    lower_added(PAIRS - 1)
                else:
                    for n in range(4):
                        slots_rest(n, y_use(i, e2, ("T", n))[0], count(i, e2, 4, 4 + n + 1))

            experts(dve, body)


def combine_block(nc, io, outs, keep):
    x, gb_row, slot_of, weight_of = keep["x"], keep["gb"], keep["slot"], keep["weight"]
    G = 4
    NBUF = 4
    with ExitStack() as ctx:
        def sem(name):
            return ctx.enter_context(nc.semaphore(name))

        rows = ctx.enter_context(nc.sbuf_tensor("rows", [P, NBUF, G, D], F32))
        gathered = [sem(f"gathered{i}") for i in range(NBUF)]
        scaled = sem("scaled")
        x_ready = sem("x_ready")
        stored = sem("out_stored")
        block = ctx.enter_context(nc.Block())

        @block.gpsimd
        def _(pool):
            for step in range(B * NT // G):
                if step >= NBUF:
                    pool.wait_ge(x_ready, step - NBUF + 1)
                for t in range(G):
                    b, n = divmod(G * step + t, NT)
                    nc.gpsimd.indirect_dma_start(
                        rows[:, step % NBUF, t], None, outs[:, :],
                        bass.IndirectOffsetOnAxis(ap=slot_of[:, b, 1, n:n + 1], axis=0),
                    ).then_inc(gathered[step % NBUF], 16)

        @block.vector
        def _(dve):
            v = nc.vector
            for step in range(B * NT // G):
                dve.wait_ge(gathered[step % NBUF], 16 * G * (step // NBUF + 1))
                for t in range(G):
                    b, n = divmod(G * step + t, NT)
                    row = rows[:, step % NBUF, t]
                    ins = v.scalar_tensor_tensor(out=row, in0=row, scalar=weight_of[:, b, 1, n:n + 1],
                                                 in1=gb_row[:, b], op0=ALU.mult, op1=ALU.mult)
                ins.then_inc(scaled, 1)
                dve.wait_ge(scaled, step + 1)
                xs = x[:, G * step:G * (step + 1), :]
                v.tensor_tensor(xs, xs, rows[:, step % NBUF], ALU.add).then_inc(x_ready, 1)

        @block.sync
        def _(sp):
            for step in range(B * NT // G):
                sp.wait_ge(x_ready, step + 1)
                sp.dma_start(io["out"][G * P * step:G * P * (step + 1), :].rearrange("(t p) d -> p t d", p=P),
                             x[:, G * step:G * (step + 1), :]).then_inc(stored, 16)
            sp.wait_ge(stored, 16 * B * NT // G)


def build(nc, io):
    disp = nc.dram_tensor("disp", (TRASH, D), F32, kind="Internal").ap()
    io["scr"] = nc.dram_tensor("scr", (B, 2, P, 6, S), BF16, kind="Internal").ap()
    io["sums"] = nc.dram_tensor("sums_d", (HU, S), F32, kind="Internal").ap()
    io["rsums"] = nc.dram_tensor("rsums_d", (HU, S), F32, kind="Internal").ap()
    outs = nc.dram_tensor("outs", (TRASH + 1, D), F32, kind="Internal").ap()
    with (
        nc.sbuf_tensor("x_rows", [P, B * NT, D], F32) as x,
        nc.sbuf_tensor("gb_row", [P, B, D], F32) as gb_row,
        ExitStack() as ctx,
        nc.sbuf_tensor("ring", [P, RING, H], F32) as ring,
        nc.sbuf_tensor("slot_of", [P, B, TOPK, NT], U32) as slot_of,
        nc.sbuf_tensor("weight_of", [P, B, TOPK, NT], F32) as weight_of,
    ):
        raw_ready = [ctx.enter_context(nc.semaphore(f"raw_ready{i}")) for i in range(RING)]
        keep = {"ring": ring[:], "raw_ready": raw_ready, "x": x, "gb": gb_row, "slot": slot_of, "weight": weight_of}
        attention_block(nc, io, disp, keep)
        expert_block(nc, io, disp, outs, keep)
        combine_block(nc, io, outs, keep)


def kernel(**inputs):
    import concourse.bacc as bacc
    from concourse.bass_utils import run_bass_kernel_spmd

    g = {k.removeprefix("L0_"): np.asarray(a) for k, a in inputs.items()}
    heads = np.arange(NH).reshape(NU, 1, HU) * DK
    pairs = np.arange(0, DK, 2).reshape(1, -1, 1)
    order = np.concatenate([(heads + pairs).ravel(), (heads + pairs + 1).ravel()])
    freq = (1.0 / np.float32(10000.0) ** (np.arange(0, DK, 2, dtype=np.float32) / DK)).astype(np.float32)
    angle = np.arange(S, dtype=np.float32)[None, :] * freq[:, None]
    arrays = {
        "x": g["attn_x"].reshape(T, D),
        "wq": g["attn_Wq"][order].T,
        "wk": g["attn_Wk"][order].T,
        "wv": g["attn_Wv"].T,
        "wo": g["attn_Wo"].T,
        "wg": g["ffn_Wg"],
        "bg": g["ffn_bg"],
        "w1": g["ffn_W1"],
        "w2": g["ffn_W2"],
        "w3": g["ffn_W3"],
        "cT": g["c"].T,
        "wmod": g["wmod"].reshape(D, 3, 2 * D).transpose(1, 0, 2),
        "cos": np.tile(np.repeat(np.cos(angle), HU, 0), (NU, 1)),
        "sin": np.tile(np.repeat(np.sin(angle), HU, 0), (NU, 1)),
    }
    arrays = {f"in_{k}": np.ascontiguousarray(a) for k, a in arrays.items()}
    nc = bacc.Bacc("TRN2", target_bir_lowering=False, num_devices=1)
    io = {k[3:]: nc.dram_tensor(k, a.shape, mybir.dt.from_np(a.dtype), kind="ExternalInput").ap()
          for k, a in arrays.items()}
    io["out"] = nc.dram_tensor("out", (T, D), F32, kind="ExternalOutput").ap()
    build(nc, io)
    r = run_bass_kernel_spmd(nc, [arrays], core_ids=[0])
    return r.results[0]["out"].reshape(B, S, D)
```
